# Optimizing a Trainium2 kernel written in Bass

```python
import numpy as np
import jax
import jax.numpy as jnp

def _softmax(x, axis=-1):
    return jax.nn.softmax(x, axis=axis)

def _gelu(x):
    return jax.nn.gelu(x, approximate=True)

def _silu(x):
    return jax.nn.silu(x)

def _sigmoid(x):
    return jax.nn.sigmoid(x)

def _layernorm(x, axis=-1, eps=1e-05):
    m = jnp.mean(x, axis=axis, keepdims=True)
    v = jnp.var(x, axis=axis, keepdims=True)
    return (x - m) / jnp.sqrt(v + eps)

def _scatter_add(tgt, idx, src, axis=0):
    return tgt.at[idx].add(src)

def _segment_sum(src, seg, n):
    return jax.ops.segment_sum(src, seg, n)
kernel_name = 'mk_prb_d1_jaxref_r4_178fbd'

def setup_inputs(seed: int=0):
    np.random.seed(seed)
    _w = jnp.asarray

    def _L0_attn_setup():
        import jax, jax.numpy as jnp
        import numpy as np
        B, T, DM = (4, 512, 256)
        H, DK, DV = (16, 64, 64)
        key = jax.random.key(seed)
        ks = jax.random.split(key, 6)
        s = 0.02
        x = jax.random.normal(ks[0], (B, T, DM), dtype=jnp.float32)
        Wq = jax.random.normal(ks[1], (H, DM, DK), dtype=jnp.float32) * s
        Wk = jax.random.normal(ks[2], (H, DM, DK), dtype=jnp.float32) * s
        Wv = jax.random.normal(ks[3], (H, DM, DV), dtype=jnp.float32) * s
        Wo = jax.random.normal(ks[4], (H * DV, DM), dtype=jnp.float32) * s
        bo = jnp.zeros((DM,), dtype=jnp.float32)
        return {'x': x, 'Wq': Wq, 'Wk': Wk, 'Wv': Wv, 'Wo': Wo, 'bo': bo}
    _L0_attn_in = _L0_attn_setup()

    def _L0_ffn_setup():
        import jax, jax.numpy as jnp
        import numpy as np
        B, S, D = (2, 512, 256)
        I = 128
        E = 16
        TOP_K = 2

        def _mlp(x, wg, wu, wd):
            return jnp.einsum('bsi,id->bsd', jax.nn.silu(x @ wg) * (x @ wu), wd)
        key = jax.random.key(seed)
        ks = jax.random.split(key, 10)
        sc_d = 1.0 / np.sqrt(D)
        sc_i = 1.0 / np.sqrt(I)
        return {'x': jax.random.normal(ks[0], (B, S, D), dtype=jnp.float32), 'gate_w': jax.random.normal(ks[1], (D, E), dtype=jnp.float32) * sc_d, 'gate_b': jnp.zeros((E,), dtype=jnp.float32), 'shared_wg': jax.random.normal(ks[2], (D, I), dtype=jnp.float32) * sc_d, 'shared_wu': jax.random.normal(ks[3], (D, I), dtype=jnp.float32) * sc_d, 'shared_wd': jax.random.normal(ks[4], (I, D), dtype=jnp.float32) * sc_i, 'experts_wg': jax.random.normal(ks[5], (E, D, I), dtype=jnp.float32) * sc_d, 'experts_wu': jax.random.normal(ks[6], (E, D, I), dtype=jnp.float32) * sc_d, 'experts_wd': jax.random.normal(ks[7], (E, I, D), dtype=jnp.float32) * sc_i}
    _L0_ffn_in = _L0_ffn_setup()
    _d = {'L0_attn_x': _L0_attn_in['x'], 'L0_attn_Wq': _L0_attn_in['Wq'], 'L0_attn_Wk': _L0_attn_in['Wk'], 'L0_attn_Wv': _L0_attn_in['Wv'], 'L0_attn_Wo': _L0_attn_in['Wo'], 'L0_attn_bo': _L0_attn_in['bo'], 'L0_ffn_gate_w': _L0_ffn_in['gate_w'], 'L0_ffn_gate_b': _L0_ffn_in['gate_b'], 'L0_ffn_shared_wg': _L0_ffn_in['shared_wg'], 'L0_ffn_shared_wu': _L0_ffn_in['shared_wu'], 'L0_ffn_shared_wd': _L0_ffn_in['shared_wd'], 'L0_ffn_experts_wg': _L0_ffn_in['experts_wg'], 'L0_ffn_experts_wu': _L0_ffn_in['experts_wu'], 'L0_ffn_experts_wd': _L0_ffn_in['experts_wd']}
    _x0 = _d['L0_attn_x']
    _d['L0_attn_x'] = jax.random.normal(jax.random.fold_in(jax.random.key(seed), 1), (16, 512, 256), dtype=_x0.dtype)
    del _x0
    return _d

def reference(L0_attn_x, L0_attn_Wq, L0_attn_Wk, L0_attn_Wv, L0_attn_Wo, L0_attn_bo, L0_ffn_gate_w, L0_ffn_gate_b, L0_ffn_shared_wg, L0_ffn_shared_wu, L0_ffn_shared_wd, L0_ffn_experts_wg, L0_ffn_experts_wu, L0_ffn_experts_wd):

    def _L0_attn_ref(x, Wq, Wk, Wv, Wo, bo):
        import jax, jax.numpy as jnp
        import numpy as np
        B, T, DM = (4, 512, 256)
        H, DK, DV = (16, 64, 64)
        Bx, Tx, _ = x.shape
        q = jnp.einsum('btd,hdk->bhtk', x, Wq)
        k = jnp.einsum('btd,hdk->bhtk', x, Wk)
        v = jnp.einsum('btd,hdv->bhtv', x, Wv)
        scale = k.shape[-1] ** (-0.5)
        wei = jnp.einsum('bhqk,bhsk->bhqs', q, k) * scale
        causal = jnp.tril(jnp.ones((Tx, Tx), dtype=bool))
        wei = jnp.where(causal, wei, -jnp.inf)
        wei = jax.nn.softmax(wei, axis=-1)
        out = jnp.einsum('bhqs,bhsv->bhqv', wei, v)
        out = out.transpose(0, 2, 1, 3).reshape(Bx, Tx, -1)
        out = out @ Wo + bo
        return out

    def _L0_ffn_ref(x, gate_w, gate_b, shared_wg, shared_wu, shared_wd, experts_wg, experts_wu, experts_wd):
        import jax, jax.numpy as jnp
        import numpy as np
        B, S, D = (2, 512, 256)
        I = 128
        E = 16
        TOP_K = 2

        def _mlp(x, wg, wu, wd):
            return jnp.einsum('bsi,id->bsd', jax.nn.silu(x @ wg) * (x @ wu), wd)
        router_logits = jax.nn.sigmoid(x @ gate_w + gate_b)
        expert_values, expert_indices = jax.lax.top_k(router_logits, k=TOP_K)
        expert_values = expert_values / jnp.sum(expert_values, axis=-1, keepdims=True)
        hg = jnp.einsum('bsd,edi->bsei', x, experts_wg)
        hu = jnp.einsum('bsd,edi->bsei', x, experts_wu)
        all_outputs = jnp.einsum('bsei,eid->bsed', jax.nn.silu(hg) * hu, experts_wd)
        selected = jnp.take_along_axis(all_outputs, expert_indices[..., None], axis=2)
        expert_weighted = jnp.sum(expert_values[..., None] * selected, axis=2)
        return x + _mlp(x, shared_wg, shared_wu, shared_wd) + expert_weighted
    x = L0_attn_x
    xn = _layernorm(x, axis=-1)
    x = x + _L0_attn_ref(xn, L0_attn_Wq, L0_attn_Wk, L0_attn_Wv, L0_attn_Wo, L0_attn_bo) + _L0_ffn_ref(xn, L0_ffn_gate_w, L0_ffn_gate_b, L0_ffn_shared_wg, L0_ffn_shared_wu, L0_ffn_shared_wd, L0_ffn_experts_wg, L0_ffn_experts_wu, L0_ffn_experts_wd)
    return x

_drawn_inputs = setup_inputs


def setup_inputs(seed=0):
    import zlib

    import numpy as np

    out = dict(_drawn_inputs(seed))
    spreads = {'L0_attn_bo': (0.0, 0.379), 'L0_ffn_gate_b': (0.0, 0.1)}
    factors = {'L0_attn_Wq': 8.0, 'L0_attn_Wk': 8.0, 'L0_attn_Wv': 5.061, 'L0_attn_Wo': 5.084}
    for name, (base, spread) in spreads.items():
        noise = np.random.default_rng([zlib.crc32(name.encode()), seed]).standard_normal(out[name].shape)
        drawn = base * np.exp(spread * noise) if base else spread * noise
        out[name] = jnp.asarray(drawn.astype(out[name].dtype))
    for name, factor in factors.items():
        out[name] = (out[name] * factor).astype(out[name].dtype)
    return out
```

```python
from contextlib import ExitStack

import numpy as np

import concourse.bass as bass
from concourse import mybir

F32 = mybir.dt.float32
F32R = mybir.dt.float32r
BF16 = mybir.dt.bfloat16
I32 = mybir.dt.int32
ALU = mybir.AluOpType
ACT = mybir.ActivationFunctionType
AX = mybir.AxisListType

P = 128
B, T, D = 16, 512, 256
H, DK = 16, 64
E, FF = 16, 128
KD = D // P
QT = T // P
NTOK = B * T
TT = NTOK // P
PAIRS = H // 2
HALVES = 2
HI, LO = 0, 1
SCALE = DK ** -0.5
EPS = 1e-5
MASKED = -1e30
SLOT_TILE = 256
SUB = SLOT_TILE // P
SLOT_TILES = 2 * NTOK // SLOT_TILE + E
SLOTS = SLOT_TILES * SLOT_TILE
WROW = 2 * (KD * FF) * 2 + 2 * D
PASSES = ((HI, HI), (LO, HI), (HI, LO))
START = 1
DMA = 16

W_GATE, W_UP, W_DOWN = 0, 2 * KD * FF, 4 * KD * FF


def gate_cols(hl, k):
    return slice(W_GATE + (hl * KD + k) * FF, W_GATE + (hl * KD + k + 1) * FF)


def up_cols(hl, k):
    return slice(W_UP + (hl * KD + k) * FF, W_UP + (hl * KD + k + 1) * FF)


def down_cols(hl):
    return slice(W_DOWN + hl * D, W_DOWN + (hl + 1) * D)


def wait_apart(eng, semaphore, value, begun):
    value = eng.to_reg(value)
    eng.wait_ge(begun, 1)
    eng.wait_ge(semaphore, value)


def stage_a(nc, ins, dram, keep):
    begun = keep["begun"]
    with ExitStack() as ctx:
        def sb(name, shape, dt=F32):
            return ctx.enter_context(nc.sbuf_tensor("a_" + name, shape, dt))

        def pb(name, shape, dt=F32):
            return ctx.enter_context(nc.psum_tensor("a_" + name, shape, dt))

        def sem(name):
            return ctx.enter_context(nc.semaphore("a_" + name))

        ident = keep["ident"]
        x_in = [sb(f"x_in{r}", [P, QT, D]) for r in range(2)]
        xn = [sb(f"xn{r}", [P, QT, D]) for r in range(2)]
        base = [sb(f"base{r}", [P, QT, D]) for r in range(2)]
        xnt = [sb(f"xnt{r}", [P, HALVES, KD, T], F32R) for r in range(2)]
        stats = [sb(f"stats{r}", [P, QT, 6]) for r in range(2)]
        mean_var = [sb(f"mean_var{r}", [P, QT, 2]) for r in range(2)]
        std = [sb(f"std{r}", [P, QT]) for r in range(2)]
        rstd = [sb(f"rstd{r}", [P, QT]) for r in range(2)]
        logits_t = [sb(f"logits_t{r}", [E, T]) for r in range(2)]
        bo = sb("bo", [P, D])
        gate_b = sb("gate_b", [E, 1])
        eps = sb("eps", [P, 1])
        gate_w = sb("gate_w", [P, KD, P])
        gate_w_split = sb("gate_w_split", [P, HALVES, KD, P], F32R)
        staged = sb("staged", [P, 4096])
        zeros = sb("zeros", [P, 2048])
        begun_at = sb("begun_at", [P, 1])
        probs = sb("probs", [P, TT, E])
        chosen = [sb(f"chosen{n}", [P, TT, E]) for n in range(2)]
        work = sb("work", [P, TT, E])
        spots = sb("spots", [P, TT, E])
        both = sb("both", [P, TT, E], BF16)
        best = [sb(f"best{n}", [P, TT]) for n in range(2)]
        mark = sb("mark", [P, TT])
        total = sb("total", [P, TT])
        rank_of_e = sb("rank_of_e", [P, E])
        rank_i = sb("rank_i", [P, E], I32)
        before = sb("before", [P, P], BF16)
        ones_b = sb("ones_b", [P, P], BF16)
        ones = sb("ones", [P, TT])
        tile_sum = sb("tile_sum", [P, TT, E])
        running = sb("running", [P, TT, E])
        padded_i = sb("padded_i", [P, E], I32)
        padded = sb("padded", [P, E])
        ends = sb("ends", [P, E])
        offset = sb("offset", [P, E])
        tile_i = sb("tile_i", [P, SLOT_TILES], I32)
        tile_start = sb("tile_start", [P, SLOT_TILES])
        row_i = sb("row_i", [P, 1], I32)
        row = sb("row", [P, 1])
        past = sb("past", [P, SLOT_TILES, E])
        expert = sb("expert", [P, SLOT_TILES])
        w_in = [sb(f"w_in{r}", [P, 3, D]) for r in range(2)]
        w_out = [sb(f"w_out{r}", [P, WROW], F32R) for r in range(2)]

        xt_ps = [pb(f"xt_ps{r}", [P, KD, T]) for r in range(2)]
        lg_ps = [pb(f"lg_ps{r}", [P, T]) for r in range(2)]
        lt_ps = [pb(f"lt_ps{r}", [P, QT, P]) for r in range(2)]

        x_loaded = [sem(f"x_loaded{r}") for r in range(2)]
        mean_done = sem("mean_done")
        std_done = sem("std_done")
        rstd_done = sem("rstd_done")
        xn_done = sem("xn_done")
        xt_ready = sem("xt_ready")
        hi_done = sem("hi_done")
        lo_done = sem("lo_done")
        base_half = sem("base_half")
        base_done = sem("base_done")
        lg_ready = sem("lg_ready")
        lg_out = sem("lg_out")
        lt_ready = sem("lt_ready")
        lt_out = sem("lt_out")
        xn_stored = [sem(f"xn_stored{r}") for r in range(2)]
        base_stored = [sem(f"base_stored{r}") for r in range(2)]
        xnt_stored = [sem(f"xnt_stored{r}") for r in range(2)]
        const_loaded = sem("const_loaded")
        gw_hi = sem("gw_hi")
        gw_split = sem("gw_split")
        made = sem("made")
        stage_loaded = sem("stage_loaded")
        stage_hi = sem("stage_hi")
        stage_used = sem("stage_used")
        zeroed = sem("zeroed")
        zero_stored = sem("zero_stored")
        w_loaded = [sem(f"w_loaded{r}") for r in range(2)]
        w_hi = sem("w_hi")
        w_split = sem("w_split")
        w_stored = [sem(f"w_stored{r}") for r in range(2)]
        sig_done = sem("sig_done")
        step = sem("step")
        both_ready = sem("both_ready")
        rank_ready = sem("rank_ready")

        x_src = ins["L0_attn_x"].rearrange("b (q p) d -> b p q d", p=P)
        wq_src = ins["L0_attn_Wq"].rearrange("h (k p) d -> k p h d", p=P)
        wk_src = ins["L0_attn_Wk"].rearrange("h (k p) d -> k p h d", p=P)
        wv_src = ins["L0_attn_Wv"].rearrange("h (k p) d -> k p h d", p=P)
        wo_src = ins["L0_attn_Wo"].rearrange("(j p) n -> p j n", p=P)
        wqk, wv, wo, shared = keep["wqk"], keep["wv"], keep["wo"], keep["shared"]

        def stage_view(n, src):
            if src is wo_src:
                return staged[:, 0:PAIRS * D].rearrange("p (j n) -> p j n", j=PAIRS)
            return staged[:, n * H * DK:(n + 1) * H * DK].rearrange("p (h d) -> p h d", h=H)

        loads = []
        for src, which in ((wq_src, 0), (wk_src, 1)):
            for k in range(KD):
                loads.append((src[k], stage_view(len(loads), src),
                              [wqk[:, :, which, hl, k, :].rearrange("p j (h d) -> p j h d", h=2) for hl in range(2)]))
        vo = [(wv_src[k], stage_view(k, wv_src), [wv[:, hl, k, :].rearrange("p (h d) -> p h d", h=H) for hl in range(2)])
              for k in range(KD)]
        rounds = [loads, vo, [(wo_src, stage_view(0, wo_src), [wo[:, hl, :, :] for hl in range(2)])]]

        def load_expert(sp, r, sources):
            for n, src in enumerate(sources):
                if n < 2:
                    sp.dma_start(w_in[r][:, n, :].rearrange("p (k f) -> p k f", k=KD),
                                 src.rearrange("(k p) f -> p k f", p=P)).then_inc(w_loaded[r], DMA)
                else:
                    sp.dma_start(w_in[r][:, n, :], src).then_inc(w_loaded[r], DMA)

        def halves(packed, hl):
            return packed.rearrange("p (w s n) -> p w s n", w=3, s=2)[:, :, hl, :]

        with nc.Block() as block:
            @block.sync
            def _(sp):
                sp.dma_start(bo[:, :], ins["L0_attn_bo"].rearrange("(a n) -> a n", a=1).broadcast_to([P, D])
                             ).then_inc(const_loaded, DMA)
                sp.dma_start(gate_b[:, :], ins["L0_ffn_gate_b"].rearrange("(n a) -> n a", a=1)).then_inc(const_loaded, DMA)
                sp.wait_ge(made, 1)
                sp.dma_start(gate_w[:, :, 0:E], ins["L0_ffn_gate_w"].rearrange("(k p) e -> p k e", p=P)
                             ).then_inc(const_loaded, DMA)
                with sp.Fori(0, B // 2) as g:
                    for r in range(2):
                        wait_apart(sp, base_done, START + g * 2, begun)
                        sp.dma_start(x_in[r][:, :, :], x_src[bass.ds(g * 2 + r, 1)].rearrange("b p q d -> (b p) q d")
                                     ).then_inc(x_loaded[r], DMA)
                    for r in range(2):
                        b = g * 2 + r
                        wait_apart(sp, xn_done, b + 1, begun)
                        sp.dma_start(dram["xn"][bass.ds(b, 1)].rearrange("b p q d -> (b p) q d"), xn[r][:, :, :]
                                     ).then_inc(xn_stored[r], DMA)
                        wait_apart(sp, lo_done, START + b * KD + KD, begun)
                        sp.dma_start(dram["xnt"][bass.ds(b, 1)].rearrange("b p n -> (b p) n"),
                                     xnt[r][:, :, :, :].rearrange("p a k t -> p (a k t)").bitcast(F32)
                                     ).then_inc(xnt_stored[r], DMA)
                        wait_apart(sp, base_done, START + b + 1, begun)
                        sp.dma_start(dram["base"][bass.ds(b, 1)].rearrange("b p q d -> (b p) q d"), base[r][:, :, :]
                                     ).then_inc(base_stored[r], DMA)
                n = 0
                for k_round, round_ in enumerate(rounds):
                    if k_round:
                        sp.wait_ge(stage_used, n)
                    for src, view, _ in round_:
                        sp.dma_start(view, src).then_inc(stage_loaded, DMA)
                        n += 1
                load_expert(sp, 0, [ins["L0_ffn_shared_wg"], ins["L0_ffn_shared_wu"], ins["L0_ffn_shared_wd"]])
                with sp.Fori(0, E // 2) as g:
                    for r in range(2):
                        wait_apart(sp, w_split, g * 2 + 1, begun)
                        load_expert(sp, r, [ins["L0_ffn_experts_" + n][bass.ds(g * 2 + r, 1)].rearrange("e a b -> (e a) b")
                                            for n in ("wg", "wu", "wd")])
                    for r in range(2):
                        e = g * 2 + r
                        sp.wait_ge(w_split, e + 2)
                        sp.dma_start(dram["experts"][bass.ds(e, 1)].rearrange("e p n -> (e p) n"),
                                     w_out[r][:, :].bitcast(F32)).then_inc(w_stored[r], DMA)
                for r in range(2):
                    sp.wait_ge(xn_stored[r], START + B // 2 * DMA)
                    sp.wait_ge(xnt_stored[r], START + B // 2 * DMA)
                    sp.wait_ge(base_stored[r], START + B // 2 * DMA)
                    sp.wait_ge(w_stored[r], START + E // 2 * DMA)

            @block.gpsimd
            def _(pool):
                for counter in (base_done, *base_stored, *xnt_stored, *xn_stored, lo_done, lg_out, lt_out, *w_stored,):
                    pool.sem_inc(counter, START)
                pool.memset(begun_at[:, :], 0.0).then_inc(begun, 1)
                pool.memset(gate_w[:, :, :], 0.0).then_inc(made, 1)
                pool.memset(zeros[:, :], 0.0).then_inc(zeroed, 1)
                pool.memset(eps[:, :], EPS).then_inc(made, 1)
                pool.memset(ones[:, :], 1.0).then_inc(made, 1)
                pool.memset(ones_b[:, :], 1.0).then_inc(made, 1)
                pool.memset(before[:, :], 1.0).then_inc(made, 1)
                pool.memset(ident[:, :], 0.0).then_inc(made, 1)
                pool.memset(keep["mask"][:, :], 0.0).then_inc(made, 1)
                pool.wait_ge(made, 7)
                pool.affine_select(out=before[:, :], in_=before[:, :], compare_op=ALU.is_gt, fill=0.0, base=0,
                                   pattern=[[1, P]], channel_multiplier=-1).then_inc(made, 1)
                pool.affine_select(out=ident[:, :], in_=ident[:, :], compare_op=ALU.not_equal, fill=1.0, base=0,
                                   pattern=[[-1, P]], channel_multiplier=1).then_inc(made, 1)
                pool.affine_select(out=keep["mask"][:, T - P:T], in_=keep["mask"][:, T - P:T], compare_op=ALU.is_ge,
                                   fill=MASKED, base=0, pattern=[[-1, P]], channel_multiplier=1).then_inc(made, 1)
                pool.iota(rank_i[:, :], pattern=[[-1, E]], base=E, channel_multiplier=0).then_inc(made, 1)
                pool.iota(tile_i[:, :], pattern=[[SLOT_TILE, SLOT_TILES]], base=0, channel_multiplier=0).then_inc(made, 1)
                pool.iota(row_i[:, :], pattern=[[0, 1]], base=0, channel_multiplier=1).then_inc(made, 1)
                pool.wait_ge(const_loaded, 3 * DMA)
                with pool.Fori(0, B // 2) as g:
                    for r in range(2):
                        b = g * 2 + r
                        wait_apart(pool, x_loaded[r], (g + 1) * DMA, begun)
                        wait_apart(pool, base_stored[r], START + g * DMA, begun)
                        wait_apart(pool, xn_done, b + 1, begun)
                        pool.tensor_tensor(base[r][:, :, :], x_in[r][:, :, :], xn[r][:, :, :], ALU.add).then_inc(base_half, 1)
                        wait_apart(pool, base_half, b + 1, begun)
                        pool.tensor_tensor(base[r][:, :, :], base[r][:, :, :],
                                           bo[:, None, :].broadcast_to([P, QT, D]), ALU.add).then_inc(base_done, 1)

            @block.scalar
            def _(act):
                act.wait_ge(zeroed, 1)
                for n in range(SLOTS * D // (P * 2048)):
                    act.dma_start(dram["queued"].rearrange("(n p q) d -> n p (q d)", p=P, q=8)[n], zeros[:, :]
                                  ).then_inc(zero_stored, DMA)
                act.wait_ge(made, MADE)
                act.wait_ge(const_loaded, 3 * DMA)
                act.activation(gate_w_split[:, HI, :, :], gate_w[:, :, :], ACT.Copy).then_inc(gw_hi, 1)
                with act.Fori(0, B // 2) as g:
                    for r in range(2):
                        b = g * 2 + r
                        act.wait_ge(mean_done, b + 1)
                        act.activation(std[r][:, :], mean_var[r][:, :, 1], ACT.Sqrt, bias=eps[:, 0:1]).then_inc(std_done, 1)
                        act.wait_ge(xnt_stored[r], START + g * DMA)
                        for k in range(KD):
                            act.wait_ge(xt_ready, b * KD + k + 1)
                            act.activation(xnt[r][:, HI, k, :], xt_ps[r][:, k, :], ACT.Copy).then_inc(hi_done, 1)
                        act.wait_ge(lg_ready, b + 1)
                        act.activation(logits_t[r][:, :], lg_ps[r][0:E, :], ACT.Identity, bias=gate_b[:, 0:1]
                                       ).then_inc(lg_out, 1)
                n = 0
                for round_ in rounds:
                    for _, view, parts in round_:
                        n += 1
                        act.wait_ge(stage_loaded, ROUND_LOADS(rounds, n) * DMA)
                        src = view if len(parts[HI].shape) == 3 else view.rearrange("p (j h) d -> p j h d", h=2)
                        act.activation(parts[HI], src, ACT.Copy).then_inc(stage_hi, 1)
                act.wait_ge(w_loaded[0], 3 * DMA)
                act.activation(halves(shared[:, :], HI), w_in[0][:, :, :], ACT.Copy).then_inc(w_hi, 1)
                with act.Fori(0, E // 2) as g:
                    for r in range(2):
                        act.wait_ge(w_loaded[r], g * 3 * DMA + (6 - 3 * r) * DMA)
                        act.wait_ge(w_stored[r], START + g * DMA)
                        act.activation(halves(w_out[r][:, :], HI), w_in[r][:, :, :], ACT.Copy).then_inc(w_hi, 1)
                act.wait_ge(zero_stored, SLOTS * D // (P * 2048) * DMA)
                act.wait_ge(lt_out, START + B)
                act.activation(probs[:, :, :], probs[:, :, :], ACT.Sigmoid).then_inc(sig_done, 1)

            @block.vector
            def _(dve):
                dve.wait_ge(gw_hi, 1)
                dve.tensor_tensor(gate_w_split[:, LO, :, :], gate_w[:, :, :], gate_w_split[:, HI, :, :].bitcast(F32),
                                  ALU.subtract).then_inc(gw_split, 1)
                with dve.Fori(0, B // 2) as g:
                    for r in range(2):
                        b = g * 2 + r
                        dve.wait_ge(x_loaded[r], (g + 1) * DMA)
                        for q in range(QT):
                            last = dve.bn_stats(stats[r][:, q, :], x_in[r][:, q, :])
                        last.then_inc(step, 1)
                        wait_apart(dve, step, b + 1, begun)
                        for q in range(QT):
                            last = dve.bn_aggr(mean_var[r][:, q, :], stats[r][:, q, :])
                        last.then_inc(mean_done, 1)
                        dve.wait_ge(std_done, b + 1)
                        dve.reciprocal(rstd[r][:, :], std[r][:, :]).then_inc(rstd_done, 1)
                        dve.wait_ge(rstd_done, b + 1)
                        dve.wait_ge(xn_stored[r], START + g * DMA)
                        dve.wait_ge(base_done, START + g * 2)
                        for q in range(QT):
                            last = dve.tensor_scalar(xn[r][:, q, :], x_in[r][:, q, :], mean_var[r][:, q, 0:1],
                                                     rstd[r][:, q:q + 1], ALU.subtract, ALU.mult)
                        last.then_inc(xn_done, 1)
                        for k in range(KD):
                            dve.wait_ge(hi_done, b * KD + k + 1)
                            dve.tensor_tensor(xnt[r][:, LO, k, :], xt_ps[r][:, k, :], xnt[r][:, HI, k, :].bitcast(F32),
                                              ALU.subtract).then_inc(lo_done, 1)
                        dve.wait_ge(lt_ready, b + 1)
                        dve.tensor_copy(probs[:, bass.ds(b * QT, QT), :], lt_ps[r][:, :, 0:E]).then_inc(lt_out, 1)
                n = 0
                for round_ in rounds:
                    for _, view, parts in round_:
                        n += 1
                        dve.wait_ge(stage_hi, n)
                        src = view if len(parts[HI].shape) == 3 else view.rearrange("p (j h) d -> p j h d", h=2)
                        dve.tensor_tensor(parts[LO], src, parts[HI].bitcast(F32), ALU.subtract).then_inc(stage_used, 1)

                dve.wait_ge(w_hi, 1)
                dve.tensor_tensor(halves(shared[:, :], LO), w_in[0][:, :, :], halves(shared[:, :], HI).bitcast(F32),
                                  ALU.subtract).then_inc(w_split, 1)
                with dve.Fori(0, E // 2) as g:
                    for r in range(2):
                        dve.wait_ge(w_hi, g * 2 + r + 2)
                        dve.tensor_tensor(halves(w_out[r][:, :], LO), w_in[r][:, :, :],
                                          halves(w_out[r][:, :], HI).bitcast(F32), ALU.subtract).then_inc(w_split, 1)

                count = [B]

                def then(instruction):
                    instruction.then_inc(step, 1)
                    count[0] += 1
                    dve.wait_ge(step, count[0])

                dve.wait_ge(made, MADE)
                then(dve.tensor_copy(rank_of_e[:, :], rank_i[:, :]))
                then(dve.tensor_copy(tile_start[:, :], tile_i[:, :]))
                then(dve.tensor_copy(row[:, :], row_i[:, :]))
                dve.wait_ge(sig_done, 1)
                by_e = lambda v: v[:, :, None].broadcast_to([P, TT, E])
                ranks = rank_of_e[:, None, :].broadcast_to([P, TT, E])
                for n in range(2):
                    then(dve.tensor_reduce(best[n][:, :], probs[:, :, :], AX.X, ALU.max))
                    then(dve.tensor_tensor(work[:, :, :], probs[:, :, :], by_e(best[n]), ALU.is_equal))
                    then(dve.tensor_tensor(work[:, :, :], work[:, :, :], ranks, ALU.mult))
                    then(dve.tensor_reduce(mark[:, :], work[:, :, :], AX.X, ALU.max))
                    then(dve.tensor_tensor(chosen[n][:, :, :], work[:, :, :], by_e(mark), ALU.is_equal))
                    if n == 0:
                        then(dve.scalar_tensor_tensor(probs[:, :, :].rearrange("p t e -> p (t e)"),
                                                      chosen[0][:, :, :].rearrange("p t e -> p (t e)"), -4.0,
                                                      probs[:, :, :].rearrange("p t e -> p (t e)"), ALU.mult, ALU.add))
                then(dve.tensor_tensor(total[:, :], best[0][:, :], best[1][:, :], ALU.add))
                then(dve.reciprocal(total[:, :], total[:, :]))
                for n in range(2):
                    then(dve.tensor_tensor(keep["weight"][n][:, :], best[n][:, :], total[:, :], ALU.mult))
                dve.tensor_tensor(both[:, :, :], chosen[0][:, :, :], chosen[1][:, :, :], ALU.add).then_inc(both_ready, 1)
                dve.wait_ge(rank_ready, 1)
                half = TT // 2
                for n in range(2):
                    then(dve.tensor_copy(tile_sum[:, n * half:(n + 1) * half, :],
                                         xt_ps[1][:, n, :].rearrange("p (t e) -> p t e", e=E)))
                for e in range(E):
                    then(dve.tensor_tensor_scan(running[:, :, e], ones[:, :], tile_sum[:, :, e], 0.0, ALU.mult, ALU.add))
                then(dve.tensor_scalar(padded[:, :], running[:, TT - 1, :], float(SLOT_TILE - 1), None, ALU.add))
                then(dve.tensor_copy(padded_i[:, :], padded[:, :]))
                shift = SLOT_TILE.bit_length() - 1
                then(dve.tensor_scalar(padded_i[:, :], padded_i[:, :], shift, shift, ALU.logical_shift_right,
                                       ALU.logical_shift_left))
                then(dve.tensor_copy(padded[:, :], padded_i[:, :]))
                then(dve.tensor_tensor_scan(ends[:, :], ones[:, 0:E], padded[:, :], 0.0, ALU.mult, ALU.add))
                then(dve.tensor_tensor(offset[:, :], ends[:, :], padded[:, :], ALU.subtract))
                then(dve.tensor_tensor(spots[:, :, :], running[:, :, :], tile_sum[:, :, :], ALU.subtract))
                then(dve.tensor_tensor(spots[:, :, :], spots[:, :, :], offset[:, None, :].broadcast_to([P, TT, E]), ALU.add))
                for n in range(2):
                    part = spots[:, n * half:(n + 1) * half, :]
                    then(dve.tensor_tensor(part, xt_ps[0][:, n, :].rearrange("p (t e) -> p t e", e=E), part, ALU.add))
                for n in range(2):
                    then(dve.tensor_tensor(work[:, :, :], chosen[n][:, :, :], spots[:, :, :], ALU.mult))
                    then(dve.tensor_reduce(mark[:, :], work[:, :, :], AX.X, ALU.add))
                    then(dve.tensor_copy(keep["slot"][n][:, :], mark[:, :]))
                then(dve.tensor_tensor(past[:, :, :], tile_start[:, :, None].broadcast_to([P, SLOT_TILES, E]),
                                       ends[:, None, :].broadcast_to([P, SLOT_TILES, E]), ALU.is_ge))
                then(dve.tensor_reduce(expert[:, :], past[:, :, :], AX.X, ALU.add))
                then(dve.tensor_scalar(expert[:, :], expert[:, :], float(E - 1), float(P), ALU.min, ALU.mult))
                then(dve.tensor_scalar(expert[:, :], expert[:, :], row[:, 0:1], None, ALU.add))
                then(dve.tensor_copy(keep["weight_row"][:, :], expert[:, :]))

            @block.tensor
            def _(pe):
                pe.wait_ge(made, MADE)
                pe.wait_ge(gw_split, 1)
                with pe.Fori(0, B // 2) as g:
                    for r in range(2):
                        b = g * 2 + r
                        pe.wait_ge(xn_done, b + 1)
                        pe.wait_ge(lo_done, START + g * 2 * KD)
                        for k in range(KD):
                            for q in range(QT):
                                last = pe.transpose(xt_ps[r][:, k, q * P:(q + 1) * P], xn[r][:, q, k * P:(k + 1) * P],
                                                    ident[:, :])
                            last.then_inc(xt_ready, 1)
                        pe.wait_ge(lo_done, START + (b + 1) * KD)
                        pe.wait_ge(lg_out, START + g * 2)
                        n = 0
                        for k in range(KD):
                            for wa, xb in PASSES:
                                n += 1
                                last = pe.matmul(lg_ps[r][:, :], gate_w_split[:, wa, k, :], xnt[r][:, xb, k, :],
                                                 start=(n == 1), stop=(n == KD * len(PASSES)))
                        last.then_inc(lg_ready, 1)
                        wait_apart(pe, lt_out, START + g * 2, begun)
                        wait_apart(pe, lg_out, START + b + 1, begun)
                        for q in range(QT):
                            last = pe.transpose(lt_ps[r][:, q, 0:E], logits_t[r][:, q * P:(q + 1) * P], ident[0:E, 0:E])
                        last.then_inc(lt_ready, 1)
                pe.wait_ge(both_ready, 1)
                flat = both[:, :, :].rearrange("p t e -> p (t e)")
                for n in range(2):
                    pe.matmul(xt_ps[0][:, n, :], before[:, :], flat[:, n * T:(n + 1) * T], start=True, stop=True)
                    last = pe.matmul(xt_ps[1][:, n, :], ones_b[:, :], flat[:, n * T:(n + 1) * T], start=True, stop=True)
                last.then_inc(rank_ready, 1)


MADE = 13


def ROUND_LOADS(rounds, n):
    upto = 0
    for round_ in rounds:
        upto += len(round_)
        if n <= upto:
            return upto
    return upto


def stage_scatter(nc, dram, keep):
    begun = keep["begun"]
    with ExitStack() as ctx:
        rows = [ctx.enter_context(nc.sbuf_tensor(f"s_rows{r}", [P, D], F32)) for r in range(2)]
        place = [[ctx.enter_context(nc.sbuf_tensor(f"s_place{r}{n}", [P, 1], I32)) for n in range(2)] for r in range(2)]
        loaded = [ctx.enter_context(nc.semaphore(f"s_loaded{r}")) for r in range(2)]
        placed = ctx.enter_context(nc.semaphore("s_placed"))
        queued = [ctx.enter_context(nc.semaphore(f"s_queued{r}")) for r in range(2)]
        with nc.Block() as block:
            @block.sync
            def _(sp):
                def load_rows(b, first):
                    for q in range(QT):
                        if not first or q >= 2:
                            wait_apart(sp, queued[q % 2], b * QT * DMA + (q // 2) * 2 * DMA, begun)
                        sp.dma_start(rows[q % 2][:, :], dram["xn"][bass.ds(b, 1), :, q, :].rearrange("b p d -> (b p) d")
                                     ).then_inc(loaded[q % 2], DMA)

                load_rows(0, True)
                with sp.Fori(1, B) as b:
                    load_rows(b, False)

            @block.vector
            def _(dve):
                def copy_places(b, first):
                    for q in range(QT):
                        if not first or q >= 2:
                            dve.wait_ge(queued[q % 2], b * QT * DMA + (q // 2) * 2 * DMA)
                        for n in range(2):
                            dve.tensor_copy(place[q % 2][n][:, :], keep["slot"][n][:, bass.ds(b * QT + q, 1)]
                                            ).then_inc(placed, 1)

                copy_places(0, True)
                with dve.Fori(1, B) as b:
                    copy_places(b, False)

            @block.gpsimd
            def _(pool):
                with pool.Fori(0, B) as b:
                    for q in range(QT):
                        wait_apart(pool, loaded[q % 2], b * 2 * DMA + (q // 2 + 1) * DMA, begun)
                        for n in range(2):
                            wait_apart(pool, placed, (b * QT + q) * 2 + n + 1, begun)
                            pool.indirect_dma_start(
                                out=dram["queued"][:, :],
                                out_offset=bass.IndirectOffsetOnAxis(ap=place[q % 2][n][:, 0:1], axis=0),
                                in_=rows[q % 2][:, :], in_offset=None,
                                bounds_check=SLOTS - 1, oob_is_err=False).then_inc(queued[q % 2], DMA)
                for r in range(2):
                    pool.wait_ge(queued[r], TT * DMA)


def stage_b(nc, dram, keep):
    begun = keep["begun"]
    with ExitStack() as ctx:
        def sb(name, shape, dt=F32):
            return ctx.enter_context(nc.sbuf_tensor("b_" + name, shape, dt))

        def sem(name):
            return ctx.enter_context(nc.semaphore("b_" + name))

        ident, mask = keep["ident"], keep["mask"]
        wv, wo = keep["wv"], keep["wo"]
        w_pair = [sb(f"w_pair{n}", [P, HALVES, KD, P], F32R) for n in range(2)]
        xnt = sb("xnt", [P, HALVES, KD, T], F32R)
        qs = [[sb(f"qs{r}{h}", [P, T], F32R) for h in range(2)] for r in range(2)]
        ks = [[[sb(f"ks{r}{h}{hl}", [P, T], F32R) for hl in range(HALVES)] for h in range(2)] for r in range(2)]
        v = sb("v", [P, QT, H * DK])
        vp = sb("vp", [P, 2, QT, P])
        probs = [[sb(f"probs{i}{h}", [P, T]) for h in range(2)] for i in range(QT)]
        probs_t = [sb(f"probs_t{h}", [P, QT, P]) for h in range(2)]
        out_t = [sb(f"out_t{hl}", [P, PAIRS, T], F32R) for hl in range(HALVES)]
        top = [sb(f"top{i}", [P, 2]) for i in range(QT)]
        bias = [sb(f"bias{i}", [P, 2]) for i in range(QT)]
        total = [sb(f"total{i}", [P, 2]) for i in range(QT)]
        inverse = [sb(f"inverse{i}", [P, 2]) for i in range(QT)]
        base = sb("base", [P, QT, D])
        summed = sb("summed", [P, QT, D])

        def bank(name):
            return ctx.enter_context(nc.psum_tensor("b_" + name, [P, T], F32))

        s_ps = [[bank(f"s_ps{r}{h}") for h in range(2)] for r in range(2)]
        t_ps = [bank(f"t_ps{h}") for h in range(2)]
        o_ps = bank("o_ps")
        m_ps = bank("m_ps")

        xnt_loaded, base_loaded, stored = sem("xnt_loaded"), sem("base_loaded"), sem("stored")
        w_loaded = [sem(f"w_loaded{n}") for n in range(2)]
        cleared = sem("cleared")
        m_ready = sem("m_ready")
        m_hi, m_out = sem("m_hi"), sem("m_out")
        s_ready = sem("s_ready")
        s_out = sem("s_out")
        bias_done = sem("bias_done")
        exp_done = sem("exp_done")
        inverse_done = sem("inverse_done")
        norm_done = sem("norm_done")
        t_ready = [sem(f"t_ready{h}") for h in range(2)]
        t_out = [sem(f"t_out{h}") for h in range(2)]
        o_ready, o_hi, o_out = sem("o_ready"), sem("o_hi"), sem("o_out")

        vp_loaded = [sem(f"vp_loaded{r}") for r in range(2)]

        V_GROUPS = 2 * QT
        T_FIRST = V_GROUPS // 2
        T_USES = [QT * PAIRS + V_GROUPS // 2, QT * PAIRS + V_GROUPS // 2 + QT // 2]
        PROJ = 2 * PAIRS
        M_USES = PROJ + QT // 2
        M_OUTS = 2 * PROJ + QT // 2
        M_FIRST = 4
        K_COLS = [max(2 * P, (i + 1) * P) for i in range(QT)]

        def unit(b, jp, r):
            return b * PAIRS + jp * 2 + r

        def head_half(h):
            return slice(h * DK, (h + 1) * DK)

        with nc.Block() as block:
            @block.sync
            def _(sp):
                def load_weights(which, pair):
                    sp.dma_start(w_pair[which][:, :, :, :].rearrange("p s k n -> p (s k n)").bitcast(F32),
                                 keep["wqk"][:, bass.ds(pair, 1), which, :, :, :].rearrange("p j s k n -> p (j s k n)").bitcast(F32)
                                 ).then_inc(w_loaded[which], DMA)

                def load_xnt(batch):
                    sp.dma_start(xnt[:, :, :, :].rearrange("p a k t -> p (a k t)").bitcast(F32),
                                 dram["xnt"][bass.ds(batch, 1)].rearrange("b p n -> (b p) n")).then_inc(xnt_loaded, DMA)

                def load_v_pair(pair, r):
                    sp.dma_start(vp[:, r, :, :], v[:, :, bass.ds(pair * P, P)]).then_inc(vp_loaded[r], DMA)

                load_xnt(0)
                load_weights(1, 0)
                load_weights(0, 0)
                sp.wait_ge(m_ready, 1)
                load_weights(1, 1)
                sp.wait_ge(m_ready, 2)
                load_weights(0, 1)
                sp.wait_ge(m_ready, 3)
                load_weights(1, 2)
                sp.wait_ge(m_ready, 4)
                load_weights(0, 2)
                for h in range(2):
                    sp.wait_ge(t_out[h], T_FIRST)
                load_v_pair(0, 0)
                with sp.Fori(0, B) as b:
                    def load_v(un, r):
                        wait_apart(sp, o_ready, START + b * PAIRS + un, begun)
                        load_v_pair(un + 1, 1 - r)

                    def load_keys(un, pair):
                        wait_apart(sp, m_ready, M_FIRST + b * M_USES + un * 2 + 1, begun)
                        load_weights(1, pair)

                    def load_queries(un, pair):
                        wait_apart(sp, m_ready, M_FIRST + b * M_USES + un * 2 + 2, begun)
                        load_weights(0, pair)

                    wait_apart(sp, m_out, b * M_OUTS + 2 * M_FIRST, begun)
                    wait_apart(sp, t_out[1], b * T_USES[1] + T_FIRST, begun)
                    sp.dma_start(base[:, :, :], dram["base"][bass.ds(b, 1)].rearrange("b p q d -> (b p) q d")
                                 ).then_inc(base_loaded, DMA)
                    with sp.Fori(0, PAIRS // 2 - 1) as jp:
                        for r in range(2):
                            un = jp * 2 + r
                            load_v(un, r)
                            load_keys(un, (un + 3) & (PAIRS - 1))
                            load_queries(un, (un + 3) & (PAIRS - 1))
                    load_xnt((b + 1) & (B - 1))
                    load_v(PAIRS - 2, 0)
                    load_keys(PAIRS - 2, 1)
                    load_queries(PAIRS - 2, 1)
                    load_keys(PAIRS - 1, 2)
                    load_queries(PAIRS - 1, 2)
                    for h in range(2):
                        wait_apart(sp, t_out[h], b * T_USES[h] + QT * PAIRS + 2 * T_FIRST, begun)
                    load_v_pair(0, 0)
                    wait_apart(sp, t_out[1], (b + 1) * T_USES[1] + T_FIRST, begun)
                    wait_apart(sp, m_out, (b + 1) * M_OUTS + 2 * M_FIRST, begun)
                    sp.dma_start(dram["attended"][bass.ds(b, 1)].rearrange("b p q d -> (b p) q d"), summed[:, :, :]
                                 ).then_inc(stored, DMA)
                sp.wait_ge(stored, START + B * DMA)
                sp.wait_ge(vp_loaded[0], (B * PAIRS // 2 + 1) * DMA)
                sp.wait_ge(vp_loaded[1], B * PAIRS // 2 * DMA)
                sp.wait_ge(w_loaded[0], (B * PAIRS + 3) * DMA)
                sp.wait_ge(w_loaded[1], (B * PAIRS + 3) * DMA)

            @block.tensor
            def _(pe):
                def project(which, loaded, before):
                    pe.wait_ge(w_loaded[which], loaded)
                    if before is not None:
                        pe.wait_ge(m_hi, before[0])
                        pe.wait_ge(m_out, before[1])
                    n = 0
                    for k in range(KD):
                        for wa, xb in PASSES:
                            n += 1
                            last = pe.matmul(m_ps[:, :], w_pair[which][:, wa, k, :], xnt[:, xb, k, :], start=(n == 1),
                                             stop=(n == KD * len(PASSES)))
                    last.then_inc(m_ready, 1)

                def scores(r, i, outs, before):
                    if outs is not None:
                        pe.wait_ge(m_out, outs)
                    for h in range(2):
                        if before is not None:
                            pe.wait_ge(s_out, before * 2 + h + 1)
                        cols = K_COLS[i]
                        for hl in range(HALVES):
                            last = pe.matmul(s_ps[i % 2][h][:, 0:cols], qs[r][h][:, i * P:(i + 1) * P],
                                             ks[r][h][hl][:, 0:cols], start=(hl == 0), stop=(hl == 1))
                        last.then_inc(s_ready, 1)

                def transposes(i, step_no, uses):
                    for h in range(2):
                        pe.wait_ge(norm_done, step_no * 2 + h + 1)
                        pe.wait_ge(t_out[h], uses[h])
                        for j in range(i + 1):
                            last = pe.transpose(t_ps[h][:, j * P:(j + 1) * P], probs[i][h][:, j * P:(j + 1) * P], ident[:, :])
                        last.then_inc(t_ready[h], 1)

                def weigh(r, i, u, uses, copied):
                    if i == 0:
                        pe.wait_ge(o_out, START + u)
                        pe.wait_ge(vp_loaded[r], copied)
                    for h in range(2):
                        pe.wait_ge(t_out[h], uses[h] + 1)
                    for j in range(i + 1):
                        for h in range(2):
                            last = pe.matmul(o_ps[head_half(h), i * P:(i + 1) * P], vp[:, r, j, head_half(h)],
                                             probs_t[h][:, j, :], start=(j == 0), stop=(j == i))
                    if i == QT - 1:
                        last.then_inc(o_ready, 1)

                def project_v(first_uses):
                    for g in range(V_GROUPS):
                        tok, half = divmod(g, 2)
                        if first_uses is not None:
                            pe.wait_ge(t_out[half], first_uses[half] + tok)
                        elif tok:
                            pe.wait_ge(t_out[half], tok)
                        n = 0
                        for k in range(KD):
                            for xa, wb in PASSES:
                                n += 1
                                last = pe.matmul(t_ps[half][:, :], xnt[:, xa, k, tok * P:(tok + 1) * P],
                                                 wv[:, wb, k, half * T:(half + 1) * T], start=(n == 1),
                                                 stop=(n == KD * len(PASSES)))
                        last.then_inc(t_ready[half], 1)

                def project_out(b, t_uses, outs):
                    for q in range(QT):
                        if q % 2 == 0:
                            to = t_ps[1]
                            pe.wait_ge(t_out[1], t_uses + q // 2)
                        else:
                            to = m_ps
                            pe.wait_ge(m_out, outs + q // 2)
                        for j in range(PAIRS):
                            if j == PAIRS - 1 and q == 0:
                                pe.wait_ge(o_out, START + (b + 1) * PAIRS)
                            elif j == 0 and q == 0:
                                pe.wait_ge(o_out, START + (b + 1) * PAIRS - 1)
                            for n, (oa, wb) in enumerate(PASSES):
                                last = pe.matmul(to[:, 0:D], out_t[oa][:, j, q * P:(q + 1) * P], wo[:, wb, j, :],
                                                 start=(j == 0 and n == 0),
                                                 stop=(j == PAIRS - 1 and n == len(PASSES) - 1))
                        last.then_inc(t_ready[1] if q % 2 == 0 else m_ready, 1)

                pe.wait_ge(xnt_loaded, DMA)
                project_v(None)
                project(1, DMA, None)
                project(0, DMA, (2, 2))
                pe.wait_ge(cleared, 2)
                project(1, 2 * DMA, (4, 4))
                project(0, 2 * DMA, (6, 6))
                scores(0, 0, None, None)
                scores(0, 1, None, None)
                scores(0, 2, None, 0)
                with pe.Fori(0, B) as b:
                    with pe.Fori(0, PAIRS // 2) as jp:
                        for r in range(2):
                            un = jp * 2 + r
                            u = unit(b, jp, r)
                            his = 2 * M_FIRST + b * 2 * PROJ + un * 4
                            outs = 2 * M_FIRST + b * M_OUTS + un * 4
                            for i in range(QT):
                                uses = [T_FIRST + b * T_USES[h] + un * QT + i for h in range(2)]
                                transposes(i, u * QT + i, uses)
                                if i == 0:
                                    scores(r, QT - 1, None, u * QT + 1)
                                else:
                                    scores(1 - r, i - 1, outs if i == 1 else None, u * QT + i + 1)
                                if i == 1:
                                    pe.wait_ge(xnt_loaded, (b + 1 + ((un + 2) >> 3)) * DMA)
                                    project(1, (u + 3) * DMA, (his, outs))
                                if i == 2:
                                    project(0, (u + 3) * DMA, (his + 2, outs + 2))
                                weigh(r, i, u, uses, (b * (PAIRS // 2) + jp + 1) * DMA)
                    v_uses = [T_FIRST + b * T_USES[h] + QT * PAIRS for h in range(2)]
                    project_v(v_uses)
                    project_out(b, v_uses[1] + T_FIRST, 2 * M_FIRST + b * M_OUTS + 2 * PROJ)

            @block.scalar
            def _(act):
                def split_keys(r, ready):
                    act.wait_ge(m_ready, ready)
                    for h in range(2):
                        for copy in range(2):
                            last = act.activation(ks[r][h][HI][head_half(copy), :], m_ps[head_half(h), :], ACT.Copy)
                        last.then_inc(m_hi, 1)

                def split_queries(r, ready):
                    act.wait_ge(m_ready, ready)
                    for h in range(2):
                        act.activation(qs[r][h][head_half(h), :], m_ps[head_half(h), :], ACT.Copy).then_inc(m_hi, 1)

                def exponentials(i, step_no):
                    act.wait_ge(bias_done, step_no + 1)
                    for h in range(2):
                        part = probs[i][h][:, 0:(i + 1) * P]
                        act.activation(part, part, ACT.Exp, bias=bias[i][:, h:h + 1], scale=SCALE,
                                       accum_out=total[i][:, h:h + 1]).then_inc(exp_done, 1)

                def take_v(copied, ready):
                    for r in range(2) if copied is not None else ():
                        act.wait_ge(vp_loaded[r], copied)
                    for tok in range(QT):
                        act.wait_ge(t_ready[0], ready + tok + 1)
                        act.activation(v[:, tok, 0:T], t_ps[0][:, :], ACT.Copy).then_inc(t_out[0], 1)

                take_v(None, 0)
                split_keys(0, 1)
                split_queries(0, 2)
                split_keys(1, 3)
                split_queries(1, 4)
                for i in range(3):
                    exponentials(i, i)
                with act.Fori(0, B) as b:
                    with act.Fori(0, PAIRS // 2) as jp:
                        for r in range(2):
                            u = unit(b, jp, r)
                            for i in range(QT):
                                act.wait_ge(t_ready[0], T_FIRST + b * T_USES[0] + (jp * 2 + r) * QT + i + 1)
                                act.activation(probs_t[0][:, 0:i + 1, :], t_ps[0][:, 0:(i + 1) * P].rearrange(
                                    "p (j n) -> p j n", n=P), ACT.Copy).then_inc(t_out[0], 1)
                                ready = M_FIRST + b * M_USES + (jp * 2 + r) * 2
                                if i == 1:
                                    split_keys(r, ready + 1)
                                if i == 2:
                                    split_queries(r, ready + 2)
                                exponentials((i + 3) % QT, u * QT + i + 3)
                            act.wait_ge(o_ready, START + u + 1)
                            act.activation(out_t[HI][:, bass.ds(jp * 2 + r, 1), :].rearrange("p a t -> p (a t)"),
                                           o_ps[:, :], ACT.Copy).then_inc(o_hi, 1)
                    take_v((b + 1) * (PAIRS // 2) * DMA, T_FIRST + b * T_USES[0] + QT * PAIRS)

            @block.vector
            def _(dve):
                def split_keys(r, his):
                    for h in range(2):
                        dve.wait_ge(m_hi, his + h + 1)
                        dve.tensor_tensor(ks[r][h][LO][head_half(h), :], m_ps[head_half(h), :],
                                          ks[r][h][HI][head_half(h), :].bitcast(F32), ALU.subtract).then_inc(m_out, 1)

                def split_queries(r, his):
                    for h in range(2):
                        dve.wait_ge(m_hi, his + h + 1)
                        dve.tensor_tensor(qs[r][h][head_half(1 - h), :], m_ps[head_half(h), :],
                                          qs[r][h][head_half(h), :].bitcast(F32), ALU.subtract).then_inc(m_out, 1)

                def maxima(i, step_no):
                    cols = (i + 1) * P
                    for h in range(2):
                        wait_apart(dve, s_ready, step_no * 2 + h + 1, begun)
                        dve.tensor_tensor_reduce(out=probs[i][h][:, 0:cols], in0=s_ps[i % 2][h][:, 0:cols],
                                                 in1=mask[:, T - cols:T], scale=1.0, scalar=-3e38, op0=ALU.add,
                                                 op1=ALU.max, accum_out=top[i][:, h:h + 1]).then_inc(s_out, 1)
                    dve.wait_ge(s_out, step_no * 2 + 2)
                    dve.tensor_scalar(bias[i][:, :], top[i][:, :], -SCALE, None, ALU.mult).then_inc(bias_done, 1)

                def invert(i, step_no):
                    dve.wait_ge(exp_done, step_no * 2 + 2)
                    dve.reciprocal(inverse[i][:, :], total[i][:, :]).then_inc(inverse_done, 1)

                def take_v(copied, ready):
                    for r in range(2) if copied is not None else ():
                        dve.wait_ge(vp_loaded[r], copied)
                    for tok in range(QT):
                        dve.wait_ge(t_ready[1], ready + tok + 1)
                        dve.tensor_copy(v[:, tok, T:2 * T], t_ps[1][:, :]).then_inc(t_out[1], 1)

                take_v(None, 0)
                split_keys(0, 0)
                split_queries(0, 2)
                split_keys(1, 4)
                split_queries(1, 6)
                for i in range(3):
                    maxima(i, i)
                for i in range(2):
                    invert(i, i)
                with dve.Fori(0, B) as b:
                    with dve.Fori(0, PAIRS // 2) as jp:
                        for r in range(2):
                            u = unit(b, jp, r)
                            for i in range(QT):
                                invert((i + 2) % QT, u * QT + i + 2)
                                dve.wait_ge(t_ready[1], T_FIRST + b * T_USES[1] + (jp * 2 + r) * QT + i + 1)
                                dve.tensor_copy(probs_t[1][:, 0:i + 1, :], t_ps[1][:, 0:(i + 1) * P].rearrange(
                                    "p (j n) -> p j n", n=P)).then_inc(t_out[1], 1)
                                maxima((i + 3) % QT, u * QT + i + 3)
                                if i == 1:
                                    split_keys(r, 2 * M_FIRST + u * 4)
                                if i == 2:
                                    split_queries(r, 2 * M_FIRST + u * 4 + 2)
                            dve.wait_ge(o_hi, u + 1)
                            dve.tensor_tensor(out_t[LO][:, bass.ds(jp * 2 + r, 1), :].rearrange("p a t -> p (a t)"),
                                              o_ps[:, :], out_t[HI][:, bass.ds(jp * 2 + r, 1), :].rearrange(
                                                  "p a t -> p (a t)").bitcast(F32), ALU.subtract).then_inc(o_out, 1)
                    take_v((b + 1) * (PAIRS // 2) * DMA, T_FIRST + b * T_USES[1] + QT * PAIRS)
                    dve.wait_ge(base_loaded, (b + 1) * DMA)
                    dve.wait_ge(stored, START + b * DMA)
                    for q in range(QT):
                        if q % 2 == 0:
                            dve.wait_ge(t_ready[1], T_FIRST + (b + 1) * T_USES[1] - QT // 2 + q // 2 + 1)
                        else:
                            dve.wait_ge(m_ready, M_FIRST + (b + 1) * M_USES - QT // 2 + q // 2 + 1)
                        dve.tensor_tensor(summed[:, q, :], (t_ps[1] if q % 2 == 0 else m_ps)[:, 0:D], base[:, q, :],
                                          ALU.add).then_inc(t_out[1] if q % 2 == 0 else m_out, 1)

            @block.gpsimd
            def _(pool):
                for counter in (o_out, o_ready, stored):
                    pool.sem_inc(counter, START)
                def normalise(i, step_no):
                    wait_apart(pool, inverse_done, step_no + 1, begun)
                    for h in range(2):
                        part = probs[i][h][:, 0:(i + 1) * P]
                        pool.tensor_scalar(part, part, inverse[i][:, h:h + 1], 1.0, ALU.mult, ALU.mult).then_inc(norm_done, 1)

                for r in range(2):
                    for h in range(2):
                        last = pool.memset(ks[r][h][LO][head_half(1 - h), :].bitcast(F32), 0.0)
                    last.then_inc(cleared, 1)
                for i in range(2):
                    normalise(i, i)
                with pool.Fori(0, B) as b:
                    with pool.Fori(0, PAIRS // 2) as jp:
                        for r in range(2):
                            for i in range(QT):
                                normalise((i + 2) % QT, unit(b, jp, r) * QT + i + 2)


def stage_c(nc, dram, keep):
    begun = keep["begun"]
    with ExitStack() as ctx:
        def sb(name, shape, dt=F32):
            return ctx.enter_context(nc.sbuf_tensor("c_" + name, shape, dt))

        def pb(name, shape, dt=F32):
            return ctx.enter_context(nc.psum_tensor("c_" + name, shape, dt))

        def sem(name):
            return ctx.enter_context(nc.semaphore("c_" + name))

        ident = keep["ident"]
        row = [sb(f"row{r}", [P, 1], I32) for r in range(2)]
        w = [sb(f"w{r}", [P, WROW], F32R) for r in range(2)]
        x = [sb(f"x{r}", [P, SUB, D]) for r in range(2)]
        xt = [sb(f"xt{r}", [P, HALVES, KD, SLOT_TILE], F32R) for r in range(2)]
        silu = [sb(f"silu{r}", [P, SLOT_TILE]) for r in range(2)]
        hidden = [sb(f"hidden{r}", [P, SLOT_TILE]) for r in range(2)]
        hs = [sb(f"hs{r}", [P, HALVES, SLOT_TILE], F32R) for r in range(2)]
        y = [sb(f"y{r}", [P, SUB, D]) for r in range(2)]
        xt_ps = [pb(f"xt_ps{r}", [P, KD, SLOT_TILE]) for r in range(2)]
        gate_ps = [pb(f"gate_ps{r}", [P, SLOT_TILE, ]) for r in range(2)]
        up_ps = [pb(f"up_ps{r}", [P, SLOT_TILE]) for r in range(2)]
        y_ps = [pb(f"y_ps{r}", [P, SUB, D]) for r in range(2)]
        row_done = sem("row_done")
        w_loaded = [sem(f"w_loaded{r}") for r in range(2)]
        x_loaded = [sem(f"x_loaded{r}") for r in range(2)]
        y_stored = [sem(f"y_stored{r}") for r in range(2)]
        xt_ready, xt_hi, xt_done = sem("xt_ready"), sem("xt_hi"), sem("xt_done")
        gu_ready, silu_done, hidden_done = sem("gu_ready"), sem("silu_done"), sem("hidden_done")
        hs_hi, hs_done, y_ready, y_done = sem("hs_hi"), sem("hs_done"), sem("y_ready"), sem("y_done")
        PAIRS_OF_TILES = SLOT_TILES // 2

        with nc.Block() as block:
            @block.sync
            def _(sp):
                with sp.Fori(0, PAIRS_OF_TILES) as g:
                    for r in range(2):
                        wait_apart(sp, xt_ready, START + g * 2, begun)
                        sp.dma_start(x[r][:, :, :], dram["queued"][bass.ds((g * 2 + r) * SLOT_TILE, SLOT_TILE), :]
                                     .rearrange("(s p) d -> p s d", p=P)).then_inc(x_loaded[r], DMA)
                    for r in range(2):
                        wait_apart(sp, y_done, START + g * 2 + r + 1, begun)
                        sp.dma_start(dram["routed"][bass.ds((g * 2 + r) * SLOT_TILE, SLOT_TILE), :]
                                     .rearrange("(s p) d -> p s d", p=P), y[r][:, :, :]).then_inc(y_stored[r], DMA)
                for r in range(2):
                    sp.wait_ge(y_stored[r], START + PAIRS_OF_TILES * DMA)

            @block.gpsimd
            def _(pool):
                for counter in (xt_ready, gu_ready, y_ready, xt_done, hidden_done, y_done, *y_stored):
                    pool.sem_inc(counter, START)
                with pool.Fori(0, PAIRS_OF_TILES) as g:
                    for r in range(2):
                        wait_apart(pool, row_done, g * 2 + r + 1, begun)
                        wait_apart(pool, y_ready, START + g * 2, begun)
                        pool.indirect_dma_start(
                            out=w[r][:, :].bitcast(F32), out_offset=None, in_=dram["experts"].rearrange("e p n -> (e p) n"),
                            in_offset=bass.IndirectOffsetOnAxis(ap=row[r][:, 0:1], axis=0),
                            bounds_check=E * P - 1, oob_is_err=False).then_inc(w_loaded[r], DMA)

            @block.tensor
            def _(pe):
                with pe.Fori(0, PAIRS_OF_TILES) as g:
                    for r in range(2):
                        t = g * 2 + r
                        pe.wait_ge(x_loaded[r], (g + 1) * DMA)
                        pe.wait_ge(xt_done, START + g * 2)
                        for k in range(KD):
                            for s in range(SUB):
                                last = pe.transpose(xt_ps[r][:, k, s * P:(s + 1) * P], x[r][:, s, k * P:(k + 1) * P],
                                                    ident[:, :])
                        last.then_inc(xt_ready, 1)
                    for r in range(2):
                        t = g * 2 + r
                        pe.wait_ge(xt_done, START + t + 1)
                        pe.wait_ge(w_loaded[r], (g + 1) * DMA)
                        pe.wait_ge(hidden_done, START + g * 2)
                        for to, cols in ((gate_ps[r], gate_cols), (up_ps[r], up_cols)):
                            n = 0
                            for k in range(KD):
                                for wa, xb in PASSES:
                                    n += 1
                                    last = pe.matmul(to[:, :], w[r][:, cols(wa, k)], xt[r][:, xb, k, :], start=(n == 1),
                                                     stop=(n == KD * len(PASSES)))
                        last.then_inc(gu_ready, 1)
                    for r in range(2):
                        t = g * 2 + r
                        pe.wait_ge(hs_done, t + 1)
                        pe.wait_ge(y_done, START + g * 2)
                        for s in range(SUB):
                            for n, (ha, wb) in enumerate(PASSES):
                                last = pe.matmul(y_ps[r][:, s, :], hs[r][:, ha, s * P:(s + 1) * P], w[r][:, down_cols(wb)],
                                                 start=(n == 0), stop=(n == len(PASSES) - 1))
                        last.then_inc(y_ready, 1)

            @block.scalar
            def _(act):
                with act.Fori(0, PAIRS_OF_TILES) as g:
                    for r in range(2):
                        act.wait_ge(xt_ready, START + g * 2 + r + 1)
                        act.activation(xt[r][:, HI, :, :], xt_ps[r][:, :, :], ACT.Copy).then_inc(xt_hi, 1)
                    for r in range(2):
                        act.wait_ge(gu_ready, START + g * 2 + r + 1)
                        act.activation(silu[r][:, :], gate_ps[r][:, :], ACT.Silu).then_inc(silu_done, 1)
                    for r in range(2):
                        act.wait_ge(hidden_done, START + g * 2 + r + 1)
                        act.activation(hs[r][:, HI, :], hidden[r][:, :], ACT.Copy).then_inc(hs_hi, 1)
                    for r in range(2):
                        act.wait_ge(y_stored[r], START + g * DMA)
                        act.wait_ge(y_ready, START + g * 2 + r + 1)
                        act.activation(y[r][:, :, :], y_ps[r][:, :, :], ACT.Copy).then_inc(y_done, 1)

            @block.vector
            def _(dve):
                with dve.Fori(0, PAIRS_OF_TILES) as g:
                    for r in range(2):
                        dve.wait_ge(gu_ready, START + g * 2)
                        dve.tensor_copy(row[r][:, :], keep["weight_row"][:, bass.ds(g * 2 + r, 1)]).then_inc(row_done, 1)
                    for r in range(2):
                        dve.wait_ge(xt_hi, g * 2 + r + 1)
                        dve.tensor_tensor(xt[r][:, LO, :, :], xt_ps[r][:, :, :], xt[r][:, HI, :, :].bitcast(F32),
                                          ALU.subtract).then_inc(xt_done, 1)
                    for r in range(2):
                        dve.wait_ge(silu_done, g * 2 + r + 1)
                        dve.tensor_tensor(hidden[r][:, :], up_ps[r][:, :], silu[r][:, :], ALU.mult).then_inc(hidden_done, 1)
                    for r in range(2):
                        dve.wait_ge(hs_hi, g * 2 + r + 1)
                        dve.tensor_tensor(hs[r][:, LO, :], hidden[r][:, :], hs[r][:, HI, :].bitcast(F32),
                                          ALU.subtract).then_inc(hs_done, 1)


def stage_d(nc, dram, keep, out):
    begun = keep["begun"]
    with ExitStack() as ctx:
        def sb(name, shape, dt=F32):
            return ctx.enter_context(nc.sbuf_tensor("d_" + name, shape, dt))

        def pb(name, shape, dt=F32):
            return ctx.enter_context(nc.psum_tensor("d_" + name, shape, dt))

        def sem(name):
            return ctx.enter_context(nc.semaphore("d_" + name))

        w = keep["shared"]
        place = [[[sb(f"place{r}{s}{n}", [P, 1], I32) for n in range(2)] for s in range(SUB)] for r in range(2)]
        xt = [sb(f"xt{r}", [P, HALVES, KD, SLOT_TILE], F32R) for r in range(2)]
        rest = [sb(f"rest{r}", [P, SUB, D]) for r in range(2)]
        silu = [sb(f"silu{r}", [P, SLOT_TILE]) for r in range(2)]
        hidden = [sb(f"hidden{r}", [P, SLOT_TILE]) for r in range(2)]
        hs = [sb(f"hs{r}", [P, HALVES, SLOT_TILE], F32R) for r in range(2)]
        y = [[[sb(f"y{r}{s}{n}", [P, D]) for n in range(2)] for s in range(SUB)] for r in range(2)]
        result = [sb(f"result{r}", [P, SUB, D]) for r in range(2)]
        gate_ps = [pb(f"gate_ps{r}", [P, SLOT_TILE]) for r in range(2)]
        up_ps = [pb(f"up_ps{r}", [P, SLOT_TILE]) for r in range(2)]
        y_ps = [pb(f"y_ps{r}", [P, SUB, D]) for r in range(2)]
        xt_loaded = [sem(f"xt_loaded{r}") for r in range(2)]
        rest_loaded = [sem(f"rest_loaded{r}") for r in range(2)]
        gathered = [sem(f"gathered{r}") for r in range(2)]
        stored = [sem(f"stored{r}") for r in range(2)]
        placed, gu_ready, silu_done, hidden_done = sem("placed"), sem("gu_ready"), sem("silu_done"), sem("hidden_done")
        hs_hi, hs_done, y_ready, summing, done = sem("hs_hi"), sem("hs_done"), sem("y_ready"), sem("summing"), sem("done")
        xnt_d = dram["xnt"].rearrange("b p (a n) -> b p a n", a=HALVES * KD)
        out_d = out.rearrange("b (q p) d -> b p q d", p=P)

        with nc.Block() as block:
            @block.sync
            def _(sp):
                with sp.Fori(0, B) as b:
                    for r in range(2):
                        wait_apart(sp, gu_ready, START + b * 2, begun)
                        sp.dma_start(xt[r][:, :, :, :].rearrange("p a k t -> p (a k) t").bitcast(F32),
                                     xnt_d[bass.ds(b, 1), :, :, r * SLOT_TILE:(r + 1) * SLOT_TILE].rearrange(
                                         "b p a n -> (b p) a n")).then_inc(xt_loaded[r], DMA)
                        wait_apart(sp, done, START + b * 2, begun)
                        sp.dma_start(rest[r][:, :, :], dram["attended"][bass.ds(b, 1), :, r * SUB:(r + 1) * SUB, :].rearrange(
                            "b p q d -> (b p) q d")).then_inc(rest_loaded[r], DMA)
                    for r in range(2):
                        wait_apart(sp, done, START + b * 2 + r + 1, begun)
                        sp.dma_start(out_d[bass.ds(b, 1), :, r * SUB:(r + 1) * SUB, :].rearrange("b p q d -> (b p) q d"),
                                     result[r][:, :, :]).then_inc(stored[r], DMA)
                for r in range(2):
                    sp.wait_ge(stored[r], START + B * DMA)

            @block.gpsimd
            def _(pool):
                for counter in (gu_ready, done, hidden_done, *stored):
                    pool.sem_inc(counter, START)
                with pool.Fori(0, B) as b:
                    for r in range(2):
                        wait_apart(pool, placed, (b * 2 + r + 1) * 2 * SUB, begun)
                        wait_apart(pool, done, START + b * 2, begun)
                        for s in range(SUB):
                            for n in range(2):
                                pool.indirect_dma_start(
                                    out=y[r][s][n][:, :], out_offset=None, in_=dram["routed"][:, :],
                                    in_offset=bass.IndirectOffsetOnAxis(ap=place[r][s][n][:, 0:1], axis=0),
                                    bounds_check=SLOTS - 1, oob_is_err=False).then_inc(gathered[r], DMA)

            @block.tensor
            def _(pe):
                with pe.Fori(0, B) as b:
                    for r in range(2):
                        pe.wait_ge(xt_loaded[r], (b + 1) * DMA)
                        pe.wait_ge(hidden_done, START + b * 2)
                        for to, cols in ((gate_ps[r], gate_cols), (up_ps[r], up_cols)):
                            n = 0
                            for k in range(KD):
                                for wa, xb in PASSES:
                                    n += 1
                                    last = pe.matmul(to[:, :], w[:, cols(wa, k)], xt[r][:, xb, k, :], start=(n == 1),
                                                     stop=(n == KD * len(PASSES)))
                        last.then_inc(gu_ready, 1)
                    for r in range(2):
                        pe.wait_ge(hs_done, b * 2 + r + 1)
                        pe.wait_ge(done, START + b * 2)
                        for s in range(SUB):
                            for n, (ha, wb) in enumerate(PASSES):
                                last = pe.matmul(y_ps[r][:, s, :], hs[r][:, ha, s * P:(s + 1) * P], w[:, down_cols(wb)],
                                                 start=(n == 0), stop=(n == len(PASSES) - 1))
                        last.then_inc(y_ready, 1)

            @block.scalar
            def _(act):
                with act.Fori(0, B) as b:
                    for r in range(2):
                        act.wait_ge(gu_ready, START + b * 2 + r + 1)
                        act.activation(silu[r][:, :], gate_ps[r][:, :], ACT.Silu).then_inc(silu_done, 1)
                    for r in range(2):
                        act.wait_ge(hidden_done, START + b * 2 + r + 1)
                        act.activation(hs[r][:, HI, :], hidden[r][:, :], ACT.Copy).then_inc(hs_hi, 1)

            @block.vector
            def _(dve):
                with dve.Fori(0, B) as b:
                    for r in range(2):
                        for s in range(SUB):
                            for n in range(2):
                                dve.tensor_copy(place[r][s][n][:, :],
                                                keep["slot"][n][:, bass.ds(b * QT + r * SUB + s, 1)]).then_inc(placed, 1)
                    for r in range(2):
                        dve.wait_ge(silu_done, b * 2 + r + 1)
                        dve.tensor_tensor(hidden[r][:, :], up_ps[r][:, :], silu[r][:, :], ALU.mult).then_inc(hidden_done, 1)
                    for r in range(2):
                        dve.wait_ge(hs_hi, b * 2 + r + 1)
                        dve.tensor_tensor(hs[r][:, LO, :], hidden[r][:, :], hs[r][:, HI, :].bitcast(F32),
                                          ALU.subtract).then_inc(hs_done, 1)
                    for r in range(2):
                        dve.wait_ge(rest_loaded[r], (b + 1) * DMA)
                        dve.wait_ge(gathered[r], (b + 1) * 2 * SUB * DMA)
                        dve.wait_ge(stored[r], START + b * DMA)
                        dve.wait_ge(y_ready, b * 2 + r + 1)
                        for s in range(SUB):
                            dve.tensor_tensor(result[r][:, s, :], y_ps[r][:, s, :], rest[r][:, s, :], ALU.add
                                              ).then_inc(summing, 1)
                        for n in range(2):
                            dve.wait_ge(summing, (b * 2 + r) * (3 * SUB - 1) + (n + 1) * SUB)
                            for s in range(SUB):
                                last = dve.scalar_tensor_tensor(result[r][:, s, :], y[r][s][n][:, :],
                                                                keep["weight"][n][:, bass.ds(b * QT + r * SUB + s, 1)],
                                                                result[r][:, s, :], ALU.mult, ALU.add)
                                last.then_inc(done if n == 1 and s == SUB - 1 else summing, 1)


def program(nc, ins, out):
    with ExitStack() as ctx:
        def sb(name, shape, dt=F32):
            return ctx.enter_context(nc.sbuf_tensor(name, shape, dt))

        dram = {
            "xn": nc.dram_tensor("xn_rows", [B, P, QT, D], F32).ap(),
            "xnt": nc.dram_tensor("xnt_split", [B, P, HALVES * KD * T], F32).ap(),
            "base": nc.dram_tensor("base_rows", [B, P, QT, D], F32).ap(),
            "attended": nc.dram_tensor("attended_rows", [B, P, QT, D], F32).ap(),
            "experts": nc.dram_tensor("expert_rows", [E, P, WROW], F32).ap(),
            "queued": nc.dram_tensor("queued_rows", [SLOTS, D], F32).ap(),
            "routed": nc.dram_tensor("routed_rows", [SLOTS, D], F32).ap(),
        }
        keep = {
            "begun": ctx.enter_context(nc.semaphore("begun")),
            "ident": sb("ident", [P, P]),
            "mask": sb("mask", [P, T]),
            "wqk": sb("wqk_all", [P, PAIRS, 2, HALVES, KD, P], F32R),
            "wv": sb("wv_all", [P, HALVES, KD, H * DK], F32R),
            "wo": sb("wo_all", [P, HALVES, PAIRS, D], F32R),
            "shared": sb("shared_all", [P, WROW], F32R),
            "weight": [sb(f"weight{n}", [P, TT]) for n in range(2)],
            "slot": [sb(f"slot{n}", [P, TT], I32) for n in range(2)],
            "weight_row": sb("weight_row", [P, SLOT_TILES], I32),
        }
        stage_a(nc, ins, dram, keep)
        stage_scatter(nc, dram, keep)
        stage_b(nc, dram, keep)
        stage_c(nc, dram, keep)
        stage_d(nc, dram, keep, out)


NAMES = ["L0_attn_x", "L0_attn_Wq", "L0_attn_Wk", "L0_attn_Wv", "L0_attn_Wo", "L0_attn_bo", "L0_ffn_gate_w",
         "L0_ffn_gate_b", "L0_ffn_shared_wg", "L0_ffn_shared_wu", "L0_ffn_shared_wd", "L0_ffn_experts_wg",
         "L0_ffn_experts_wu", "L0_ffn_experts_wd"]


def kernel(**inputs):
    import concourse.bacc as bacc
    from concourse.bass_utils import run_bass_kernel_spmd

    nc = bacc.Bacc("TRN2", target_bir_lowering=False, num_devices=1)
    arrays, ins = {}, {}
    for name in NAMES:
        a = np.ascontiguousarray(inputs[name])
        arrays[f"in_{name}"] = a
        ins[name] = nc.dram_tensor(f"in_{name}", a.shape, mybir.dt.from_np(a.dtype), kind="ExternalInput").ap()
    out = nc.dram_tensor("out_0", (B, T, D), F32, kind="ExternalOutput").ap()
    program(nc, ins, out)
    result = run_bass_kernel_spmd(nc, [arrays], core_ids=[0])
    return result.results[0]["out_0"]
```

```python
from contextlib import ExitStack

import numpy as np

import concourse.bass as bass
from concourse import mybir

F32 = mybir.dt.float32
F32R = mybir.dt.float32r
BF16 = mybir.dt.bfloat16
I32 = mybir.dt.int32
ALU = mybir.AluOpType
ACT = mybir.ActivationFunctionType
AX = mybir.AxisListType

P = 128
B, T, D = 16, 512, 256
H, DK = 16, 64
E, FF = 16, 128
KD = D // P
QT = T // P
NTOK = B * T
TT = NTOK // P
PAIRS = H // 2
HALVES = 2
HI, LO = 0, 1
SCALE = DK ** -0.5
EPS = 1e-5
MASKED = -1e30
SLOT_TILE = 256
SUB = SLOT_TILE // P
SLOT_TILES = 2 * NTOK // SLOT_TILE + E
SLOTS = SLOT_TILES * SLOT_TILE
WPART = KD * FF
WROW = 3 * WPART
PASSES = ((HI, HI), (LO, HI), (HI, LO))
START = 1
DMA = 16


def gate_cols(k):
    return slice(k * FF, (k + 1) * FF)


def up_cols(k):
    return slice(WPART + k * FF, WPART + (k + 1) * FF)


DOWN_COLS = slice(2 * WPART, 3 * WPART)


def wait_apart(eng, semaphore, value, begun):
    value = eng.to_reg(value)
    eng.wait_ge(begun, 1)
    eng.wait_ge(semaphore, value)


def stage_a(nc, ins, dram, keep):
    begun = keep["begun"]
    with ExitStack() as ctx:
        def sb(name, shape, dt=F32):
            return ctx.enter_context(nc.sbuf_tensor("a_" + name, shape, dt))

        def pb(name, shape, dt=F32):
            return ctx.enter_context(nc.psum_tensor("a_" + name, shape, dt))

        def sem(name):
            return ctx.enter_context(nc.semaphore("a_" + name))

        ident = keep["ident"]
        x_in = [sb(f"x_in{r}", [P, QT, D]) for r in range(2)]
        xn = [sb(f"xn{r}", [P, QT, D]) for r in range(2)]
        xnt = [sb(f"xnt{r}", [P, HALVES, KD, T], F32R) for r in range(2)]
        stats = [sb(f"stats{r}", [P, QT, 6]) for r in range(2)]
        mean_var = [sb(f"mean_var{r}", [P, QT, 2]) for r in range(2)]
        std = [sb(f"std{r}", [P, QT]) for r in range(2)]
        rstd = [sb(f"rstd{r}", [P, QT]) for r in range(2)]
        logits_t = [sb(f"logits_t{r}", [E, T]) for r in range(2)]
        gate_b = sb("gate_b", [E, 1])
        eps = sb("eps", [P, 1])
        gate_w = sb("gate_w", [P, KD, P])
        gate_w_split = sb("gate_w_split", [P, HALVES, KD, P], F32R)
        staged = sb("staged", [P, 4096])
        zeros = sb("zeros", [P, 2048])
        begun_at = sb("begun_at", [P, 1])
        probs = sb("probs", [P, TT, E])
        chosen = [sb(f"chosen{n}", [P, TT, E]) for n in range(2)]
        work = sb("work", [P, TT, E])
        spots = sb("spots", [P, TT, E])
        both = sb("both", [P, TT, E], BF16)
        best = [sb(f"best{n}", [P, TT]) for n in range(2)]
        mark = sb("mark", [P, TT])
        total = sb("total", [P, TT])
        rank_of_e = sb("rank_of_e", [P, E])
        rank_i = sb("rank_i", [P, E], I32)
        before = sb("before", [P, P], BF16)
        ones_b = sb("ones_b", [P, P], BF16)
        ones = sb("ones", [P, TT])
        tile_sum = sb("tile_sum", [P, TT, E])
        running = sb("running", [P, TT, E])
        padded_i = sb("padded_i", [P, E], I32)
        padded = sb("padded", [P, E])
        ends = sb("ends", [P, E])
        offset = sb("offset", [P, E])
        tile_i = sb("tile_i", [P, SLOT_TILES], I32)
        tile_start = sb("tile_start", [P, SLOT_TILES])
        row_i = sb("row_i", [P, 1], I32)
        row = sb("row", [P, 1])
        past = sb("past", [P, SLOT_TILES, E])
        expert = sb("expert", [P, SLOT_TILES])
        shared_in = sb("shared_in", [P, WROW])

        xt_ps = [pb(f"xt_ps{r}", [P, KD, T]) for r in range(2)]
        lg_ps = [pb(f"lg_ps{r}", [P, T]) for r in range(2)]
        lt_ps = [pb(f"lt_ps{r}", [P, QT, P]) for r in range(2)]

        x_loaded = [sem(f"x_loaded{r}") for r in range(2)]
        mean_done = sem("mean_done")
        std_done = sem("std_done")
        rstd_done = sem("rstd_done")
        xn_done = sem("xn_done")
        xt_ready = sem("xt_ready")
        hi_done = sem("hi_done")
        lo_done = sem("lo_done")
        lg_ready = sem("lg_ready")
        lg_out = sem("lg_out")
        lt_ready = sem("lt_ready")
        lt_out = sem("lt_out")
        xn_stored = [sem(f"xn_stored{r}") for r in range(2)]
        xnt_stored = [sem(f"xnt_stored{r}") for r in range(2)]
        const_loaded = sem("const_loaded")
        gw_hi = sem("gw_hi")
        gw_split = sem("gw_split")
        made = sem("made")
        stage_loaded = sem("stage_loaded")
        stage_hi = sem("stage_hi")
        stage_used = sem("stage_used")
        zeroed = sem("zeroed")
        zero_stored = sem("zero_stored")
        shared_loaded = sem("shared_loaded")
        shared_hi = sem("shared_hi")
        shared_split = sem("shared_split")
        sig_done = sem("sig_done")
        step = sem("step")
        both_ready = sem("both_ready")
        rank_ready = sem("rank_ready")

        x_src = ins["L0_attn_x"].rearrange("b (q p) d -> b p q d", p=P)
        wq_src = ins["L0_attn_Wq"].rearrange("h (k p) d -> k p h d", p=P)
        wk_src = ins["L0_attn_Wk"].rearrange("h (k p) d -> k p h d", p=P)
        wv_src = ins["L0_attn_Wv"].rearrange("h (k p) d -> k p h d", p=P)
        wo_src = ins["L0_attn_Wo"].rearrange("(j p) n -> p j n", p=P)
        wqk, wv, wo, shared = keep["wqk"], keep["wv"], keep["wo"], keep["shared"]

        def stage_view(n, src):
            if src is wo_src:
                return staged[:, 0:PAIRS * D].rearrange("p (j n) -> p j n", j=PAIRS)
            return staged[:, n * H * DK:(n + 1) * H * DK].rearrange("p (h d) -> p h d", h=H)

        loads = []
        for src, which in ((wq_src, 0), (wk_src, 1)):
            for k in range(KD):
                loads.append((src[k], stage_view(len(loads), src),
                              [wqk[:, :, which, hl, k, :].rearrange("p j (h d) -> p j h d", h=2) for hl in range(2)]))
        vo = [(wv_src[k], stage_view(k, wv_src), [wv[:, hl, k, :].rearrange("p (h d) -> p h d", h=H) for hl in range(2)])
              for k in range(KD)]
        rounds = [loads, vo, [(wo_src, stage_view(0, wo_src), [wo[:, hl, :, :] for hl in range(2)])]]

        with nc.Block() as block:
            @block.sync
            def _(sp):
                sp.dma_start(gate_b[:, :], ins["L0_ffn_gate_b"].rearrange("(n a) -> n a", a=1)).then_inc(const_loaded, DMA)
                sp.wait_ge(made, 1)
                sp.dma_start(gate_w[:, :, 0:E], ins["L0_ffn_gate_w"].rearrange("(k p) e -> p k e", p=P)
                             ).then_inc(const_loaded, DMA)

                def load_x(b, r):
                    sp.dma_start(x_in[r][:, :, :], x_src[bass.ds(b, 1)].rearrange("b p q d -> (b p) q d")
                                 ).then_inc(x_loaded[r], DMA)

                def store(b, r, more):
                    wait_apart(sp, xn_done, START + b + 1, begun)
                    if more:
                        load_x(b + 2, r)
                    sp.dma_start(dram["xn"][bass.ds(b, 1)].rearrange("b p q d -> (b p) q d"), xn[r][:, :, :]
                                 ).then_inc(xn_stored[r], DMA)
                    wait_apart(sp, lo_done, START + b * KD + KD, begun)
                    sp.dma_start(dram["xnt"][bass.ds(b, 1)].rearrange("b p n -> (b p) n"),
                                 xnt[r][:, :, :, :].rearrange("p a k t -> p (a k t)").bitcast(F32)
                                 ).then_inc(xnt_stored[r], DMA)

                load_x(0, 0)
                load_x(1, 1)
                with sp.Fori(0, B // 2 - 1) as g:
                    for r in range(2):
                        store(g * 2 + r, r, True)
                for r in range(2):
                    store(B - 2 + r, r, False)
                n = 0
                for k_round, round_ in enumerate(rounds):
                    if k_round:
                        sp.wait_ge(stage_used, n)
                    for src, view, _ in round_:
                        sp.dma_start(view, src).then_inc(stage_loaded, DMA)
                        n += 1
                    if k_round == 0:
                        for n_part, name in enumerate(("wg", "wu", "wd")):
                            src = ins["L0_ffn_shared_" + name]
                            to = shared_in[:, n_part * WPART:(n_part + 1) * WPART]
                            if n_part < 2:
                                to, src = to.rearrange("p (k f) -> p k f", k=KD), src.rearrange("(k p) f -> p k f", p=P)
                            sp.dma_start(to, src).then_inc(shared_loaded, DMA)
                for r in range(2):
                    sp.wait_ge(xn_stored[r], START + B // 2 * DMA)
                    sp.wait_ge(xnt_stored[r], START + B // 2 * DMA)

            @block.gpsimd
            def _(pool):
                for counter in (xn_done, xt_ready, lg_out, lt_out, *xnt_stored, *xn_stored, lo_done):
                    pool.sem_inc(counter, START)
                pool.memset(begun_at[:, :], 0.0).then_inc(begun, 1)
                pool.memset(gate_w[:, :, :], 0.0).then_inc(made, 1)
                pool.memset(zeros[:, :], 0.0).then_inc(zeroed, 1)
                pool.memset(eps[:, :], EPS).then_inc(made, 1)
                pool.memset(ones[:, :], 1.0).then_inc(made, 1)
                pool.memset(ones_b[:, :], 1.0).then_inc(made, 1)
                pool.memset(before[:, :], 1.0).then_inc(made, 1)
                pool.memset(ident[:, :], 0.0).then_inc(made, 1)
                pool.memset(keep["mask"][:, :], 0.0).then_inc(made, 1)
                pool.wait_ge(made, 7)
                pool.affine_select(out=before[:, :], in_=before[:, :], compare_op=ALU.is_gt, fill=0.0, base=0,
                                   pattern=[[1, P]], channel_multiplier=-1).then_inc(made, 1)
                pool.affine_select(out=ident[:, :], in_=ident[:, :], compare_op=ALU.not_equal, fill=1.0, base=0,
                                   pattern=[[-1, P]], channel_multiplier=1).then_inc(made, 1)
                pool.affine_select(out=keep["mask"][:, T - P:T], in_=keep["mask"][:, T - P:T], compare_op=ALU.is_ge,
                                   fill=MASKED, base=0, pattern=[[-1, P]], channel_multiplier=1).then_inc(made, 1)
                pool.iota(rank_i[:, :], pattern=[[-1, E]], base=E, channel_multiplier=0).then_inc(made, 1)
                pool.iota(tile_i[:, :], pattern=[[SLOT_TILE, SLOT_TILES]], base=0, channel_multiplier=0).then_inc(made, 1)
                pool.iota(row_i[:, :], pattern=[[0, 1]], base=0, channel_multiplier=1).then_inc(made, 1)
                n = 0
                for round_ in rounds:
                    for _, view, parts in round_:
                        n += 1
                        pool.wait_ge(stage_hi, n)
                        src = view if len(parts[HI].shape) == 3 else view.rearrange("p (j h) d -> p j h d", h=2)
                        pool.tensor_tensor(parts[LO], src, parts[HI].bitcast(F32), ALU.subtract).then_inc(stage_used, 1)
                pool.wait_ge(shared_hi, 1)
                pool.tensor_tensor(shared[:, LO, :], shared_in[:, :], shared[:, HI, :].bitcast(F32), ALU.subtract
                                   ).then_inc(shared_split, 1)

            @block.scalar
            def _(act):
                act.wait_ge(zeroed, 1)
                for n in range(SLOTS * D // (P * 2048)):
                    act.dma_start(dram["queued"].rearrange("(n p q) d -> n p (q d)", p=P, q=8)[n], zeros[:, :]
                                  ).then_inc(zero_stored, DMA)
                act.wait_ge(made, MADE)
                act.wait_ge(const_loaded, 2 * DMA)
                act.activation(gate_w_split[:, HI, :, :], gate_w[:, :, :], ACT.Copy).then_inc(gw_hi, 1)

                def deviation(b, r):
                    act.wait_ge(mean_done, b + 1)
                    act.activation(std[r][:, :], mean_var[r][:, :, 1], ACT.Sqrt, bias=eps[:, 0:1]).then_inc(std_done, 1)

                def split_xt(b, g, r):
                    act.wait_ge(xnt_stored[r], START + g * DMA)
                    for k in range(KD):
                        act.wait_ge(xt_ready, START + b * KD + k + 1)
                        act.activation(xnt[r][:, HI, k, :], xt_ps[r][:, k, :], ACT.Copy).then_inc(hi_done, 1)

                def take_logits(b, r):
                    act.wait_ge(lg_ready, b + 1)
                    act.activation(logits_t[r][:, :], lg_ps[r][0:E, :], ACT.Identity, bias=gate_b[:, 0:1]
                                   ).then_inc(lg_out, 1)

                deviation(0, 0)
                with act.Fori(0, B // 2 - 1) as g:
                    for r in range(2):
                        deviation(g * 2 + r + 1, 1 - r)
                        split_xt(g * 2 + r, g, r)
                        take_logits(g * 2 + r, r)
                deviation(B - 1, 1)
                for r in range(2):
                    split_xt(B - 2 + r, B // 2 - 1, r)
                    take_logits(B - 2 + r, r)
                n = 0
                for k_round, round_ in enumerate(rounds):
                    for _, view, parts in round_:
                        n += 1
                        act.wait_ge(stage_loaded, ROUND_LOADS(rounds, n) * DMA)
                        src = view if len(parts[HI].shape) == 3 else view.rearrange("p (j h) d -> p j h d", h=2)
                        act.activation(parts[HI], src, ACT.Copy).then_inc(stage_hi, 1)
                    if k_round == 0:
                        act.wait_ge(lt_out, START + B)
                        act.activation(probs[:, :, :], probs[:, :, :], ACT.Sigmoid).then_inc(sig_done, 1)
                act.wait_ge(shared_loaded, 3 * DMA)
                act.activation(shared[:, HI, :], shared_in[:, :], ACT.Copy).then_inc(shared_hi, 1)
                act.wait_ge(zero_stored, SLOTS * D // (P * 2048) * DMA)

            @block.vector
            def _(dve):
                dve.wait_ge(gw_hi, 1)
                dve.tensor_tensor(gate_w_split[:, LO, :, :], gate_w[:, :, :], gate_w_split[:, HI, :, :].bitcast(F32),
                                  ALU.subtract).then_inc(gw_split, 1)

                def moments(b, loads, r):
                    dve.wait_ge(x_loaded[r], loads * DMA)
                    for q in range(QT):
                        last = dve.bn_stats(stats[r][:, q, :], x_in[r][:, q, :])
                    last.then_inc(step, 1)
                    wait_apart(dve, step, b + 1, begun)
                    for q in range(QT):
                        last = dve.bn_aggr(mean_var[r][:, q, :], stats[r][:, q, :])
                    last.then_inc(mean_done, 1)

                def normalise(b, loads, r, free):
                    dve.wait_ge(std_done, b + 1)
                    dve.reciprocal(rstd[r][:, :], std[r][:, :]).then_inc(rstd_done, 1)
                    dve.wait_ge(rstd_done, b + 1)
                    dve.wait_ge(xn_stored[r], START + (loads - 1) * DMA)
                    if free is not None:
                        dve.wait_ge(xt_ready, free)
                    for q in range(QT):
                        last = dve.tensor_scalar(xn[r][:, q, :], x_in[r][:, q, :], mean_var[r][:, q, 0:1],
                                                 rstd[r][:, q:q + 1], ALU.subtract, ALU.mult)
                    last.then_inc(xn_done, 1)

                def split_xt(b, r):
                    for k in range(KD):
                        dve.wait_ge(hi_done, b * KD + k + 1)
                        dve.tensor_tensor(xnt[r][:, LO, k, :], xt_ps[r][:, k, :], xnt[r][:, HI, k, :].bitcast(F32),
                                          ALU.subtract).then_inc(lo_done, 1)

                def take_logits(b, r):
                    dve.wait_ge(lt_ready, b + 1)
                    dve.tensor_copy(probs[:, bass.ds(b * QT, QT), :], lt_ps[r][:, :, 0:E]).then_inc(lt_out, 1)

                moments(0, 1, 0)
                normalise(0, 1, 0, None)
                with dve.Fori(0, B // 2 - 1) as g:
                    for r in range(2):
                        b = g * 2 + r
                        moments(b + 1, g + 1 + r, 1 - r)
                        split_xt(b, r)
                        normalise(b + 1, g + 1 + r, 1 - r, START + b * KD)
                        take_logits(b, r)
                moments(B - 1, B // 2, 1)
                split_xt(B - 2, 0)
                normalise(B - 1, B // 2, 1, START + (B - 2) * KD)
                take_logits(B - 2, 0)
                split_xt(B - 1, 1)
                take_logits(B - 1, 1)

                count = [B]

                def then(instruction):
                    instruction.then_inc(step, 1)
                    count[0] += 1
                    dve.wait_ge(step, count[0])

                dve.wait_ge(made, MADE)
                then(dve.tensor_copy(rank_of_e[:, :], rank_i[:, :]))
                then(dve.tensor_copy(tile_start[:, :], tile_i[:, :]))
                then(dve.tensor_copy(row[:, :], row_i[:, :]))
                dve.wait_ge(sig_done, 1)
                by_e = lambda v: v[:, :, None].broadcast_to([P, TT, E])
                ranks = rank_of_e[:, None, :].broadcast_to([P, TT, E])
                for n in range(2):
                    then(dve.tensor_reduce(best[n][:, :], probs[:, :, :], AX.X, ALU.max))
                    then(dve.tensor_tensor(work[:, :, :], probs[:, :, :], by_e(best[n]), ALU.is_equal))
                    then(dve.tensor_tensor(work[:, :, :], work[:, :, :], ranks, ALU.mult))
                    then(dve.tensor_reduce(mark[:, :], work[:, :, :], AX.X, ALU.max))
                    then(dve.tensor_tensor(chosen[n][:, :, :], work[:, :, :], by_e(mark), ALU.is_equal))
                    if n == 0:
                        then(dve.scalar_tensor_tensor(probs[:, :, :].rearrange("p t e -> p (t e)"),
                                                      chosen[0][:, :, :].rearrange("p t e -> p (t e)"), -4.0,
                                                      probs[:, :, :].rearrange("p t e -> p (t e)"), ALU.mult, ALU.add))
                then(dve.tensor_tensor(total[:, :], best[0][:, :], best[1][:, :], ALU.add))
                then(dve.reciprocal(total[:, :], total[:, :]))
                for n in range(2):
                    then(dve.tensor_tensor(keep["weight"][n][:, :], best[n][:, :], total[:, :], ALU.mult))
                dve.tensor_tensor(both[:, :, :], chosen[0][:, :, :], chosen[1][:, :, :], ALU.add).then_inc(both_ready, 1)
                dve.wait_ge(rank_ready, 1)
                half = TT // 2
                for n in range(2):
                    then(dve.tensor_copy(tile_sum[:, n * half:(n + 1) * half, :],
                                         xt_ps[1][:, n, :].rearrange("p (t e) -> p t e", e=E)))
                for e in range(E):
                    then(dve.tensor_tensor_scan(running[:, :, e], ones[:, :], tile_sum[:, :, e], 0.0, ALU.mult, ALU.add))
                then(dve.tensor_scalar(padded[:, :], running[:, TT - 1, :], float(SLOT_TILE - 1), None, ALU.add))
                then(dve.tensor_copy(padded_i[:, :], padded[:, :]))
                shift = SLOT_TILE.bit_length() - 1
                then(dve.tensor_scalar(padded_i[:, :], padded_i[:, :], shift, shift, ALU.logical_shift_right,
                                       ALU.logical_shift_left))
                then(dve.tensor_copy(padded[:, :], padded_i[:, :]))
                then(dve.tensor_tensor_scan(ends[:, :], ones[:, 0:E], padded[:, :], 0.0, ALU.mult, ALU.add))
                then(dve.tensor_tensor(offset[:, :], ends[:, :], padded[:, :], ALU.subtract))
                then(dve.tensor_tensor(spots[:, :, :], running[:, :, :], tile_sum[:, :, :], ALU.subtract))
                then(dve.tensor_tensor(spots[:, :, :], spots[:, :, :], offset[:, None, :].broadcast_to([P, TT, E]), ALU.add))
                for n in range(2):
                    part = spots[:, n * half:(n + 1) * half, :]
                    then(dve.tensor_tensor(part, xt_ps[0][:, n, :].rearrange("p (t e) -> p t e", e=E), part, ALU.add))
                for n in range(2):
                    then(dve.tensor_tensor(work[:, :, :], chosen[n][:, :, :], spots[:, :, :], ALU.mult))
                    then(dve.tensor_reduce(mark[:, :], work[:, :, :], AX.X, ALU.add))
                    then(dve.tensor_copy(keep["slot"][n][:, :], mark[:, :]))
                then(dve.tensor_tensor(past[:, :, :], tile_start[:, :, None].broadcast_to([P, SLOT_TILES, E]),
                                       ends[:, None, :].broadcast_to([P, SLOT_TILES, E]), ALU.is_ge))
                then(dve.tensor_reduce(expert[:, :], past[:, :, :], AX.X, ALU.add))
                then(dve.tensor_scalar(expert[:, :], expert[:, :], float(E - 1), float(P), ALU.min, ALU.mult))
                then(dve.tensor_scalar(expert[:, :], expert[:, :], row[:, 0:1], None, ALU.add))
                then(dve.tensor_copy(keep["weight_row"][:, :], expert[:, :]))

            @block.tensor
            def _(pe):
                pe.wait_ge(made, MADE)
                pe.wait_ge(gw_split, 1)
                with pe.Fori(0, B // 2) as g:
                    for r in range(2):
                        b = g * 2 + r
                        pe.wait_ge(xn_done, START + b + 1)
                        pe.wait_ge(lo_done, START + g * 2 * KD)
                        for k in range(KD):
                            for q in range(QT):
                                last = pe.transpose(xt_ps[r][:, k, q * P:(q + 1) * P], xn[r][:, q, k * P:(k + 1) * P],
                                                    ident[:, :])
                            last.then_inc(xt_ready, 1)
                        pe.wait_ge(lo_done, START + (b + 1) * KD)
                        pe.wait_ge(lg_out, START + g * 2)
                        n = 0
                        for k in range(KD):
                            for wa, xb in PASSES:
                                n += 1
                                last = pe.matmul(lg_ps[r][:, :], gate_w_split[:, wa, k, :], xnt[r][:, xb, k, :],
                                                 start=(n == 1), stop=(n == KD * len(PASSES)))
                        last.then_inc(lg_ready, 1)
                        wait_apart(pe, lt_out, START + g * 2, begun)
                        wait_apart(pe, lg_out, START + b + 1, begun)
                        for q in range(QT):
                            last = pe.transpose(lt_ps[r][:, q, 0:E], logits_t[r][:, q * P:(q + 1) * P], ident[0:E, 0:E])
                        last.then_inc(lt_ready, 1)
                pe.wait_ge(both_ready, 1)
                flat = both[:, :, :].rearrange("p t e -> p (t e)")
                for n in range(2):
                    pe.matmul(xt_ps[0][:, n, :], before[:, :], flat[:, n * T:(n + 1) * T], start=True, stop=True)
                    last = pe.matmul(xt_ps[1][:, n, :], ones_b[:, :], flat[:, n * T:(n + 1) * T], start=True, stop=True)
                last.then_inc(rank_ready, 1)


MADE = 13


def ROUND_LOADS(rounds, n):
    upto = 0
    for round_ in rounds:
        upto += len(round_)
        if n <= upto:
            return upto
    return upto


def stage_b(nc, ins, dram, keep):
    begun = keep["begun"]
    with ExitStack() as ctx:
        def sb(name, shape, dt=F32):
            return ctx.enter_context(nc.sbuf_tensor("b_" + name, shape, dt))

        def pb(name, shape, dt=F32):
            return ctx.enter_context(nc.psum_tensor("b_" + name, shape, dt))

        def sem(name):
            return ctx.enter_context(nc.semaphore("b_" + name))

        ident, w = keep["ident"], keep["shared"]
        rows = [sb(f"rows{r}", [P, QT, D]) for r in range(2)]
        x = [sb(f"x{r}", [P, QT, D]) for r in range(2)]
        base = [sb(f"base{r}", [P, QT, D]) for r in range(2)]
        bo = sb("bo", [P, D])
        place = [sb(f"place{r}", [P, 2, QT], I32) for r in range(2)]
        xt = [sb(f"xt{r}", [P, HALVES, KD, T], F32R) for r in range(2)]
        tanh = sb("tanh", [P, T])
        gated = sb("gated", [P, T])
        hidden = [sb(f"hidden{r}", [P, T]) for r in range(2)]
        hs = [sb(f"hs{r}", [P, HALVES, T], F32R) for r in range(2)]
        xt_ps = [pb(f"xt_ps{r}", [P, KD, T]) for r in range(2)]
        gate_ps = pb("gate_ps", [P, T])
        up_ps = pb("up_ps", [P, T])
        y_ps = pb("y_ps", [P, QT, D])
        rows_loaded = [sem(f"rows_loaded{r}") for r in range(2)]
        x_loaded = [sem(f"x_loaded{r}") for r in range(2)]
        bo_loaded = sem("bo_loaded")
        placed = sem("placed")
        queued = [sem(f"queued{r}") for r in range(2)]
        packed = sem("packed")
        xt_ready, xt_hi, xt_done = sem("xt_ready"), sem("xt_hi"), sem("xt_done")
        gu_ready, tanh_done, gated_done, hidden_done = sem("gu_ready"), sem("tanh_done"), sem("gated_done"), sem("hidden_done")
        hs_hi, hs_done, y_ready = sem("hs_hi"), sem("hs_done"), sem("y_ready")
        x_summed, bo_summed, base_done = sem("x_summed"), sem("bo_summed"), sem("base_done")
        base_stored = [sem(f"base_stored{r}") for r in range(2)]
        x_src = ins["L0_attn_x"].rearrange("b (q p) d -> b p q d", p=P)
        SCATTERS = 2 * QT

        with nc.Block() as block:
            @block.sync
            def _(sp):
                def load(b, g, r):
                    if g is not None:
                        wait_apart(sp, queued[r], g * SCATTERS * DMA, begun)
                        wait_apart(sp, x_summed, b - 1, begun)
                        wait_apart(sp, xt_ready, (b - 1) * KD, begun)
                    sp.dma_start(rows[r][:, :, :], dram["xn"][bass.ds(b, 1)].rearrange("b p q d -> (b p) q d")
                                 ).then_inc(rows_loaded[r], DMA)
                    sp.dma_start(x[r][:, :, :], x_src[bass.ds(b, 1)].rearrange("b p q d -> (b p) q d")
                                 ).then_inc(x_loaded[r], DMA)

                def store(b, r):
                    wait_apart(sp, base_done, START + b + 1, begun)
                    sp.dma_start(dram["base"][bass.ds(b, 1)].rearrange("b p q d -> (b p) q d"), base[r][:, :, :]
                                 ).then_inc(base_stored[r], DMA)

                load(0, None, 0)
                load(1, None, 1)
                sp.dma_start(bo[:, :], ins["L0_attn_bo"].rearrange("(a n) -> a n", a=1).broadcast_to([P, D])
                             ).then_inc(bo_loaded, DMA)
                with sp.Fori(0, B // 2 - 1) as g:
                    for r in range(2):
                        load(g * 2 + r + 2, g + 1, r)
                    for r in range(2):
                        store(g * 2 + r, r)
                for r in range(2):
                    store(B - 2 + r, r)
                    sp.wait_ge(base_stored[r], START + B // 2 * DMA)

            @block.gpsimd
            def _(pool):
                for counter in (gu_ready, hidden_done, base_done, y_ready, *base_stored, xt_done):
                    pool.sem_inc(counter, START)
                with pool.Fori(0, B // 2) as g:
                    for r in range(2):
                        wait_apart(pool, rows_loaded[r], (g + 1) * DMA, begun)
                        wait_apart(pool, placed, (g * 2 + r + 1) * 2, begun)
                        for q in range(QT):
                            for n in range(2):
                                pool.indirect_dma_start(
                                    out=dram["queued"][:, :],
                                    out_offset=bass.IndirectOffsetOnAxis(ap=place[r][:, n, q:q + 1], axis=0),
                                    in_=rows[r][:, q, :], in_offset=None,
                                    bounds_check=SLOTS - 1, oob_is_err=False).then_inc(queued[r], DMA)
                for r in range(2):
                    pool.wait_ge(queued[r], B // 2 * SCATTERS * DMA)

            @block.tensor
            def _(pe):
                with pe.Fori(0, B // 2) as g:
                    for r in range(2):
                        pe.wait_ge(rows_loaded[r], (g + 1) * DMA)
                        pe.wait_ge(xt_done, START + g * 2 * KD)
                        for k in range(KD):
                            for q in range(QT):
                                last = pe.transpose(xt_ps[r][:, k, q * P:(q + 1) * P], rows[r][:, q, k * P:(k + 1) * P],
                                                    ident[:, :])
                            last.then_inc(xt_ready, 1)
                    for r in range(2):
                        b = g * 2 + r
                        pe.wait_ge(xt_done, START + (b + 1) * KD)
                        pe.wait_ge(hidden_done, START + b)
                        for to, cols in ((gate_ps, gate_cols), (up_ps, up_cols)):
                            n = 0
                            for k in range(KD):
                                for wa, xb in PASSES:
                                    n += 1
                                    last = pe.matmul(to[:, :], w[:, wa, cols(k)], xt[r][:, xb, k, :], start=(n == 1),
                                                     stop=(n == KD * len(PASSES)))
                        last.then_inc(gu_ready, 1)
                    for r in range(2):
                        b = g * 2 + r
                        pe.wait_ge(hs_done, b + 1)
                        pe.wait_ge(base_done, START + b)
                        for q in range(QT):
                            for n, (ha, wb) in enumerate(PASSES):
                                last = pe.matmul(y_ps[:, q, :], hs[r][:, ha, q * P:(q + 1) * P], w[:, wb, DOWN_COLS],
                                                 start=(n == 0), stop=(n == len(PASSES) - 1))
                        last.then_inc(y_ready, 1)

            @block.scalar
            def _(act):
                for n, name in enumerate(("wg", "wu", "wd")):
                    to = dram["experts"][:, :, n * WPART:(n + 1) * WPART]
                    src = ins["L0_ffn_experts_" + name]
                    for k in range(KD if n < 2 else 1):
                        part = (to[:, :, k * FF:(k + 1) * FF], src[:, k * P:(k + 1) * P, :]) if n < 2 else (to, src)
                        act.dma_start(*part).then_inc(packed, DMA)
                with act.Fori(0, B // 2) as g:
                    for r in range(2):
                        b = g * 2 + r
                        act.wait_ge(gu_ready, START + g * 2)
                        for k in range(KD):
                            act.wait_ge(xt_ready, b * KD + k + 1)
                            act.activation(xt[r][:, HI, k, :], xt_ps[r][:, k, :], ACT.Copy).then_inc(xt_hi, 1)
                    for r in range(2):
                        b = g * 2 + r
                        act.wait_ge(gu_ready, START + b + 1)
                        act.wait_ge(hidden_done, START + b)
                        act.activation(tanh[:, :], gate_ps[:, :], ACT.Tanh, scale=0.5).then_inc(tanh_done, 1)
                        act.wait_ge(hidden_done, START + b + 1)
                        act.wait_ge(y_ready, START + g * 2)
                        act.activation(hs[r][:, HI, :], hidden[r][:, :], ACT.Copy).then_inc(hs_hi, 1)
                act.wait_ge(packed, (2 * KD + 1) * DMA)

            @block.vector
            def _(dve):
                dve.wait_ge(bo_loaded, DMA)
                with dve.Fori(0, B // 2) as g:
                    def split_xt(r):
                        for k in range(KD):
                            dve.wait_ge(xt_hi, (g * 2 + r) * KD + k + 1)
                            dve.tensor_tensor(xt[r][:, LO, k, :], xt_ps[r][:, k, :], xt[r][:, HI, k, :].bitcast(F32),
                                              ALU.subtract).then_inc(xt_done, 1)

                    def hide(r):
                        b = g * 2 + r
                        dve.wait_ge(tanh_done, b + 1)
                        dve.scalar_tensor_tensor(gated[:, :], tanh[:, :], 1.0, gate_ps[:, :], ALU.add, ALU.mult
                                                 ).then_inc(gated_done, 1)
                        dve.wait_ge(gated_done, b + 1)
                        dve.scalar_tensor_tensor(hidden[r][:, :], gated[:, :], 0.5, up_ps[:, :], ALU.mult, ALU.mult
                                                 ).then_inc(hidden_done, 1)

                    def split_hidden(r):
                        dve.wait_ge(hs_hi, g * 2 + r + 1)
                        dve.tensor_tensor(hs[r][:, LO, :], hidden[r][:, :], hs[r][:, HI, :].bitcast(F32),
                                          ALU.subtract).then_inc(hs_done, 1)

                    def add_x(r):
                        dve.wait_ge(x_loaded[r], (g + 1) * DMA)
                        dve.wait_ge(base_stored[r], START + g * DMA)
                        dve.tensor_tensor(base[r][:, :, :], x[r][:, :, :], rows[r][:, :, :], ALU.add).then_inc(x_summed, 1)

                    def add_bo(r):
                        dve.wait_ge(x_summed, g * 2 + r + 1)
                        dve.tensor_tensor(base[r][:, :, :], base[r][:, :, :], bo[:, None, :].broadcast_to([P, QT, D]),
                                          ALU.add).then_inc(bo_summed, 1)

                    def add_shared(r):
                        b = g * 2 + r
                        dve.wait_ge(y_ready, START + b + 1)
                        dve.wait_ge(bo_summed, b + 1)
                        dve.tensor_tensor(base[r][:, :, :], y_ps[:, :, :], base[r][:, :, :], ALU.add).then_inc(base_done, 1)

                    for r in range(2):
                        dve.wait_ge(rows_loaded[r], (g + 1) * DMA)
                        for n in range(2):
                            dve.tensor_copy(place[r][:, n, :], keep["slot"][n][:, bass.ds((g * 2 + r) * QT, QT)]
                                            ).then_inc(placed, 1)
                        split_xt(r)
                    add_x(0)
                    hide(0)
                    add_x(1)
                    split_hidden(0)
                    add_bo(0)
                    hide(1)
                    add_bo(1)
                    split_hidden(1)
                    add_shared(0)
                    add_shared(1)


def stage_c(nc, dram, keep):
    begun = keep["begun"]
    with ExitStack() as ctx:
        def sb(name, shape, dt=F32):
            return ctx.enter_context(nc.sbuf_tensor("c_" + name, shape, dt))

        def pb(name, shape, dt=F32):
            return ctx.enter_context(nc.psum_tensor("c_" + name, shape, dt))

        def sem(name):
            return ctx.enter_context(nc.semaphore("c_" + name))

        DEEP = 4
        FETCH = 6
        ident = keep["ident"]
        row = [sb(f"row{r}", [P, 1], I32) for r in range(DEEP)]
        w_in = [sb(f"w_in{r}", [P, WROW]) for r in range(DEEP)]
        w = [sb(f"w{r}", [P, HALVES, WROW], F32R) for r in range(DEEP)]
        x = [sb(f"x{r}", [P, SUB, D]) for r in range(DEEP)]
        xt = [sb(f"xt{r}", [P, HALVES, KD, SLOT_TILE], F32R) for r in range(2)]
        tanh = [sb(f"tanh{r}", [P, SLOT_TILE]) for r in range(2)]
        gated = [sb(f"gated{r}", [P, SLOT_TILE]) for r in range(2)]
        hidden = [sb(f"hidden{r}", [P, SLOT_TILE]) for r in range(2)]
        hs = [sb(f"hs{r}", [P, HALVES, SLOT_TILE], F32R) for r in range(2)]
        y = [sb(f"y{r}", [P, SUB, D]) for r in range(DEEP)]
        xt_ps = [pb(f"xt_ps{r}", [P, KD, SLOT_TILE]) for r in range(2)]
        gu_ps = [pb(f"gu_ps{r}", [P, 2, SLOT_TILE]) for r in range(2)]
        y_ps = [pb(f"y_ps{r}", [P, SUB, D]) for r in range(2)]
        row_done = sem("row_done")
        w_loaded = [sem(f"w_loaded{r}") for r in range(DEEP)]
        x_loaded = [sem(f"x_loaded{r}") for r in range(DEEP)]
        y_stored = [sem(f"y_stored{r}") for r in range(DEEP)]
        w_hi, w_split = sem("w_hi"), sem("w_split")
        xt_ready, xt_hi, xt_done = sem("xt_ready"), sem("xt_hi"), sem("xt_done")
        gu_ready, tanh_done, gated_done, hidden_done = sem("gu_ready"), sem("tanh_done"), sem("gated_done"), sem("hidden_done")
        hs_hi, hs_done, y_ready, y_done = sem("hs_hi"), sem("hs_done"), sem("y_ready"), sem("y_done")
        ROUNDS = SLOT_TILES // DEEP

        def ticks(eng, before, tick):
            for t in range(-before, 0):
                tick(t, -1, t % DEEP, lambda a, t=t: t + a >= 0)
            with eng.Fori(0, ROUNDS - 2) as g:
                for r in range(DEEP):
                    tick(g * DEEP + r, g, r, lambda a: True)
            for t in range(SLOT_TILES - 2 * DEEP, SLOT_TILES):
                tick(t, t // DEEP, t % DEEP, lambda a, t=t: t + a < SLOT_TILES)

        def round_of(g, r, ahead):
            return g + (r + ahead) // DEEP

        with nc.Block() as block:
            @block.sync
            def _(sp):
                def load(t, r):
                    sp.dma_start(x[r][:, :, :], dram["queued"][bass.ds(t * SLOT_TILE, SLOT_TILE), :]
                                 .rearrange("(s p) d -> p s d", p=P)).then_inc(x_loaded[r], DMA)

                def tick(t, g, r, there):
                    if there(FETCH):
                        wait_apart(sp, xt_ready, START + t + FETCH - DEEP + 1, begun)
                        load(t + FETCH, (r + FETCH) % DEEP)
                    wait_apart(sp, y_done, START + t + 1, begun)
                    sp.dma_start(dram["routed"][bass.ds(t * SLOT_TILE, SLOT_TILE), :]
                                 .rearrange("(s p) d -> p s d", p=P), y[r][:, :, :]).then_inc(y_stored[r], DMA)

                for t in range(FETCH):
                    if t >= DEEP:
                        sp.wait_ge(xt_ready, START + t - DEEP + 1)
                    load(t, t % DEEP)
                ticks(sp, 0, tick)
                for r in range(DEEP):
                    sp.wait_ge(y_stored[r], START + ROUNDS * DMA)

            @block.gpsimd
            def _(pool):
                for counter in (xt_ready, gu_ready, y_ready, xt_done, hidden_done, y_done, *y_stored, w_split):
                    pool.sem_inc(counter, START)

                def gather(t, r):
                    wait_apart(pool, row_done, t + 1, begun)
                    pool.indirect_dma_start(
                        out=w_in[r][:, :], out_offset=None, in_=dram["experts"].rearrange("e p n -> (e p) n"),
                        in_offset=bass.IndirectOffsetOnAxis(ap=row[r][:, 0:1], axis=0),
                        bounds_check=E * P - 1, oob_is_err=False).then_inc(w_loaded[r], DMA)

                def split(t, r):
                    wait_apart(pool, w_hi, t + 1, begun)
                    pool.tensor_tensor(w[r][:, LO, :], w_in[r][:, :], w[r][:, HI, :].bitcast(F32), ALU.subtract
                                       ).then_inc(w_split, 1)

                def tick(t, g, r, there):
                    if there(3):
                        split(t + 3, (r + 3) % DEEP)
                    if there(FETCH):
                        wait_apart(pool, w_split, START + t + 3, begun)
                        gather(t + FETCH, (r + FETCH) % DEEP)

                for r in range(DEEP):
                    gather(r, r)
                for r in range(3):
                    split(r, r)
                    if r + DEEP < FETCH:
                        wait_apart(pool, w_split, START + r + 1, begun)
                        gather(r + DEEP, r)
                ticks(pool, 0, tick)

            @block.tensor
            def _(pe):
                def tick(t, g, r, there):
                    if there(2):
                        h = (r + 2) % DEEP
                        pe.wait_ge(x_loaded[h], (round_of(g, r, 2) + 1) * DMA)
                        if there(0):
                            pe.wait_ge(xt_done, START + t + 1)
                        for k in range(KD):
                            for s in range(SUB):
                                last = pe.transpose(xt_ps[r % 2][:, k, s * P:(s + 1) * P], x[h][:, s, k * P:(k + 1) * P],
                                                    ident[:, :])
                        last.then_inc(xt_ready, 1)
                    if there(1):
                        o, h = (r + 1) % 2, (r + 1) % DEEP
                        pe.wait_ge(xt_done, START + t + 2)
                        pe.wait_ge(w_split, START + t + 2)
                        if there(0):
                            pe.wait_ge(hidden_done, START + t)
                        for part, cols in enumerate((gate_cols, up_cols)):
                            n = 0
                            for k in range(KD):
                                for wa, xb in PASSES:
                                    n += 1
                                    last = pe.matmul(gu_ps[o][:, part, :], w[h][:, wa, cols(k)], xt[o][:, xb, k, :],
                                                     start=(n == 1), stop=(n == KD * len(PASSES)))
                        last.then_inc(gu_ready, 1)
                    if there(0):
                        pe.wait_ge(hs_done, t + 1)
                        pe.wait_ge(y_done, START + t)
                        for s in range(SUB):
                            for n, (ha, wb) in enumerate(PASSES):
                                last = pe.matmul(y_ps[r % 2][:, s, :], hs[r % 2][:, ha, s * P:(s + 1) * P],
                                                 w[r][:, wb, DOWN_COLS], start=(n == 0), stop=(n == len(PASSES) - 1))
                        last.then_inc(y_ready, 1)

                pe.wait_ge(w_split, START)
                ticks(pe, 2, tick)

            @block.scalar
            def _(act):
                def split_weights(g, r):
                    act.wait_ge(w_loaded[r], (g + 1) * DMA)
                    act.activation(w[r][:, HI, :], w_in[r][:, :], ACT.Copy).then_inc(w_hi, 1)

                def take_y(t, g, r):
                    act.wait_ge(y_ready, START + t + 1)
                    act.wait_ge(y_stored[r], START + g * DMA)
                    act.activation(y[r][:, :, :], y_ps[r % 2][:, :, :], ACT.Copy).then_inc(y_done, 1)

                def tick(t, g, r, there):
                    if there(2):
                        act.wait_ge(xt_ready, START + t + 3)
                        if there(0):
                            act.wait_ge(gu_ready, START + t + 1)
                        act.activation(xt[r % 2][:, HI, :, :], xt_ps[r % 2][:, :, :], ACT.Copy).then_inc(xt_hi, 1)
                    if there(1):
                        o = (r + 1) % 2
                        act.wait_ge(gu_ready, START + t + 2)
                        act.activation(tanh[o][:, :], gu_ps[o][:, 0, :], ACT.Tanh, scale=0.5).then_inc(tanh_done, 1)
                    if there(0) and there(3):
                        act.wait_ge(y_ready, START + t)
                        split_weights(round_of(g, r, 3), (r + 3) % DEEP)
                    if there(1):
                        if there(0):
                            act.wait_ge(y_ready, START + t)
                        act.wait_ge(hidden_done, START + t + 2)
                        act.activation(hs[o][:, HI, :], hidden[o][:, :], ACT.Copy).then_inc(hs_hi, 1)
                    if there(0):
                        take_y(t, g, r)

                for r in range(3):
                    split_weights(0, r)
                ticks(act, 2, tick)

            @block.vector
            def _(dve):
                def look_up(t, r):
                    dve.tensor_copy(row[r][:, :], keep["weight_row"][:, bass.ds(t, 1)]).then_inc(row_done, 1)

                def tick(t, g, r, there):
                    if there(0) and there(FETCH):
                        dve.wait_ge(w_loaded[(r + 2) % DEEP], (round_of(g, r, 2) + 1) * DMA)
                        look_up(t + FETCH, (r + FETCH) % DEEP)
                    if there(2):
                        dve.wait_ge(xt_hi, t + 3)
                        dve.tensor_tensor(xt[r % 2][:, LO, :, :], xt_ps[r % 2][:, :, :],
                                          xt[r % 2][:, HI, :, :].bitcast(F32), ALU.subtract).then_inc(xt_done, 1)
                    if there(1):
                        o = (r + 1) % 2
                        dve.wait_ge(tanh_done, t + 2)
                        dve.scalar_tensor_tensor(gated[o][:, :], tanh[o][:, :], 1.0, gu_ps[o][:, 0, :], ALU.add, ALU.mult
                                                 ).then_inc(gated_done, 1)
                        dve.wait_ge(gated_done, t + 2)
                        dve.scalar_tensor_tensor(hidden[o][:, :], gated[o][:, :], 0.5, gu_ps[o][:, 1, :], ALU.mult,
                                                 ALU.mult).then_inc(hidden_done, 1)
                        dve.wait_ge(hs_hi, t + 2)
                        dve.tensor_tensor(hs[o][:, LO, :], hidden[o][:, :], hs[o][:, HI, :].bitcast(F32),
                                          ALU.subtract).then_inc(hs_done, 1)

                for t in range(FETCH):
                    if t >= DEEP:
                        dve.wait_ge(w_loaded[t % DEEP], DMA)
                    look_up(t, t % DEEP)
                ticks(dve, 2, tick)


def stage_d(nc, dram, keep, out):
    begun = keep["begun"]
    with ExitStack() as ctx:
        def sb(name, shape, dt=F32):
            return ctx.enter_context(nc.sbuf_tensor("d_" + name, shape, dt))

        def sem(name):
            return ctx.enter_context(nc.semaphore("d_" + name))

        ident, mask = keep["ident"], keep["mask"]
        wv, wo = keep["wv"], keep["wo"]
        w_pair = [sb(f"w_pair{n}", [P, HALVES, KD, P], F32R) for n in range(2)]
        xnt = sb("xnt", [P, HALVES, KD, T], F32R)
        qs = [[sb(f"qs{r}{h}", [P, T], F32R) for h in range(2)] for r in range(2)]
        ks = [[[sb(f"ks{r}{h}{hl}", [P, T], F32R) for hl in range(HALVES)] for h in range(2)] for r in range(2)]
        v = sb("v", [P, QT, H * DK])
        vp = sb("vp", [P, 2, QT, P])
        probs = [[sb(f"probs{i}{h}", [P, T]) for h in range(2)] for i in range(QT)]
        probs_t = [[sb(f"probs_t{h}{i}", [P, QT, P]) for i in range(2)] for h in range(2)]
        out_t = [sb(f"out_t{hl}", [P, PAIRS, T], F32R) for hl in range(HALVES)]
        top = [sb(f"top{i}", [P, 2]) for i in range(QT)]
        bias = [sb(f"bias{i}", [P, 2]) for i in range(QT)]
        total = [sb(f"total{i}", [P, 2]) for i in range(QT)]
        inverse = [sb(f"inverse{i}", [P, 2]) for i in range(QT)]
        base = sb("base", [P, QT, D])
        summed = sb("summed", [P, QT, D])
        routed = sb("routed", [P, 2, QT, D])
        place = sb("place", [P, 2, QT], I32)
        share = sb("share", [P, 2, QT])

        def bank(name):
            return ctx.enter_context(nc.psum_tensor("d_" + name, [P, T], F32))

        s_ps = [[bank(f"s_ps{r}{h}") for h in range(2)] for r in range(2)]
        t_ps = [bank(f"t_ps{h}") for h in range(2)]
        o_ps = bank("o_ps")
        m_ps = bank("m_ps")

        xnt_loaded, base_loaded, stored = sem("xnt_loaded"), sem("base_loaded"), sem("stored")
        w_loaded = [sem(f"w_loaded{n}") for n in range(2)]
        cleared = sem("cleared")
        m_ready = sem("m_ready")
        m_hi, m_out = sem("m_hi"), sem("m_out")
        s_ready = sem("s_ready")
        s_out = sem("s_out")
        bias_done = sem("bias_done")
        exp_done = sem("exp_done")
        inverse_done = sem("inverse_done")
        norm_done = sem("norm_done")
        t_ready = [sem(f"t_ready{h}") for h in range(2)]
        t_out = [sem(f"t_out{h}") for h in range(2)]
        o_ready, o_hi, o_out = sem("o_ready"), sem("o_hi"), sem("o_out")

        placed, gathered, shared_out = sem("placed"), sem("gathered"), sem("shared_out")
        weighted, first_added, routed_added = sem("weighted"), sem("first_added"), sem("routed_added")
        out_d = out.rearrange("b (q p) d -> b p q d", p=P)

        vp_loaded = [sem(f"vp_loaded{r}") for r in range(2)]
        k_copied = [sem(f"k_copied{r}") for r in range(2)]

        V_GROUPS = 2 * QT
        T_FIRST = V_GROUPS // 2
        T_USES = [QT * PAIRS + V_GROUPS // 2, QT * PAIRS + V_GROUPS // 2 + QT // 2]
        PROJ = 2 * PAIRS
        M_USES = PROJ + QT // 2
        M_OUTS = 2 * PROJ + QT // 2
        M_FIRST = 4
        GATHERS = 2 * QT
        K_COLS = [max(2 * P, (i + 1) * P) for i in range(QT)]

        def unit(b, jp, r):
            return b * PAIRS + jp * 2 + r

        def head_half(h):
            return slice(h * DK, (h + 1) * DK)

        with nc.Block() as block:
            @block.sync
            def _(sp):
                def load_weights(which, pair):
                    sp.dma_start(w_pair[which][:, :, :, :].rearrange("p s k n -> p (s k n)").bitcast(F32),
                                 keep["wqk"][:, bass.ds(pair, 1), which, :, :, :].rearrange("p j s k n -> p (j s k n)").bitcast(F32)
                                 ).then_inc(w_loaded[which], DMA)

                def load_xnt(batch):
                    sp.dma_start(xnt[:, :, :, :].rearrange("p a k t -> p (a k t)").bitcast(F32),
                                 dram["xnt"][bass.ds(batch, 1)].rearrange("b p n -> (b p) n")).then_inc(xnt_loaded, DMA)

                def load_v_pair(pair, r):
                    sp.dma_start(vp[:, r, :, :], v[:, :, bass.ds(pair * P, P)]).then_inc(vp_loaded[r], DMA)

                def copy_keys(r):
                    for h in range(2):
                        sp.dma_start(ks[r][h][HI][head_half(1 - h), :].bitcast(F32), ks[r][h][HI][head_half(h), :].bitcast(F32)
                                     ).then_inc(k_copied[r], DMA)

                load_xnt(0)
                load_weights(1, 0)
                load_weights(0, 0)
                sp.wait_ge(m_ready, 1)
                load_weights(1, 1)
                sp.wait_ge(m_ready, 2)
                load_weights(0, 1)
                sp.wait_ge(m_hi, 2)
                copy_keys(0)
                sp.wait_ge(m_ready, 3)
                load_weights(1, 2)
                sp.wait_ge(m_ready, 4)
                load_weights(0, 2)
                sp.wait_ge(m_hi, 6)
                copy_keys(1)
                for h in range(2):
                    sp.wait_ge(t_out[h], T_FIRST)
                load_v_pair(0, 0)
                with sp.Fori(0, B) as b:
                    def load_v(un, r):
                        wait_apart(sp, o_ready, START + b * PAIRS + un, begun)
                        load_v_pair(un + 1, 1 - r)

                    def load_keys(un, pair):
                        wait_apart(sp, m_ready, M_FIRST + b * M_USES + un * 2 + 1, begun)
                        load_weights(1, pair)

                    def copy_split_keys(un, r):
                        wait_apart(sp, m_hi, 2 * M_FIRST + (b * PAIRS + un) * 4 + 2, begun)
                        copy_keys(r)

                    def load_queries(un, pair):
                        wait_apart(sp, m_ready, M_FIRST + b * M_USES + un * 2 + 2, begun)
                        load_weights(0, pair)

                    wait_apart(sp, m_out, b * M_OUTS + 2 * M_FIRST, begun)
                    wait_apart(sp, t_out[1], b * T_USES[1] + T_FIRST, begun)
                    sp.dma_start(base[:, :, :], dram["base"][bass.ds(b, 1)].rearrange("b p q d -> (b p) q d")
                                 ).then_inc(base_loaded, DMA)
                    with sp.Fori(0, PAIRS // 2 - 1) as jp:
                        for r in range(2):
                            un = jp * 2 + r
                            load_v(un, r)
                            load_keys(un, (un + 3) & (PAIRS - 1))
                            copy_split_keys(un, r)
                            load_queries(un, (un + 3) & (PAIRS - 1))
                    load_xnt((b + 1) & (B - 1))
                    load_v(PAIRS - 2, 0)
                    load_keys(PAIRS - 2, 1)
                    copy_split_keys(PAIRS - 2, 0)
                    load_queries(PAIRS - 2, 1)
                    load_keys(PAIRS - 1, 2)
                    copy_split_keys(PAIRS - 1, 1)
                    load_queries(PAIRS - 1, 2)
                    for h in range(2):
                        wait_apart(sp, t_out[h], b * T_USES[h] + QT * PAIRS + 2 * T_FIRST, begun)
                    load_v_pair(0, 0)
                    wait_apart(sp, t_out[1], (b + 1) * T_USES[1] + T_FIRST, begun)
                    wait_apart(sp, m_out, (b + 1) * M_OUTS + 2 * M_FIRST, begun)
                    sp.dma_start(out_d[bass.ds(b, 1)].rearrange("b p q d -> (b p) q d"), summed[:, :, :]
                                 ).then_inc(stored, DMA)
                sp.wait_ge(stored, START + B * DMA)
                sp.wait_ge(vp_loaded[0], (B * PAIRS // 2 + 1) * DMA)
                sp.wait_ge(vp_loaded[1], B * PAIRS // 2 * DMA)
                for r in range(2):
                    sp.wait_ge(k_copied[r], (B * PAIRS // 2 + 1) * 2 * DMA)
                sp.wait_ge(w_loaded[0], (B * PAIRS + 3) * DMA)
                sp.wait_ge(w_loaded[1], (B * PAIRS + 3) * DMA)

            @block.tensor
            def _(pe):
                def project(which, loaded, before):
                    pe.wait_ge(w_loaded[which], loaded)
                    if before is not None:
                        pe.wait_ge(m_hi, before[0])
                        pe.wait_ge(m_out, before[1])
                    n = 0
                    for k in range(KD):
                        for wa, xb in PASSES:
                            n += 1
                            last = pe.matmul(m_ps[:, :], w_pair[which][:, wa, k, :], xnt[:, xb, k, :], start=(n == 1),
                                             stop=(n == KD * len(PASSES)))
                    last.then_inc(m_ready, 1)

                def scores(r, i, outs, before):
                    if outs is not None:
                        pe.wait_ge(m_out, outs[0])
                        pe.wait_ge(k_copied[r], outs[1])
                    for h in range(2):
                        if before is not None:
                            pe.wait_ge(s_out, before * 2 + h + 1)
                        cols = K_COLS[i]
                        for hl in range(HALVES):
                            last = pe.matmul(s_ps[i % 2][h][:, 0:cols], qs[r][h][:, i * P:(i + 1) * P],
                                             ks[r][h][hl][:, 0:cols], start=(hl == 0), stop=(hl == 1))
                        last.then_inc(s_ready, 1)

                def transposes(i, step_no, uses):
                    for h in range(2):
                        pe.wait_ge(norm_done, step_no * 2 + h + 1)
                        pe.wait_ge(t_out[h], uses[h])
                        for j in range(i + 1):
                            last = pe.transpose(t_ps[h][:, j * P:(j + 1) * P], probs[i][h][:, j * P:(j + 1) * P], ident[:, :])
                        last.then_inc(t_ready[h], 1)

                def weigh(r, i, u, uses, copied):
                    if i == 0:
                        pe.wait_ge(o_out, START + u)
                        pe.wait_ge(vp_loaded[r], copied)
                    for h in range(2):
                        pe.wait_ge(t_out[h], uses[h] + 1)
                    for j in range(i + 1):
                        for h in range(2):
                            last = pe.matmul(o_ps[head_half(h), i * P:(i + 1) * P], vp[:, r, j, head_half(h)],
                                             probs_t[h][i % 2][:, j, :], start=(j == 0), stop=(j == i))
                    if i == QT - 1:
                        last.then_inc(o_ready, 1)

                def project_v(first_uses):
                    for g in range(V_GROUPS):
                        tok, half = divmod(g, 2)
                        if first_uses is not None:
                            pe.wait_ge(t_out[half], first_uses[half] + tok)
                        elif tok:
                            pe.wait_ge(t_out[half], tok)
                        n = 0
                        for k in range(KD):
                            for xa, wb in PASSES:
                                n += 1
                                last = pe.matmul(t_ps[half][:, :], xnt[:, xa, k, tok * P:(tok + 1) * P],
                                                 wv[:, wb, k, half * T:(half + 1) * T], start=(n == 1),
                                                 stop=(n == KD * len(PASSES)))
                        last.then_inc(t_ready[half], 1)

                def project_out(b, t_uses, outs):
                    for q in range(QT):
                        if q % 2 == 0:
                            to = t_ps[1]
                            pe.wait_ge(t_out[1], t_uses + q // 2)
                        else:
                            to = m_ps
                            pe.wait_ge(m_out, outs + q // 2)
                        for j in range(PAIRS):
                            if j == PAIRS - 1 and q == 0:
                                pe.wait_ge(o_out, START + (b + 1) * PAIRS)
                            elif j == 0 and q == 0:
                                pe.wait_ge(o_out, START + (b + 1) * PAIRS - 1)
                            for n, (oa, wb) in enumerate(PASSES):
                                last = pe.matmul(to[:, 0:D], out_t[oa][:, j, q * P:(q + 1) * P], wo[:, wb, j, :],
                                                 start=(j == 0 and n == 0),
                                                 stop=(j == PAIRS - 1 and n == len(PASSES) - 1))
                        last.then_inc(t_ready[1] if q % 2 == 0 else m_ready, 1)

                pe.wait_ge(xnt_loaded, DMA)
                project_v(None)
                project(1, DMA, None)
                project(0, DMA, (2, 2))
                pe.wait_ge(cleared, 2)
                project(1, 2 * DMA, (4, 4))
                project(0, 2 * DMA, (6, 6))
                scores(0, 0, (4, 2 * DMA), None)
                scores(0, 1, None, None)
                scores(0, 2, None, 0)
                with pe.Fori(0, B) as b:
                    with pe.Fori(0, PAIRS // 2) as jp:
                        for r in range(2):
                            un = jp * 2 + r
                            u = unit(b, jp, r)
                            his = 2 * M_FIRST + b * 2 * PROJ + un * 4
                            outs = 2 * M_FIRST + b * M_OUTS + un * 4

                            def uses(i):
                                return [T_FIRST + b * T_USES[h] + un * QT + i for h in range(2)]

                            for i in range(QT):
                                transposes(i, u * QT + i, uses(i))
                                if i == 0:
                                    scores(r, QT - 1, None, u * QT + 1)
                                else:
                                    scores(1 - r, i - 1, (outs, (b * (PAIRS // 2) + jp + 1 + r) * 2 * DMA) if i == 1 else None,
                                           u * QT + i + 1)
                                if i == 0:
                                    pe.wait_ge(xnt_loaded, (b + 1 + ((un + 2) >> 3)) * DMA)
                                    project(1, (u + 3) * DMA, (his, outs))
                                if i == 2:
                                    project(0, (u + 3) * DMA, (his + 2, outs + 2))
                                if i:
                                    weigh(r, i - 1, u, uses(i - 1), (b * (PAIRS // 2) + jp + 1) * DMA)
                            weigh(r, QT - 1, u, uses(QT - 1), None)
                    v_uses = [T_FIRST + b * T_USES[h] + QT * PAIRS for h in range(2)]
                    project_v(v_uses)
                    project_out(b, v_uses[1] + T_FIRST, 2 * M_FIRST + b * M_OUTS + 2 * PROJ)

            @block.scalar
            def _(act):
                def split_keys(r, ready):
                    act.wait_ge(m_ready, ready)
                    for h in range(2):
                        act.activation(ks[r][h][HI][head_half(h), :], m_ps[head_half(h), :], ACT.Copy).then_inc(m_hi, 1)

                def split_queries(r, ready):
                    act.wait_ge(m_ready, ready)
                    for h in range(2):
                        act.activation(qs[r][h][head_half(h), :], m_ps[head_half(h), :], ACT.Copy).then_inc(m_hi, 1)

                def exponentials(i, step_no):
                    act.wait_ge(bias_done, step_no + 1)
                    for h in range(2):
                        part = probs[i][h][:, 0:(i + 1) * P]
                        act.activation(part, part, ACT.Exp, bias=bias[i][:, h:h + 1], scale=SCALE,
                                       accum_out=total[i][:, h:h + 1]).then_inc(exp_done, 1)

                def take_v(copied, ready):
                    for r in range(2) if copied is not None else ():
                        act.wait_ge(vp_loaded[r], copied)
                    for tok in range(QT):
                        act.wait_ge(t_ready[0], ready + tok + 1)
                        act.activation(v[:, tok, 0:T], t_ps[0][:, :], ACT.Copy).then_inc(t_out[0], 1)

                take_v(None, 0)
                split_keys(0, 1)
                split_queries(0, 2)
                split_keys(1, 3)
                split_queries(1, 4)
                for i in range(2):
                    exponentials(i, i)
                with act.Fori(0, B) as b:
                    with act.Fori(0, PAIRS // 2) as jp:
                        for r in range(2):
                            u = unit(b, jp, r)
                            for i in range(QT):
                                act.wait_ge(t_ready[0], T_FIRST + b * T_USES[0] + (jp * 2 + r) * QT + i + 1)
                                act.activation(probs_t[0][i % 2][:, 0:i + 1, :], t_ps[0][:, 0:(i + 1) * P].rearrange(
                                    "p (j n) -> p j n", n=P), ACT.Copy).then_inc(t_out[0], 1)
                                ready = M_FIRST + b * M_USES + (jp * 2 + r) * 2
                                if i == 1:
                                    split_keys(r, ready + 1)
                                if i == 3:
                                    split_queries(r, ready + 2)
                                exponentials((i + 2) % QT, u * QT + i + 2)
                            act.wait_ge(o_ready, START + u + 1)
                            act.activation(out_t[HI][:, bass.ds(jp * 2 + r, 1), :].rearrange("p a t -> p (a t)"),
                                           o_ps[:, :], ACT.Copy).then_inc(o_hi, 1)
                    take_v((b + 1) * (PAIRS // 2) * DMA, T_FIRST + b * T_USES[0] + QT * PAIRS)

            @block.vector
            def _(dve):
                def split_keys(r, his):
                    for h in range(2):
                        dve.wait_ge(m_hi, his + h + 1)
                        dve.tensor_tensor(ks[r][h][LO][head_half(h), :], m_ps[head_half(h), :],
                                          ks[r][h][HI][head_half(h), :].bitcast(F32), ALU.subtract).then_inc(m_out, 1)

                def split_queries(r, his):
                    for h in range(2):
                        dve.wait_ge(m_hi, his + h + 1)
                        dve.tensor_tensor(qs[r][h][head_half(1 - h), :], m_ps[head_half(h), :],
                                          qs[r][h][head_half(h), :].bitcast(F32), ALU.subtract).then_inc(m_out, 1)

                def maxima(i, step_no):
                    cols = (i + 1) * P
                    for h in range(2):
                        wait_apart(dve, s_ready, step_no * 2 + h + 1, begun)
                        dve.tensor_tensor_reduce(out=probs[i][h][:, 0:cols], in0=s_ps[i % 2][h][:, 0:cols],
                                                 in1=mask[:, T - cols:T], scale=1.0, scalar=-3e38, op0=ALU.add,
                                                 op1=ALU.max, accum_out=top[i][:, h:h + 1]).then_inc(s_out, 1)
                    dve.wait_ge(s_out, step_no * 2 + 2)
                    dve.tensor_scalar(bias[i][:, :], top[i][:, :], -SCALE, None, ALU.mult).then_inc(bias_done, 1)

                def invert(i, step_no):
                    dve.wait_ge(exp_done, step_no * 2 + 2)
                    dve.reciprocal(inverse[i][:, :], total[i][:, :]).then_inc(inverse_done, 1)

                def take_v(copied, ready):
                    for r in range(2) if copied is not None else ():
                        dve.wait_ge(vp_loaded[r], copied)
                    for tok in range(QT):
                        dve.wait_ge(t_ready[1], ready + tok + 1)
                        dve.tensor_copy(v[:, tok, T:2 * T], t_ps[1][:, :]).then_inc(t_out[1], 1)

                def look_up(batch):
                    for n in range(2):
                        dve.tensor_copy(place[:, n, :], keep["slot"][n][:, bass.ds(batch * QT, QT)]).then_inc(placed, 1)

                look_up(0)
                take_v(None, 0)
                split_keys(0, 0)
                split_queries(0, 2)
                split_keys(1, 4)
                split_queries(1, 6)
                for i in range(3):
                    maxima(i, i)
                invert(0, 0)
                with dve.Fori(0, B) as b:
                    with dve.Fori(0, PAIRS // 2) as jp:
                        for r in range(2):
                            u = unit(b, jp, r)
                            for i in range(QT):
                                invert((i + 1) % QT, u * QT + i + 1)
                                dve.wait_ge(t_ready[1], T_FIRST + b * T_USES[1] + (jp * 2 + r) * QT + i + 1)
                                dve.tensor_copy(probs_t[1][i % 2][:, 0:i + 1, :], t_ps[1][:, 0:(i + 1) * P].rearrange(
                                    "p (j n) -> p j n", n=P)).then_inc(t_out[1], 1)
                                if i == 1:
                                    split_keys(r, 2 * M_FIRST + u * 4)
                                if i == 3:
                                    split_queries(r, 2 * M_FIRST + u * 4 + 2)
                                maxima((i + 3) % QT, u * QT + i + 3)
                            dve.wait_ge(o_hi, u + 1)
                            dve.tensor_tensor(out_t[LO][:, bass.ds(jp * 2 + r, 1), :].rearrange("p a t -> p (a t)"),
                                              o_ps[:, :], out_t[HI][:, bass.ds(jp * 2 + r, 1), :].rearrange(
                                                  "p a t -> p (a t)").bitcast(F32), ALU.subtract).then_inc(o_out, 1)
                    dve.wait_ge(routed_added, START + b)
                    for n in range(2):
                        dve.tensor_copy(share[:, n, :], keep["weight"][n][:, bass.ds(b * QT, QT)]).then_inc(shared_out, 1)
                    dve.wait_ge(gathered, (b + 1) * GATHERS * DMA)
                    look_up((b + 1) & (B - 1))
                    take_v((b + 1) * (PAIRS // 2) * DMA, T_FIRST + b * T_USES[1] + QT * PAIRS)
                    dve.wait_ge(routed_added, START + b + 1)
                    dve.wait_ge(stored, START + b * DMA)
                    for q in range(QT):
                        if q % 2 == 0:
                            dve.wait_ge(t_ready[1], T_FIRST + (b + 1) * T_USES[1] - QT // 2 + q // 2 + 1)
                        else:
                            dve.wait_ge(m_ready, M_FIRST + (b + 1) * M_USES - QT // 2 + q // 2 + 1)
                        dve.tensor_tensor(summed[:, q, :], (t_ps[1] if q % 2 == 0 else m_ps)[:, 0:D], base[:, q, :],
                                          ALU.add).then_inc(t_out[1] if q % 2 == 0 else m_out, 1)

            @block.gpsimd
            def _(pool):
                for counter in (o_out, o_ready, stored, routed_added):
                    pool.sem_inc(counter, START)

                def gather(nth):
                    wait_apart(pool, placed, (nth + 1) * 2, begun)
                    for q in range(QT):
                        for n in range(2):
                            pool.indirect_dma_start(
                                out=routed[:, n, q, :], out_offset=None, in_=dram["routed"][:, :],
                                in_offset=bass.IndirectOffsetOnAxis(ap=place[:, n, q:q + 1], axis=0),
                                bounds_check=SLOTS - 1, oob_is_err=False).then_inc(gathered, DMA)

                gather(0)
                def normalise(i, step_no):
                    wait_apart(pool, inverse_done, step_no + 1, begun)
                    for h in range(2):
                        part = probs[i][h][:, 0:(i + 1) * P]
                        pool.tensor_scalar(part, part, inverse[i][:, h:h + 1], 1.0, ALU.mult, ALU.mult).then_inc(norm_done, 1)

                for r in range(2):
                    for h in range(2):
                        last = pool.memset(ks[r][h][LO][head_half(1 - h), :].bitcast(F32), 0.0)
                    last.then_inc(cleared, 1)
                normalise(0, 0)
                with pool.Fori(0, B) as b:
                    with pool.Fori(0, PAIRS // 2) as jp:
                        for r in range(2):
                            for i in range(QT):
                                normalise((i + 1) % QT, unit(b, jp, r) * QT + i + 1)
                    wait_apart(pool, shared_out, (b + 1) * 2, begun)
                    wait_apart(pool, base_loaded, (b + 1) * DMA, begun)
                    wait_apart(pool, gathered, (b + 1) * GATHERS * DMA, begun)
                    for n in range(2):
                        for q in range(QT):
                            last = pool.tensor_scalar(routed[:, n, q, :], routed[:, n, q, :], share[:, n, q:q + 1], 1.0,
                                                      ALU.mult, ALU.mult)
                        last.then_inc(weighted, 1)
                    wait_apart(pool, weighted, (b + 1) * 2, begun)
                    pool.tensor_tensor(base[:, :, :], base[:, :, :], routed[:, 0, :, :], ALU.add).then_inc(first_added, 1)
                    wait_apart(pool, first_added, b + 1, begun)
                    pool.tensor_tensor(base[:, :, :], base[:, :, :], routed[:, 1, :, :], ALU.add).then_inc(routed_added, 1)
                    wait_apart(pool, routed_added, START + b + 1, begun)
                    gather(b + 1)
                pool.wait_ge(gathered, (B + 1) * GATHERS * DMA)


def program(nc, ins, out):
    with ExitStack() as ctx:
        def sb(name, shape, dt=F32):
            return ctx.enter_context(nc.sbuf_tensor(name, shape, dt))

        dram = {
            "xn": nc.dram_tensor("xn_rows", [B, P, QT, D], F32).ap(),
            "xnt": nc.dram_tensor("xnt_split", [B, P, HALVES * KD * T], F32).ap(),
            "base": nc.dram_tensor("base_rows", [B, P, QT, D], F32).ap(),
            "experts": nc.dram_tensor("expert_rows", [E, P, WROW], F32).ap(),
            "queued": nc.dram_tensor("queued_rows", [SLOTS, D], F32).ap(),
            "routed": nc.dram_tensor("routed_rows", [SLOTS, D], F32).ap(),
        }
        keep = {
            "begun": ctx.enter_context(nc.semaphore("begun")),
            "ident": sb("ident", [P, P]),
            "mask": sb("mask", [P, T]),
            "wqk": sb("wqk_all", [P, PAIRS, 2, HALVES, KD, P], F32R),
            "wv": sb("wv_all", [P, HALVES, KD, H * DK], F32R),
            "wo": sb("wo_all", [P, HALVES, PAIRS, D], F32R),
            "shared": sb("shared_all", [P, HALVES, WROW], F32R),
            "weight": [sb(f"weight{n}", [P, TT]) for n in range(2)],
            "slot": [sb(f"slot{n}", [P, TT], I32) for n in range(2)],
            "weight_row": sb("weight_row", [P, SLOT_TILES], I32),
        }
        stage_a(nc, ins, dram, keep)
        stage_b(nc, ins, dram, keep)
        stage_c(nc, dram, keep)
        stage_d(nc, dram, keep, out)


NAMES = ["L0_attn_x", "L0_attn_Wq", "L0_attn_Wk", "L0_attn_Wv", "L0_attn_Wo", "L0_attn_bo", "L0_ffn_gate_w",
         "L0_ffn_gate_b", "L0_ffn_shared_wg", "L0_ffn_shared_wu", "L0_ffn_shared_wd", "L0_ffn_experts_wg",
         "L0_ffn_experts_wu", "L0_ffn_experts_wd"]


def kernel(**inputs):
    import concourse.bacc as bacc
    from concourse.bass_utils import run_bass_kernel_spmd

    nc = bacc.Bacc("TRN2", target_bir_lowering=False, num_devices=1)
    arrays, ins = {}, {}
    for name in NAMES:
        a = np.ascontiguousarray(inputs[name])
        arrays[f"in_{name}"] = a
        ins[name] = nc.dram_tensor(f"in_{name}", a.shape, mybir.dt.from_np(a.dtype), kind="ExternalInput").ap()
    out = nc.dram_tensor("out_0", (B, T, D), F32, kind="ExternalOutput").ap()
    program(nc, ins, out)
    result = run_bass_kernel_spmd(nc, [arrays], core_ids=[0])
    return result.results[0]["out_0"]
```

```python
from contextlib import ExitStack

import numpy as np

import concourse.bass as bass
from concourse import mybir

F32 = mybir.dt.float32
F32R = mybir.dt.float32r
BF16 = mybir.dt.bfloat16
I32 = mybir.dt.int32
ALU = mybir.AluOpType
ACT = mybir.ActivationFunctionType
AX = mybir.AxisListType

P = 128
B, T, D = 16, 512, 256
H, DK = 16, 64
E, FF = 16, 128
KD = D // P
QT = T // P
NTOK = B * T
TT = NTOK // P
PAIRS = H // 2
HALVES = 2
HI, LO = 0, 1
SCALE = DK ** -0.5
EPS = 1e-5
MASKED = -1e30
SLOT_TILE = 256
SUB = SLOT_TILE // P
SLOT_TILES = 2 * NTOK // SLOT_TILE + E
SLOTS = SLOT_TILES * SLOT_TILE
WPART = KD * FF
WROW = 3 * WPART
PASSES = ((HI, HI), (LO, HI), (HI, LO))
START = 1
DMA = 16


def gate_cols(k):
    return slice(k * FF, (k + 1) * FF)


def up_cols(k):
    return slice(WPART + k * FF, WPART + (k + 1) * FF)


DOWN_COLS = slice(2 * WPART, 3 * WPART)


def wait_apart(eng, semaphore, value, begun):
    value = eng.to_reg(value)
    eng.wait_ge(begun, 1)
    eng.wait_ge(semaphore, value)


def stage_a(nc, ins, dram, keep):
    begun = keep["begun"]
    with ExitStack() as ctx:
        def sb(name, shape, dt=F32):
            return ctx.enter_context(nc.sbuf_tensor("a_" + name, shape, dt))

        def pb(name, shape, dt=F32):
            return ctx.enter_context(nc.psum_tensor("a_" + name, shape, dt))

        def sem(name):
            return ctx.enter_context(nc.semaphore("a_" + name))

        ident = keep["ident"]
        x_in = [sb(f"x_in{r}", [P, QT, D]) for r in range(2)]
        xn = [sb(f"xn{r}", [P, QT, D]) for r in range(2)]
        xnt = [sb(f"xnt{r}", [P, HALVES, KD, T], F32R) for r in range(2)]
        stats = [sb(f"stats{r}", [P, QT, 6]) for r in range(2)]
        mean_var = [sb(f"mean_var{r}", [P, QT, 2]) for r in range(2)]
        std = [sb(f"std{r}", [P, QT]) for r in range(2)]
        rstd = [sb(f"rstd{r}", [P, QT]) for r in range(2)]
        logits_t = [sb(f"logits_t{r}", [E, T]) for r in range(2)]
        gate_b = sb("gate_b", [E, 1])
        eps = sb("eps", [P, 1])
        gate_w = sb("gate_w", [P, KD, P])
        gate_w_split = sb("gate_w_split", [P, HALVES, KD, P], F32R)
        staged = sb("staged", [P, 8192])
        zeros = sb("zeros", [P, 2048])
        begun_at = sb("begun_at", [P, 1])
        probs = sb("probs", [P, TT, E])
        chosen = [sb(f"chosen{n}", [P, TT, E]) for n in range(2)]
        work = sb("work", [P, TT, E])
        spots = sb("spots", [P, TT, E])
        both = sb("both", [P, TT, E], BF16)
        best = [sb(f"best{n}", [P, TT]) for n in range(2)]
        mark = sb("mark", [P, TT])
        total = sb("total", [P, TT])
        rank_of_e = sb("rank_of_e", [P, E])
        rank_i = sb("rank_i", [P, E], I32)
        before = sb("before", [P, P], BF16)
        ones_b = sb("ones_b", [P, P], BF16)
        ones = sb("ones", [P, TT])
        tile_sum = sb("tile_sum", [P, TT, E])
        running = sb("running", [P, TT, E])
        padded_i = sb("padded_i", [P, E], I32)
        padded = sb("padded", [P, E])
        ends = sb("ends", [P, E])
        offset = sb("offset", [P, E])
        tile_i = sb("tile_i", [P, SLOT_TILES], I32)
        tile_start = sb("tile_start", [P, SLOT_TILES])
        row_i = sb("row_i", [P, 1], I32)
        row = sb("row", [P, 1])
        past = sb("past", [P, SLOT_TILES, E])
        expert = sb("expert", [P, SLOT_TILES])
        shared_in = sb("shared_in", [P, WROW])

        xt_ps = [pb(f"xt_ps{r}", [P, KD, T]) for r in range(2)]
        lg_ps = [pb(f"lg_ps{r}", [P, T]) for r in range(2)]
        lt_ps = [pb(f"lt_ps{r}", [P, QT, P]) for r in range(2)]

        x_loaded = [sem(f"x_loaded{r}") for r in range(2)]
        mean_done = sem("mean_done")
        std_done = sem("std_done")
        rstd_done = sem("rstd_done")
        xn_done = sem("xn_done")
        xt_ready = sem("xt_ready")
        hi_done = sem("hi_done")
        lo_done = sem("lo_done")
        lg_ready = sem("lg_ready")
        lg_out = sem("lg_out")
        lt_ready = sem("lt_ready")
        lt_out = sem("lt_out")
        xn_stored = [sem(f"xn_stored{r}") for r in range(2)]
        xnt_stored = [sem(f"xnt_stored{r}") for r in range(2)]
        const_loaded = sem("const_loaded")
        gw_hi = sem("gw_hi")
        gw_split = sem("gw_split")
        made = sem("made")
        stage_loaded = sem("stage_loaded")
        stage_hi = sem("stage_hi")
        stage_used = sem("stage_used")
        zeroed = sem("zeroed")
        zero_stored = sem("zero_stored")
        shared_hi = sem("shared_hi")
        shared_split = sem("shared_split")
        sig_done = sem("sig_done")
        step = sem("step")
        both_ready = sem("both_ready")
        rank_ready = sem("rank_ready")

        ZERO_PARTS = SLOTS * D // (P * 2048)
        x_src = ins["L0_attn_x"].rearrange("b (q p) d -> b p q d", p=P)
        wq_src = ins["L0_attn_Wq"].rearrange("h (k p) d -> k p h d", p=P)
        wk_src = ins["L0_attn_Wk"].rearrange("h (k p) d -> k p h d", p=P)
        wv_src = ins["L0_attn_Wv"].rearrange("h (k p) d -> k p h d", p=P)
        wo_src = ins["L0_attn_Wo"].rearrange("(j p) n -> p j n", p=P)
        wqk, wv, wo, shared = keep["wqk"], keep["wv"], keep["wo"], keep["shared"]

        def stage_view(n):
            return staged[:, n * H * DK:(n + 1) * H * DK].rearrange("p (h d) -> p h d", h=H)

        loads = []
        for src, which in ((wq_src, 0), (wk_src, 1)):
            for k in range(KD):
                loads.append((src[k], stage_view(len(loads)),
                              [wqk[:, :, which, hl, k, :].rearrange("p j (h d) -> p j h d", h=2) for hl in range(2)]))
        for k in range(KD):
            loads.append((wv_src[k], stage_view(len(loads)),
                          [wv[:, hl, k, :].rearrange("p (h d) -> p h d", h=H) for hl in range(2)]))
        loads.append((wo_src, staged[:, 6 * H * DK:6 * H * DK + PAIRS * D].rearrange("p (j n) -> p j n", j=PAIRS),
                      [wo[:, hl, :, :] for hl in range(2)]))

        with nc.Block() as block:
            @block.sync
            def _(sp):
                sp.dma_start(gate_b[:, :], ins["L0_ffn_gate_b"].rearrange("(n a) -> n a", a=1)).then_inc(const_loaded, DMA)
                sp.wait_ge(made, 1)
                sp.dma_start(gate_w[:, :, 0:E], ins["L0_ffn_gate_w"].rearrange("(k p) e -> p k e", p=P)
                             ).then_inc(const_loaded, DMA)

                def load_x(b, r):
                    sp.dma_start(x_in[r][:, :, :], x_src[bass.ds(b, 1)].rearrange("b p q d -> (b p) q d")
                                 ).then_inc(x_loaded[r], DMA)

                def store(b, r, more):
                    wait_apart(sp, xn_done, START + b + 1, begun)
                    if more:
                        load_x(b + 2, r)
                    sp.dma_start(dram["xn"][bass.ds(b, 1)].rearrange("b p q d -> (b p) q d"), xn[r][:, :, :]
                                 ).then_inc(xn_stored[r], DMA)
                    wait_apart(sp, lo_done, START + b * KD + KD, begun)
                    sp.dma_start(dram["xnt"][bass.ds(b, 1)].rearrange("b p n -> (b p) n"),
                                 xnt[r][:, :, :, :].rearrange("p a k t -> p (a k t)").bitcast(F32)
                                 ).then_inc(xnt_stored[r], DMA)

                load_x(0, 0)
                load_x(1, 1)
                for src, view, _ in loads:
                    sp.dma_start(view, src).then_inc(stage_loaded, DMA)
                for n, name in enumerate(("wg", "wu", "wd")):
                    src = ins["L0_ffn_shared_" + name]
                    to = shared_in[:, n * WPART:(n + 1) * WPART]
                    if n < 2:
                        to, src = to.rearrange("p (k f) -> p k f", k=KD), src.rearrange("(k p) f -> p k f", p=P)
                    sp.dma_start(to, src).then_inc(stage_loaded, DMA)
                with sp.Fori(0, B // 2 - 1) as g:
                    for r in range(2):
                        store(g * 2 + r, r, True)
                for r in range(2):
                    store(B - 2 + r, r, False)
                for r in range(2):
                    sp.wait_ge(xn_stored[r], START + B // 2 * DMA)
                    sp.wait_ge(xnt_stored[r], START + B // 2 * DMA)

            @block.gpsimd
            def _(pool):
                for counter in (xn_done, xt_ready, lg_out, lt_out, *xnt_stored, *xn_stored, lo_done):
                    pool.sem_inc(counter, START)
                pool.memset(begun_at[:, :], 0.0).then_inc(begun, 1)
                pool.memset(gate_w[:, :, :], 0.0).then_inc(made, 1)
                pool.memset(zeros[:, :], 0.0).then_inc(zeroed, 1)
                pool.memset(eps[:, :], EPS).then_inc(made, 1)
                pool.memset(ones[:, :], 1.0).then_inc(made, 1)
                pool.memset(ones_b[:, :], 1.0).then_inc(made, 1)
                pool.memset(before[:, :], 1.0).then_inc(made, 1)
                pool.memset(ident[:, :], 0.0).then_inc(made, 1)
                pool.memset(keep["mask"][:, :], 0.0).then_inc(made, 1)
                pool.wait_ge(made, 7)
                pool.affine_select(out=before[:, :], in_=before[:, :], compare_op=ALU.is_gt, fill=0.0, base=0,
                                   pattern=[[1, P]], channel_multiplier=-1).then_inc(made, 1)
                pool.affine_select(out=ident[:, :], in_=ident[:, :], compare_op=ALU.not_equal, fill=1.0, base=0,
                                   pattern=[[-1, P]], channel_multiplier=1).then_inc(made, 1)
                pool.affine_select(out=keep["mask"][:, T - P:T], in_=keep["mask"][:, T - P:T], compare_op=ALU.is_ge,
                                   fill=MASKED, base=0, pattern=[[-1, P]], channel_multiplier=1).then_inc(made, 1)
                pool.iota(rank_i[:, :], pattern=[[-1, E]], base=E, channel_multiplier=0).then_inc(made, 1)
                pool.iota(tile_i[:, :], pattern=[[SLOT_TILE, SLOT_TILES]], base=0, channel_multiplier=0).then_inc(made, 1)
                pool.iota(row_i[:, :], pattern=[[0, 1]], base=0, channel_multiplier=1).then_inc(made, 1)
                for n, (_, view, parts) in enumerate(loads):
                    pool.wait_ge(stage_hi, n + 1)
                    src = view if len(parts[HI].shape) == 3 else view.rearrange("p (j h) d -> p j h d", h=2)
                    pool.tensor_tensor(parts[LO], src, parts[HI].bitcast(F32), ALU.subtract).then_inc(stage_used, 1)
                pool.wait_ge(shared_hi, 1)
                pool.tensor_tensor(shared[:, LO, :], shared_in[:, :], shared[:, HI, :].bitcast(F32), ALU.subtract
                                   ).then_inc(shared_split, 1)

            @block.scalar
            def _(act):
                act.wait_ge(zeroed, 1)

                def clear(n):
                    rows = SLOTS // ZERO_PARTS
                    act.dma_start(dram["queued"][bass.ds(n * rows, rows), :].rearrange("(p q) d -> p (q d)", p=P),
                                  zeros[:, :]).then_inc(zero_stored, DMA)

                act.wait_ge(made, MADE)
                act.wait_ge(const_loaded, 2 * DMA)
                act.activation(gate_w_split[:, HI, :, :], gate_w[:, :, :], ACT.Copy).then_inc(gw_hi, 1)

                def deviation(b, r):
                    act.wait_ge(mean_done, b + 1)
                    act.activation(std[r][:, :], mean_var[r][:, :, 1], ACT.Sqrt, bias=eps[:, 0:1]).then_inc(std_done, 1)

                def split_xt(b, g, r):
                    act.wait_ge(xnt_stored[r], START + g * DMA)
                    for k in range(KD):
                        act.wait_ge(xt_ready, START + b * KD + k + 1)
                        act.activation(xnt[r][:, HI, k, :], xt_ps[r][:, k, :], ACT.Copy).then_inc(hi_done, 1)

                def take_logits(b, r):
                    act.wait_ge(lg_ready, b + 1)
                    act.activation(logits_t[r][:, :], lg_ps[r][0:E, :], ACT.Identity, bias=gate_b[:, 0:1]
                                   ).then_inc(lg_out, 1)

                for r in range(2):
                    deviation(r, r)
                with act.Fori(0, B // 2 - 1) as g:
                    for r in range(2):
                        split_xt(g * 2 + r, g, r)
                        if r == 0:
                            clear(g)
                        take_logits(g * 2 + r, r)
                        deviation(g * 2 + r + 2, r)
                for r in range(2):
                    split_xt(B - 2 + r, B // 2 - 1, r)
                    take_logits(B - 2 + r, r)
                act.wait_ge(lt_out, START + B)
                act.activation(probs[:, :, :], probs[:, :, :], ACT.Sigmoid).then_inc(sig_done, 1)
                for n in range(B // 2 - 1, ZERO_PARTS):
                    clear(n)
                act.wait_ge(stage_loaded, (len(loads) + 3) * DMA)
                for _, view, parts in loads:
                    src = view if len(parts[HI].shape) == 3 else view.rearrange("p (j h) d -> p j h d", h=2)
                    act.activation(parts[HI], src, ACT.Copy).then_inc(stage_hi, 1)
                act.activation(shared[:, HI, :], shared_in[:, :], ACT.Copy).then_inc(shared_hi, 1)
                act.wait_ge(zero_stored, ZERO_PARTS * DMA)

            @block.vector
            def _(dve):
                dve.wait_ge(gw_hi, 1)
                dve.tensor_tensor(gate_w_split[:, LO, :, :], gate_w[:, :, :], gate_w_split[:, HI, :, :].bitcast(F32),
                                  ALU.subtract).then_inc(gw_split, 1)

                def moments(b, loads, r):
                    dve.wait_ge(x_loaded[r], loads * DMA)
                    for q in range(QT):
                        last = dve.bn_stats(stats[r][:, q, :], x_in[r][:, q, :])
                    last.then_inc(step, 1)
                    wait_apart(dve, step, b + 1, begun)
                    for q in range(QT):
                        last = dve.bn_aggr(mean_var[r][:, q, :], stats[r][:, q, :])
                    last.then_inc(mean_done, 1)

                def normalise(b, loads, r, free):
                    dve.wait_ge(std_done, b + 1)
                    dve.reciprocal(rstd[r][:, :], std[r][:, :]).then_inc(rstd_done, 1)
                    dve.wait_ge(rstd_done, b + 1)
                    dve.wait_ge(xn_stored[r], START + (loads - 1) * DMA)
                    if free is not None:
                        dve.wait_ge(xt_ready, free)
                    for q in range(QT):
                        last = dve.tensor_scalar(xn[r][:, q, :], x_in[r][:, q, :], mean_var[r][:, q, 0:1],
                                                 rstd[r][:, q:q + 1], ALU.subtract, ALU.mult)
                    last.then_inc(xn_done, 1)

                def split_xt(b, r):
                    for k in range(KD):
                        dve.wait_ge(hi_done, b * KD + k + 1)
                        dve.tensor_tensor(xnt[r][:, LO, k, :], xt_ps[r][:, k, :], xnt[r][:, HI, k, :].bitcast(F32),
                                          ALU.subtract).then_inc(lo_done, 1)

                def take_logits(b, r):
                    dve.wait_ge(lt_ready, b + 1)
                    dve.tensor_copy(probs[:, bass.ds(b * QT, QT), :], lt_ps[r][:, :, 0:E]).then_inc(lt_out, 1)

                moments(0, 1, 0)
                normalise(0, 1, 0, None)
                moments(1, 1, 1)
                with dve.Fori(0, B // 2 - 1) as g:
                    for r in range(2):
                        b = g * 2 + r
                        split_xt(b, r)
                        normalise(b + 1, g + 1 + r, 1 - r, START + b * KD)
                        moments(b + 2, g + 2, r)
                        take_logits(b, r)
                split_xt(B - 2, 0)
                normalise(B - 1, B // 2, 1, START + (B - 2) * KD)
                take_logits(B - 2, 0)
                split_xt(B - 1, 1)
                take_logits(B - 1, 1)

                count = [B]

                def then(instruction):
                    instruction.then_inc(step, 1)
                    count[0] += 1
                    dve.wait_ge(step, count[0])

                dve.wait_ge(made, MADE)
                then(dve.tensor_copy(rank_of_e[:, :], rank_i[:, :]))
                then(dve.tensor_copy(tile_start[:, :], tile_i[:, :]))
                then(dve.tensor_copy(row[:, :], row_i[:, :]))
                dve.wait_ge(sig_done, 1)
                by_e = lambda v: v[:, :, None].broadcast_to([P, TT, E])
                ranks = rank_of_e[:, None, :].broadcast_to([P, TT, E])
                for n in range(2):
                    then(dve.tensor_reduce(best[n][:, :], probs[:, :, :], AX.X, ALU.max))
                    then(dve.tensor_tensor(work[:, :, :], probs[:, :, :], by_e(best[n]), ALU.is_equal))
                    then(dve.tensor_tensor(work[:, :, :], work[:, :, :], ranks, ALU.mult))
                    then(dve.tensor_reduce(mark[:, :], work[:, :, :], AX.X, ALU.max))
                    then(dve.tensor_tensor(chosen[n][:, :, :], work[:, :, :], by_e(mark), ALU.is_equal))
                    if n == 0:
                        then(dve.scalar_tensor_tensor(probs[:, :, :].rearrange("p t e -> p (t e)"),
                                                      chosen[0][:, :, :].rearrange("p t e -> p (t e)"), -4.0,
                                                      probs[:, :, :].rearrange("p t e -> p (t e)"), ALU.mult, ALU.add))
                then(dve.tensor_tensor(total[:, :], best[0][:, :], best[1][:, :], ALU.add))
                then(dve.reciprocal(total[:, :], total[:, :]))
                for n in range(2):
                    then(dve.tensor_tensor(keep["weight"][n][:, :], best[n][:, :], total[:, :], ALU.mult))
                dve.tensor_tensor(both[:, :, :], chosen[0][:, :, :], chosen[1][:, :, :], ALU.add).then_inc(both_ready, 1)
                dve.wait_ge(rank_ready, 1)
                half = TT // 2
                for n in range(2):
                    then(dve.tensor_copy(tile_sum[:, n * half:(n + 1) * half, :],
                                         xt_ps[1][:, n, :].rearrange("p (t e) -> p t e", e=E)))
                for e in range(E):
                    then(dve.tensor_tensor_scan(running[:, :, e], ones[:, :], tile_sum[:, :, e], 0.0, ALU.mult, ALU.add))
                then(dve.tensor_scalar(padded[:, :], running[:, TT - 1, :], float(SLOT_TILE - 1), None, ALU.add))
                then(dve.tensor_copy(padded_i[:, :], padded[:, :]))
                shift = SLOT_TILE.bit_length() - 1
                then(dve.tensor_scalar(padded_i[:, :], padded_i[:, :], shift, shift, ALU.logical_shift_right,
                                       ALU.logical_shift_left))
                then(dve.tensor_copy(padded[:, :], padded_i[:, :]))
                then(dve.tensor_tensor_scan(ends[:, :], ones[:, 0:E], padded[:, :], 0.0, ALU.mult, ALU.add))
                then(dve.tensor_tensor(offset[:, :], ends[:, :], padded[:, :], ALU.subtract))
                then(dve.tensor_tensor(spots[:, :, :], running[:, :, :], tile_sum[:, :, :], ALU.subtract))
                then(dve.tensor_tensor(spots[:, :, :], spots[:, :, :], offset[:, None, :].broadcast_to([P, TT, E]), ALU.add))
                for n in range(2):
                    part = spots[:, n * half:(n + 1) * half, :]
                    then(dve.tensor_tensor(part, xt_ps[0][:, n, :].rearrange("p (t e) -> p t e", e=E), part, ALU.add))
                for n in range(2):
                    then(dve.tensor_tensor(work[:, :, :], chosen[n][:, :, :], spots[:, :, :], ALU.mult))
                    then(dve.tensor_reduce(mark[:, :], work[:, :, :], AX.X, ALU.add))
                    then(dve.tensor_copy(keep["slot"][n][:, :], mark[:, :]))
                then(dve.tensor_tensor(past[:, :, :], tile_start[:, :, None].broadcast_to([P, SLOT_TILES, E]),
                                       ends[:, None, :].broadcast_to([P, SLOT_TILES, E]), ALU.is_ge))
                then(dve.tensor_reduce(expert[:, :], past[:, :, :], AX.X, ALU.add))
                then(dve.tensor_scalar(expert[:, :], expert[:, :], float(E - 1), float(P), ALU.min, ALU.mult))
                then(dve.tensor_scalar(expert[:, :], expert[:, :], row[:, 0:1], None, ALU.add))
                then(dve.tensor_copy(keep["weight_row"][:, :], expert[:, :]))

            @block.tensor
            def _(pe):
                pe.wait_ge(made, MADE)
                pe.wait_ge(gw_split, 1)
                with pe.Fori(0, B // 2) as g:
                    for r in range(2):
                        b = g * 2 + r
                        pe.wait_ge(xn_done, START + b + 1)
                        pe.wait_ge(lo_done, START + g * 2 * KD)
                        for k in range(KD):
                            for q in range(QT):
                                last = pe.transpose(xt_ps[r][:, k, q * P:(q + 1) * P], xn[r][:, q, k * P:(k + 1) * P],
                                                    ident[:, :])
                            last.then_inc(xt_ready, 1)
                        pe.wait_ge(lo_done, START + (b + 1) * KD)
                        pe.wait_ge(lg_out, START + g * 2)
                        n = 0
                        for k in range(KD):
                            for wa, xb in PASSES:
                                n += 1
                                last = pe.matmul(lg_ps[r][:, :], gate_w_split[:, wa, k, :], xnt[r][:, xb, k, :],
                                                 start=(n == 1), stop=(n == KD * len(PASSES)))
                        last.then_inc(lg_ready, 1)
                        wait_apart(pe, lt_out, START + g * 2, begun)
                        wait_apart(pe, lg_out, START + b + 1, begun)
                        for q in range(QT):
                            last = pe.transpose(lt_ps[r][:, q, 0:E], logits_t[r][:, q * P:(q + 1) * P], ident[0:E, 0:E])
                        last.then_inc(lt_ready, 1)
                pe.wait_ge(both_ready, 1)
                flat = both[:, :, :].rearrange("p t e -> p (t e)")
                for n in range(2):
                    pe.matmul(xt_ps[0][:, n, :], before[:, :], flat[:, n * T:(n + 1) * T], start=True, stop=True)
                    last = pe.matmul(xt_ps[1][:, n, :], ones_b[:, :], flat[:, n * T:(n + 1) * T], start=True, stop=True)
                last.then_inc(rank_ready, 1)


MADE = 13


def stage_b(nc, ins, dram, keep):
    begun = keep["begun"]
    with ExitStack() as ctx:
        def sb(name, shape, dt=F32):
            return ctx.enter_context(nc.sbuf_tensor("b_" + name, shape, dt))

        def pb(name, shape, dt=F32):
            return ctx.enter_context(nc.psum_tensor("b_" + name, shape, dt))

        def sem(name):
            return ctx.enter_context(nc.semaphore("b_" + name))

        DEEP = 4
        ident, w = keep["ident"], keep["shared"]
        rows = [sb(f"rows{r}", [P, QT, D]) for r in range(DEEP)]
        x = [sb(f"x{r}", [P, QT, D]) for r in range(2)]
        base = [sb(f"base{r}", [P, QT, D]) for r in range(2)]
        bo = sb("bo", [P, D])
        place = [sb(f"place{r}", [P, 2, QT], I32) for r in range(DEEP)]
        xt = [sb(f"xt{r}", [P, HALVES, KD, T], F32R) for r in range(2)]
        tanh = sb("tanh", [P, T])
        gated = sb("gated", [P, T])
        hidden = [sb(f"hidden{r}", [P, T]) for r in range(2)]
        hs = [sb(f"hs{r}", [P, HALVES, T], F32R) for r in range(2)]
        xt_ps = pb("xt_ps", [P, KD, T])
        gate_ps = [pb(f"gate_ps{r}", [P, T]) for r in range(2)]
        up_ps = [pb(f"up_ps{r}", [P, T]) for r in range(2)]
        y_ps = pb("y_ps", [P, QT, D])
        rows_loaded = [sem(f"rows_loaded{r}") for r in range(DEEP)]
        x_loaded = [sem(f"x_loaded{r}") for r in range(2)]
        bo_loaded = sem("bo_loaded")
        placed = sem("placed")
        queued = [sem(f"queued{r}") for r in range(DEEP)]
        packed = sem("packed")
        xt_ready, xt_hi, xt_done = sem("xt_ready"), sem("xt_hi"), sem("xt_done")
        gu_ready, tanh_done, gated_done, hidden_done = sem("gu_ready"), sem("tanh_done"), sem("gated_done"), sem("hidden_done")
        hs_hi, hs_done, y_ready = sem("hs_hi"), sem("hs_done"), sem("y_ready")
        x_summed, bo_summed, base_done = sem("x_summed"), sem("bo_summed"), sem("base_done")
        base_stored = [sem(f"base_stored{r}") for r in range(2)]
        x_src = ins["L0_attn_x"].rearrange("b (q p) d -> b p q d", p=P)
        SCATTERS = 2 * QT

        def batches(eng, step):
            with eng.Fori(0, B // DEEP - 1) as g:
                for r in range(DEEP):
                    step(g * DEEP + r, g, r, lambda a: True)
            for r in range(DEEP):
                step(B - DEEP + r, B // DEEP - 1, r, lambda a, r=r: r + a < DEEP)

        def round_of(g, r, ahead):
            return g + (r + ahead) // DEEP

        with nc.Block() as block:
            @block.sync
            def _(sp):
                def load_rows(b, r):
                    sp.dma_start(rows[r][:, :, :], dram["xn"][bass.ds(b, 1)].rearrange("b p q d -> (b p) q d")
                                 ).then_inc(rows_loaded[r], DMA)

                def load_x(b, r):
                    sp.dma_start(x[r % 2][:, :, :], x_src[bass.ds(b, 1)].rearrange("b p q d -> (b p) q d")
                                 ).then_inc(x_loaded[r % 2], DMA)

                def pack(expert):
                    for n, name in enumerate(("wg", "wu", "wd")):
                        to = dram["experts"][bass.ds(expert, 2), :, n * WPART:(n + 1) * WPART]
                        src = ins["L0_ffn_experts_" + name][bass.ds(expert, 2), :, :]
                        for k in range(KD if n < 2 else 1):
                            part = (to[:, :, k * FF:(k + 1) * FF], src[:, k * P:(k + 1) * P, :]) if n < 2 else (to, src)
                            sp.dma_start(*part).then_inc(packed, DMA)

                def step(b, g, r, there):
                    if there(2):
                        wait_apart(sp, x_summed, b + 1, begun)
                        load_x(b + 2, r)
                    wait_apart(sp, base_done, START + b + 1, begun)
                    sp.dma_start(dram["base"][bass.ds(b, 1)].rearrange("b p q d -> (b p) q d"), base[r % 2][:, :, :]
                                 ).then_inc(base_stored[r % 2], DMA)
                    if r % 2 == 0:
                        pack(b)
                    if there(DEEP):
                        wait_apart(sp, xt_ready, (b + 1) * KD, begun)
                        wait_apart(sp, queued[r], (g + 1) * SCATTERS * DMA, begun)
                        load_rows(b + DEEP, r)

                for r in range(DEEP):
                    load_rows(r, r)
                    if r < 2:
                        load_x(r, r)
                sp.dma_start(bo[:, :], ins["L0_attn_bo"].rearrange("(a n) -> a n", a=1).broadcast_to([P, D])
                             ).then_inc(bo_loaded, DMA)
                batches(sp, step)
                for r in range(2):
                    sp.wait_ge(base_stored[r], START + B // 2 * DMA)
                sp.wait_ge(packed, E // 2 * (2 * KD + 1) * DMA)

            @block.gpsimd
            def _(pool):
                for counter in (gu_ready, hidden_done, base_done, y_ready, *base_stored, xt_done):
                    pool.sem_inc(counter, START)
                with pool.Fori(0, B // DEEP) as g:
                    for r in range(DEEP):
                        wait_apart(pool, rows_loaded[r], (g + 1) * DMA, begun)
                        wait_apart(pool, placed, (g * DEEP + r + 1) * 2, begun)
                        for q in range(QT):
                            for n in range(2):
                                pool.indirect_dma_start(
                                    out=dram["queued"][:, :],
                                    out_offset=bass.IndirectOffsetOnAxis(ap=place[r][:, n, q:q + 1], axis=0),
                                    in_=rows[r][:, q, :], in_offset=None,
                                    bounds_check=SLOTS - 1, oob_is_err=False).then_inc(queued[r], DMA)
                for r in range(DEEP):
                    pool.wait_ge(queued[r], B // DEEP * SCATTERS * DMA)

            @block.tensor
            def _(pe):
                def transposes(b, g, r):
                    pe.wait_ge(rows_loaded[r], (g + 1) * DMA)
                    pe.wait_ge(xt_done, START + b * KD)
                    for k in range(KD):
                        for q in range(QT):
                            last = pe.transpose(xt_ps[:, k, q * P:(q + 1) * P], rows[r][:, q, k * P:(k + 1) * P],
                                                ident[:, :])
                        last.then_inc(xt_ready, 1)

                def step(b, g, r, there):
                    pe.wait_ge(xt_done, START + (b + 1) * KD)
                    pe.wait_ge(hidden_done, START + b)
                    for to, cols in ((gate_ps[r % 2], gate_cols), (up_ps[r % 2], up_cols)):
                        n = 0
                        for k in range(KD):
                            for wa, xb in PASSES:
                                n += 1
                                last = pe.matmul(to[:, :], w[:, wa, cols(k)], xt[r % 2][:, xb, k, :], start=(n == 1),
                                                 stop=(n == KD * len(PASSES)))
                    last.then_inc(gu_ready, 1)
                    if there(1):
                        transposes(b + 1, round_of(g, r, 1), (r + 1) % DEEP)
                    pe.wait_ge(hs_done, b + 1)
                    pe.wait_ge(base_done, START + b)
                    for q in range(QT):
                        for n, (ha, wb) in enumerate(PASSES):
                            last = pe.matmul(y_ps[:, q, :], hs[r % 2][:, ha, q * P:(q + 1) * P], w[:, wb, DOWN_COLS],
                                             start=(n == 0), stop=(n == len(PASSES) - 1))
                    last.then_inc(y_ready, 1)

                transposes(0, 0, 0)
                batches(pe, step)

            @block.scalar
            def _(act):
                def split_xt(b, r):
                    for k in range(KD):
                        act.wait_ge(xt_ready, b * KD + k + 1)
                        act.activation(xt[r % 2][:, HI, k, :], xt_ps[:, k, :], ACT.Copy).then_inc(xt_hi, 1)

                def step(b, g, r, there):
                    act.wait_ge(gu_ready, START + b + 1)
                    act.activation(tanh[:, :], gate_ps[r % 2][:, :], ACT.Tanh, scale=0.5).then_inc(tanh_done, 1)
                    if there(1):
                        split_xt(b + 1, r + 1)
                    act.wait_ge(hidden_done, START + b + 1)
                    act.wait_ge(y_ready, START + b)
                    act.activation(hs[r % 2][:, HI, :], hidden[r % 2][:, :], ACT.Copy).then_inc(hs_hi, 1)

                split_xt(0, 0)
                batches(act, step)

            @block.vector
            def _(dve):
                def look_up(b, g, r):
                    dve.wait_ge(rows_loaded[r], (g + 1) * DMA)
                    for n in range(2):
                        dve.tensor_copy(place[r][:, n, :], keep["slot"][n][:, bass.ds(b * QT, QT)]).then_inc(placed, 1)

                def split_xt(b, r):
                    for k in range(KD):
                        dve.wait_ge(xt_hi, b * KD + k + 1)
                        dve.tensor_tensor(xt[r % 2][:, LO, k, :], xt_ps[:, k, :], xt[r % 2][:, HI, k, :].bitcast(F32),
                                          ALU.subtract).then_inc(xt_done, 1)

                def step(b, g, r, there):
                    if there(2):
                        look_up(b + 2, round_of(g, r, 2), (r + 2) % DEEP)
                    dve.wait_ge(tanh_done, b + 1)
                    dve.scalar_tensor_tensor(gated[:, :], tanh[:, :], 1.0, gate_ps[r % 2][:, :], ALU.add, ALU.mult
                                             ).then_inc(gated_done, 1)
                    dve.wait_ge(gated_done, b + 1)
                    dve.scalar_tensor_tensor(hidden[r % 2][:, :], gated[:, :], 0.5, up_ps[r % 2][:, :], ALU.mult,
                                             ALU.mult).then_inc(hidden_done, 1)
                    if there(1):
                        split_xt(b + 1, r + 1)
                    dve.wait_ge(hs_hi, b + 1)
                    dve.tensor_tensor(hs[r % 2][:, LO, :], hidden[r % 2][:, :], hs[r % 2][:, HI, :].bitcast(F32),
                                      ALU.subtract).then_inc(hs_done, 1)
                    dve.wait_ge(x_loaded[r % 2], (g * 2 + r // 2 + 1) * DMA)
                    dve.wait_ge(base_stored[r % 2], START + (g * 2 + r // 2) * DMA)
                    dve.tensor_tensor(base[r % 2][:, :, :], x[r % 2][:, :, :], rows[r][:, :, :], ALU.add
                                      ).then_inc(x_summed, 1)
                    dve.wait_ge(x_summed, b + 1)
                    dve.tensor_tensor(base[r % 2][:, :, :], base[r % 2][:, :, :], bo[:, None, :].broadcast_to([P, QT, D]),
                                      ALU.add).then_inc(bo_summed, 1)
                    dve.wait_ge(y_ready, START + b + 1)
                    dve.wait_ge(bo_summed, b + 1)
                    dve.tensor_tensor(base[r % 2][:, :, :], y_ps[:, :, :], base[r % 2][:, :, :], ALU.add
                                      ).then_inc(base_done, 1)

                dve.wait_ge(bo_loaded, DMA)
                look_up(0, 0, 0)
                look_up(1, 0, 1)
                split_xt(0, 0)
                batches(dve, step)


def stage_c(nc, dram, keep):
    begun = keep["begun"]
    with ExitStack() as ctx:
        def sb(name, shape, dt=F32):
            return ctx.enter_context(nc.sbuf_tensor("c_" + name, shape, dt))

        def pb(name, shape, dt=F32):
            return ctx.enter_context(nc.psum_tensor("c_" + name, shape, dt))

        def sem(name):
            return ctx.enter_context(nc.semaphore("c_" + name))

        DEEP = 4
        FETCH = 6
        ident = keep["ident"]
        row = [sb(f"row{r}", [P, 1], I32) for r in range(DEEP)]
        w_in = [sb(f"w_in{r}", [P, WROW]) for r in range(DEEP)]
        w = [sb(f"w{r}", [P, HALVES, WROW], F32R) for r in range(DEEP)]
        x = [sb(f"x{r}", [P, SUB, D]) for r in range(DEEP)]
        xt = [sb(f"xt{r}", [P, HALVES, KD, SLOT_TILE], F32R) for r in range(2)]
        tanh = [sb(f"tanh{r}", [P, SLOT_TILE]) for r in range(2)]
        gated = [sb(f"gated{r}", [P, SLOT_TILE]) for r in range(2)]
        hidden = [sb(f"hidden{r}", [P, SLOT_TILE]) for r in range(2)]
        hs = [sb(f"hs{r}", [P, HALVES, SLOT_TILE], F32R) for r in range(2)]
        y = [sb(f"y{r}", [P, SUB, D]) for r in range(DEEP)]
        xt_ps = [pb(f"xt_ps{r}", [P, KD, SLOT_TILE]) for r in range(2)]
        gu_ps = [pb(f"gu_ps{r}", [P, 2, SLOT_TILE]) for r in range(2)]
        y_ps = [pb(f"y_ps{r}", [P, SUB, D]) for r in range(2)]
        row_done = sem("row_done")
        w_loaded = [sem(f"w_loaded{r}") for r in range(DEEP)]
        x_loaded = [sem(f"x_loaded{r}") for r in range(DEEP)]
        y_stored = [sem(f"y_stored{r}") for r in range(DEEP)]
        w_hi = sem("w_hi")
        w_split, down_split = sem("w_split"), sem("down_split")
        xt_ready, xt_hi, xt_done = sem("xt_ready"), sem("xt_hi"), sem("xt_done")
        gu_ready, tanh_done, gated_done, hidden_done = sem("gu_ready"), sem("tanh_done"), sem("gated_done"), sem("hidden_done")
        hs_hi, hs_done, y_ready, y_done = sem("hs_hi"), sem("hs_done"), sem("y_ready"), sem("y_done")
        ROUNDS = SLOT_TILES // DEEP

        def ticks(eng, before, tick):
            for t in range(-before, 0):
                tick(t, -1, t % DEEP, lambda a, t=t: t + a >= 0)
            with eng.Fori(0, ROUNDS - 2) as g:
                for r in range(DEEP):
                    tick(g * DEEP + r, g, r, lambda a: True)
            for t in range(SLOT_TILES - 2 * DEEP, SLOT_TILES):
                tick(t, t // DEEP, t % DEEP, lambda a, t=t: t + a < SLOT_TILES)

        def round_of(g, r, ahead):
            return g + (r + ahead) // DEEP

        with nc.Block() as block:
            @block.sync
            def _(sp):
                def load(t, r):
                    sp.dma_start(x[r][:, :, :], dram["queued"][bass.ds(t * SLOT_TILE, SLOT_TILE), :]
                                 .rearrange("(s p) d -> p s d", p=P)).then_inc(x_loaded[r], DMA)

                def tick(t, g, r, there):
                    if there(FETCH):
                        wait_apart(sp, xt_ready, START + t + FETCH - DEEP + 1, begun)
                        load(t + FETCH, (r + FETCH) % DEEP)
                    wait_apart(sp, y_done, START + t + 1, begun)
                    sp.dma_start(dram["routed"][bass.ds(t * SLOT_TILE, SLOT_TILE), :]
                                 .rearrange("(s p) d -> p s d", p=P), y[r][:, :, :]).then_inc(y_stored[r], DMA)

                for t in range(FETCH):
                    if t >= DEEP:
                        sp.wait_ge(xt_ready, START + t - DEEP + 1)
                    load(t, t % DEEP)
                ticks(sp, 0, tick)
                for r in range(DEEP):
                    sp.wait_ge(y_stored[r], START + ROUNDS * DMA)

            @block.gpsimd
            def _(pool):
                for counter in (xt_ready, gu_ready, y_ready, xt_done, hidden_done, y_done, down_split, *y_stored, w_split):
                    pool.sem_inc(counter, START)

                def gather(t, r):
                    wait_apart(pool, row_done, t + 1, begun)
                    pool.indirect_dma_start(
                        out=w_in[r][:, :], out_offset=None, in_=dram["experts"].rearrange("e p n -> (e p) n"),
                        in_offset=bass.IndirectOffsetOnAxis(ap=row[r][:, 0:1], axis=0),
                        bounds_check=E * P - 1, oob_is_err=False).then_inc(w_loaded[r], DMA)

                def split(t, r):
                    wait_apart(pool, w_hi, t + 1, begun)
                    cols = slice(0, 2 * WPART)
                    pool.tensor_tensor(w[r][:, LO, cols], w_in[r][:, cols], w[r][:, HI, cols].bitcast(F32), ALU.subtract
                                       ).then_inc(w_split, 1)

                def tick(t, g, r, there):
                    if there(3):
                        split(t + 3, (r + 3) % DEEP)
                    if there(FETCH):
                        wait_apart(pool, w_split, START + t + 3, begun)
                        wait_apart(pool, down_split, START + t + 3, begun)
                        gather(t + FETCH, (r + FETCH) % DEEP)

                for r in range(DEEP):
                    gather(r, r)
                for r in range(3):
                    split(r, r)
                    if r + DEEP < FETCH:
                        wait_apart(pool, w_split, START + r + 1, begun)
                        wait_apart(pool, down_split, START + r + 1, begun)
                        gather(r + DEEP, r)
                ticks(pool, 0, tick)

            @block.tensor
            def _(pe):
                def tick(t, g, r, there):
                    if there(2):
                        h = (r + 2) % DEEP
                        pe.wait_ge(x_loaded[h], (round_of(g, r, 2) + 1) * DMA)
                        if there(0):
                            pe.wait_ge(xt_done, START + t + 1)
                        for k in range(KD):
                            for s in range(SUB):
                                last = pe.transpose(xt_ps[r % 2][:, k, s * P:(s + 1) * P], x[h][:, s, k * P:(k + 1) * P],
                                                    ident[:, :])
                        last.then_inc(xt_ready, 1)
                    if there(1):
                        o, h = (r + 1) % 2, (r + 1) % DEEP
                        pe.wait_ge(xt_done, START + t + 2)
                        pe.wait_ge(w_split, START + t + 2)
                        if there(0):
                            pe.wait_ge(hidden_done, START + t)
                        for part, cols in enumerate((gate_cols, up_cols)):
                            n = 0
                            for k in range(KD):
                                for wa, xb in PASSES:
                                    n += 1
                                    last = pe.matmul(gu_ps[o][:, part, :], w[h][:, wa, cols(k)], xt[o][:, xb, k, :],
                                                     start=(n == 1), stop=(n == KD * len(PASSES)))
                        last.then_inc(gu_ready, 1)
                    if there(0):
                        pe.wait_ge(hs_done, t + 1)
                        pe.wait_ge(down_split, START + t + 1)
                        pe.wait_ge(y_done, START + t)
                        for s in range(SUB):
                            for n, (ha, wb) in enumerate(PASSES):
                                last = pe.matmul(y_ps[r % 2][:, s, :], hs[r % 2][:, ha, s * P:(s + 1) * P],
                                                 w[r][:, wb, DOWN_COLS], start=(n == 0), stop=(n == len(PASSES) - 1))
                        last.then_inc(y_ready, 1)

                pe.wait_ge(w_split, START)
                ticks(pe, 2, tick)

            @block.scalar
            def _(act):
                def split_weights(g, r):
                    act.wait_ge(w_loaded[r], (g + 1) * DMA)
                    act.activation(w[r][:, HI, :], w_in[r][:, :], ACT.Copy).then_inc(w_hi, 1)

                def take_y(t, g, r):
                    act.wait_ge(y_ready, START + t + 1)
                    act.wait_ge(y_stored[r], START + g * DMA)
                    act.activation(y[r][:, :, :], y_ps[r % 2][:, :, :], ACT.Copy).then_inc(y_done, 1)

                def tick(t, g, r, there):
                    if there(2):
                        act.wait_ge(xt_ready, START + t + 3)
                        if there(0):
                            act.wait_ge(gu_ready, START + t + 1)
                        act.activation(xt[r % 2][:, HI, :, :], xt_ps[r % 2][:, :, :], ACT.Copy).then_inc(xt_hi, 1)
                    if there(1):
                        o = (r + 1) % 2
                        act.wait_ge(gu_ready, START + t + 2)
                        act.activation(tanh[o][:, :], gu_ps[o][:, 0, :], ACT.Tanh, scale=0.5).then_inc(tanh_done, 1)
                    if there(0) and there(3):
                        act.wait_ge(y_ready, START + t)
                        split_weights(round_of(g, r, 3), (r + 3) % DEEP)
                    if there(0):
                        take_y(t, g, r)
                    if there(1):
                        if there(0):
                            act.wait_ge(y_ready, START + t)
                        act.wait_ge(hidden_done, START + t + 2)
                        act.activation(hs[o][:, HI, :], hidden[o][:, :], ACT.Copy).then_inc(hs_hi, 1)

                for r in range(3):
                    split_weights(0, r)
                ticks(act, 2, tick)

            @block.vector
            def _(dve):
                def look_up(t, r):
                    dve.tensor_copy(row[r][:, :], keep["weight_row"][:, bass.ds(t, 1)]).then_inc(row_done, 1)

                def tick(t, g, r, there):
                    if there(0) and there(FETCH):
                        dve.wait_ge(w_loaded[(r + 2) % DEEP], (round_of(g, r, 2) + 1) * DMA)
                        look_up(t + FETCH, (r + FETCH) % DEEP)
                    if there(2):
                        dve.wait_ge(xt_hi, t + 3)
                        dve.tensor_tensor(xt[r % 2][:, LO, :, :], xt_ps[r % 2][:, :, :],
                                          xt[r % 2][:, HI, :, :].bitcast(F32), ALU.subtract).then_inc(xt_done, 1)
                    if there(1):
                        o = (r + 1) % 2
                        dve.wait_ge(tanh_done, t + 2)
                        dve.scalar_tensor_tensor(gated[o][:, :], tanh[o][:, :], 1.0, gu_ps[o][:, 0, :], ALU.add, ALU.mult
                                                 ).then_inc(gated_done, 1)
                        dve.wait_ge(gated_done, t + 2)
                        dve.scalar_tensor_tensor(hidden[o][:, :], gated[o][:, :], 0.5, gu_ps[o][:, 1, :], ALU.mult,
                                                 ALU.mult).then_inc(hidden_done, 1)
                    if there(0) and there(3):
                        split_down(t + 3, (r + 3) % DEEP)
                    if there(1):
                        dve.wait_ge(hs_hi, t + 2)
                        dve.tensor_tensor(hs[o][:, LO, :], hidden[o][:, :], hs[o][:, HI, :].bitcast(F32),
                                          ALU.subtract).then_inc(hs_done, 1)

                def split_down(t, r):
                    dve.wait_ge(w_hi, t + 1)
                    dve.tensor_tensor(w[r][:, LO, DOWN_COLS], w_in[r][:, DOWN_COLS], w[r][:, HI, DOWN_COLS].bitcast(F32),
                                      ALU.subtract).then_inc(down_split, 1)

                for t in range(FETCH):
                    if t >= DEEP:
                        dve.wait_ge(w_loaded[t % DEEP], DMA)
                    look_up(t, t % DEEP)
                for t in range(3):
                    split_down(t, t)
                ticks(dve, 2, tick)


def stage_d(nc, dram, keep, out):
    begun = keep["begun"]
    with ExitStack() as ctx:
        def sb(name, shape, dt=F32):
            return ctx.enter_context(nc.sbuf_tensor("d_" + name, shape, dt))

        def sem(name):
            return ctx.enter_context(nc.semaphore("d_" + name))

        ident, mask = keep["ident"], keep["mask"]
        wv, wo = keep["wv"], keep["wo"]
        w_pair = [sb(f"w_pair{n}", [P, HALVES, KD, P], F32R) for n in range(2)]
        xnt = sb("xnt", [P, HALVES, KD, T], F32R)
        qs = [[sb(f"qs{r}{h}", [P, T], F32R) for h in range(2)] for r in range(2)]
        ks = [[[sb(f"ks{r}{h}{hl}", [P, T], F32R) for hl in range(HALVES)] for h in range(2)] for r in range(2)]
        v = sb("v", [P, QT, H * DK])
        vp = sb("vp", [P, 2, QT, P])
        probs = [[sb(f"probs{i}{h}", [P, T]) for h in range(2)] for i in range(QT)]
        probs_t = [[sb(f"probs_t{h}{i}", [P, QT, P]) for i in range(2)] for h in range(2)]
        out_t = [sb(f"out_t{hl}", [P, PAIRS, T], F32R) for hl in range(HALVES)]
        top = [sb(f"top{i}", [P, 2]) for i in range(QT)]
        bias = [sb(f"bias{i}", [P, 2]) for i in range(QT)]
        total = [sb(f"total{i}", [P, 2]) for i in range(QT)]
        inverse = [sb(f"inverse{i}", [P, 2]) for i in range(QT)]
        base = sb("base", [P, QT, D])
        summed = sb("summed", [P, QT, D])
        routed = sb("routed", [P, 2, QT, D])
        place = sb("place", [P, 2, QT], I32)
        share = sb("share", [P, 2, QT])

        def bank(name):
            return ctx.enter_context(nc.psum_tensor("d_" + name, [P, T], F32))

        s_ps = [[bank(f"s_ps{r}{h}") for h in range(2)] for r in range(2)]
        t_ps = [bank(f"t_ps{h}") for h in range(2)]
        o_ps = bank("o_ps")
        m_ps = bank("m_ps")

        base_loaded, stored = sem("base_loaded"), sem("stored")
        xnt_loaded = [sem(f"xnt_loaded{k}") for k in range(KD)]
        w_loaded = [sem(f"w_loaded{n}") for n in range(2)]
        cleared = sem("cleared")
        m_ready = sem("m_ready")
        m_hi, m_out = sem("m_hi"), sem("m_out")
        s_ready = sem("s_ready")
        s_out = sem("s_out")
        bias_done = sem("bias_done")
        exp_done = sem("exp_done")
        inverse_done = sem("inverse_done")
        norm_done = sem("norm_done")
        t_ready = [sem(f"t_ready{h}") for h in range(2)]
        t_out = [sem(f"t_out{h}") for h in range(2)]
        o_ready, o_hi, o_out = sem("o_ready"), sem("o_hi"), sem("o_out")

        placed, gathered, shared_out = sem("placed"), sem("gathered"), sem("shared_out")
        weighted, first_added, routed_added = sem("weighted"), sem("first_added"), sem("routed_added")
        out_d = out.rearrange("b (q p) d -> b p q d", p=P)

        vp_loaded = [sem(f"vp_loaded{r}") for r in range(2)]
        k_copied = [sem(f"k_copied{r}") for r in range(2)]

        V_GROUPS = 2 * QT
        T_FIRST = V_GROUPS // 2
        M = 2
        OUT_VIA = (M, 1, 0, M)
        T_USES = [QT * PAIRS + V_GROUPS // 2 + OUT_VIA.count(h) for h in range(2)]
        PROJ = 2 * PAIRS
        M_USES = PROJ + QT // 2
        M_OUTS = 2 * PROJ + QT // 2
        M_FIRST = 4
        GATHERS = 2 * QT
        K_COLS = [max(2 * P, (i + 1) * P) for i in range(QT)]

        def unit(b, jp, r):
            return b * PAIRS + jp * 2 + r

        def head_half(h):
            return slice(h * DK, (h + 1) * DK)

        def v_uses_of(final):
            return 0 if final else T_FIRST

        with nc.Block() as block:
            @block.sync
            def _(sp):
                def load_weights(which, pair):
                    sp.dma_start(w_pair[which][:, :, :, :].rearrange("p s k n -> p (s k n)").bitcast(F32),
                                 keep["wqk"][:, bass.ds(pair, 1), which, :, :, :].rearrange("p j s k n -> p (j s k n)").bitcast(F32)
                                 ).then_inc(w_loaded[which], DMA)

                def load_xnt(batch):
                    for k in range(KD):
                        sp.dma_start(xnt[:, :, k, :].bitcast(F32), dram["xnt"][bass.ds(batch, 1)].rearrange(
                            "b p (a k t) -> (b p) a k t", a=HALVES, k=KD)[:, :, k, :]).then_inc(xnt_loaded[k], DMA)

                def load_v_pair(pair, r):
                    sp.dma_start(vp[:, r, :, :], v[:, :, bass.ds(pair * P, P)]).then_inc(vp_loaded[r], DMA)

                def copy_keys(r):
                    for h in range(2):
                        sp.dma_start(ks[r][h][HI][head_half(1 - h), :].bitcast(F32), ks[r][h][HI][head_half(h), :].bitcast(F32)
                                     ).then_inc(k_copied[r], DMA)

                load_xnt(0)
                load_weights(1, 0)
                load_weights(0, 0)
                sp.wait_ge(m_ready, 1)
                load_weights(1, 1)
                sp.wait_ge(m_ready, 2)
                load_weights(0, 1)
                sp.wait_ge(m_hi, 2)
                copy_keys(0)
                sp.wait_ge(m_ready, 3)
                load_weights(1, 2)
                sp.wait_ge(m_ready, 4)
                load_weights(0, 2)
                sp.wait_ge(m_hi, 6)
                copy_keys(1)
                for h in range(2):
                    sp.wait_ge(t_out[h], T_FIRST)
                load_v_pair(0, 0)
                def batch(b, final):
                    def load_v(un, r):
                        wait_apart(sp, o_ready, START + b * PAIRS + un, begun)
                        load_v_pair(un + 1, 1 - r)

                    def load_keys(un, pair):
                        wait_apart(sp, m_ready, M_FIRST + b * M_USES + un * 2 + 1, begun)
                        load_weights(1, pair)

                    def copy_split_keys(un, r):
                        wait_apart(sp, m_hi, 2 * M_FIRST + (b * PAIRS + un) * 4 + 2, begun)
                        copy_keys(r)

                    def load_queries(un, pair):
                        wait_apart(sp, m_ready, M_FIRST + b * M_USES + un * 2 + 2, begun)
                        load_weights(0, pair)

                    wait_apart(sp, m_out, b * M_OUTS + 2 * M_FIRST, begun)
                    wait_apart(sp, t_out[1], b * T_USES[1] + T_FIRST, begun)
                    sp.dma_start(base[:, :, :], dram["base"][bass.ds(b, 1)].rearrange("b p q d -> (b p) q d")
                                 ).then_inc(base_loaded, DMA)
                    with sp.Fori(0, PAIRS // 2 - 2) as jp:
                        for r in range(2):
                            un = jp * 2 + r
                            load_v(un, r)
                            load_keys(un, (un + 3) & (PAIRS - 1))
                            copy_split_keys(un, r)
                            load_queries(un, (un + 3) & (PAIRS - 1))
                    load_v(PAIRS - 4, 0)
                    load_keys(PAIRS - 4, PAIRS - 1)
                    copy_split_keys(PAIRS - 4, 0)
                    load_queries(PAIRS - 4, PAIRS - 1)
                    load_v(PAIRS - 3, 1)
                    load_keys(PAIRS - 3, 0)
                    copy_split_keys(PAIRS - 3, 1)
                    wait_apart(sp, m_ready, M_FIRST + b * M_USES + (PAIRS - 3) * 2 + 2, begun)
                    load_xnt((b + 1) & (B - 1))
                    load_weights(0, 0)
                    load_v(PAIRS - 2, 0)
                    load_keys(PAIRS - 2, 1)
                    copy_split_keys(PAIRS - 2, 0)
                    load_queries(PAIRS - 2, 1)
                    load_keys(PAIRS - 1, 2)
                    copy_split_keys(PAIRS - 1, 1)
                    load_queries(PAIRS - 1, 2)
                    if not final:
                        for h in range(2):
                            wait_apart(sp, t_out[h], b * T_USES[h] + QT * PAIRS + 2 * T_FIRST, begun)
                        load_v_pair(0, 0)
                    wait_apart(sp, t_out[1], (b + 1) * T_USES[1] + v_uses_of(final), begun)
                    wait_apart(sp, m_out, (b + 1) * M_OUTS + 2 * M_FIRST, begun)
                    sp.dma_start(out_d[bass.ds(b, 1)].rearrange("b p q d -> (b p) q d"), summed[:, :, :]
                                 ).then_inc(stored, DMA)

                with sp.Fori(0, B - 1) as b:
                    batch(b, False)
                batch(B - 1, True)
                sp.wait_ge(stored, START + B * DMA)
                sp.wait_ge(vp_loaded[0], B * PAIRS // 2 * DMA)
                sp.wait_ge(vp_loaded[1], B * PAIRS // 2 * DMA)
                for r in range(2):
                    sp.wait_ge(k_copied[r], (B * PAIRS // 2 + 1) * 2 * DMA)
                sp.wait_ge(w_loaded[0], (B * PAIRS + 3) * DMA)
                sp.wait_ge(w_loaded[1], (B * PAIRS + 3) * DMA)

            @block.tensor
            def _(pe):
                def project(which, loaded, before, xnts=None):
                    pe.wait_ge(w_loaded[which], loaded)
                    if before is not None:
                        pe.wait_ge(m_hi, before[0])
                        pe.wait_ge(m_out, before[1])
                    n = 0
                    for k in range(KD):
                        if xnts is not None:
                            pe.wait_ge(xnt_loaded[k], xnts * DMA)
                        for wa, xb in PASSES:
                            n += 1
                            last = pe.matmul(m_ps[:, :], w_pair[which][:, wa, k, :], xnt[:, xb, k, :], start=(n == 1),
                                             stop=(n == KD * len(PASSES)))
                    last.then_inc(m_ready, 1)

                def scores(r, i, outs, before):
                    if outs is not None:
                        pe.wait_ge(m_out, outs[0])
                        pe.wait_ge(k_copied[r], outs[1])
                    for h in range(2):
                        if before is not None:
                            pe.wait_ge(s_out, before * 2 + h + 1)
                        cols = K_COLS[i]
                        for hl in range(HALVES):
                            last = pe.matmul(s_ps[i % 2][h][:, 0:cols], qs[r][h][:, i * P:(i + 1) * P],
                                             ks[r][h][hl][:, 0:cols], start=(hl == 0), stop=(hl == 1))
                        last.then_inc(s_ready, 1)

                def transposes(i, step_no, uses):
                    for h in range(2):
                        pe.wait_ge(norm_done, step_no * 2 + h + 1)
                        pe.wait_ge(t_out[h], uses[h])
                        for j in range(i + 1):
                            last = pe.transpose(t_ps[h][:, j * P:(j + 1) * P], probs[i][h][:, j * P:(j + 1) * P], ident[:, :])
                        last.then_inc(t_ready[h], 1)

                def weigh(r, i, u, uses, copied):
                    if i == 0:
                        pe.wait_ge(o_out, START + u)
                        pe.wait_ge(vp_loaded[r], copied)
                    for h in range(2):
                        pe.wait_ge(t_out[h], uses[h] + 1)
                    for j in range(i + 1):
                        for h in range(2):
                            last = pe.matmul(o_ps[head_half(h), i * P:(i + 1) * P], vp[:, r, j, head_half(h)],
                                             probs_t[h][i % 2][:, j, :], start=(j == 0), stop=(j == i))
                    if i == QT - 1:
                        last.then_inc(o_ready, 1)

                def project_v(first_uses):
                    for g in range(V_GROUPS):
                        tok, half = divmod(g, 2)
                        if first_uses is not None:
                            pe.wait_ge(t_out[half], first_uses[half] + tok)
                        elif tok:
                            pe.wait_ge(t_out[half], tok)
                        n = 0
                        for k in range(KD):
                            for xa, wb in PASSES:
                                n += 1
                                last = pe.matmul(t_ps[half][:, :], xnt[:, xa, k, tok * P:(tok + 1) * P],
                                                 wv[:, wb, k, half * T:(half + 1) * T], start=(n == 1),
                                                 stop=(n == KD * len(PASSES)))
                        last.then_inc(t_ready[half], 1)

                def project_out(b, t_uses, outs):
                    for q, via in enumerate(OUT_VIA):
                        if via == M:
                            to, ready = m_ps, m_ready
                            pe.wait_ge(m_out, outs + OUT_VIA[:q].count(M))
                        else:
                            to, ready = t_ps[via], t_ready[via]
                            pe.wait_ge(t_out[via], t_uses[via])
                        for j in range(PAIRS):
                            if j == PAIRS - 1 and q == 0:
                                pe.wait_ge(o_out, START + (b + 1) * PAIRS)
                            elif j == 0 and q == 0:
                                pe.wait_ge(o_out, START + (b + 1) * PAIRS - 1)
                            for n, (oa, wb) in enumerate(PASSES):
                                last = pe.matmul(to[:, 0:D], out_t[oa][:, j, q * P:(q + 1) * P], wo[:, wb, j, :],
                                                 start=(j == 0 and n == 0),
                                                 stop=(j == PAIRS - 1 and n == len(PASSES) - 1))
                        last.then_inc(ready, 1)

                for k in range(KD):
                    pe.wait_ge(xnt_loaded[k], DMA)
                project_v(None)
                project(1, DMA, None)
                project(0, DMA, (2, 2))
                pe.wait_ge(cleared, 2)
                project(1, 2 * DMA, (4, 4))
                project(0, 2 * DMA, (6, 6))
                scores(0, 0, (4, 2 * DMA), None)
                scores(0, 1, None, None)
                scores(0, 2, None, 0)
                def batch(b, final):
                    with pe.Fori(0, PAIRS // 2) as jp:
                        for r in range(2):
                            un = jp * 2 + r
                            u = unit(b, jp, r)
                            his = 2 * M_FIRST + b * 2 * PROJ + un * 4
                            outs = 2 * M_FIRST + b * M_OUTS + un * 4

                            def uses(i):
                                return [T_FIRST + b * T_USES[h] + un * QT + i for h in range(2)]

                            for i in range(QT):
                                transposes(i, u * QT + i, uses(i))
                                if i == 0:
                                    scores(r, QT - 1, None, u * QT + 1)
                                else:
                                    scores(1 - r, i - 1, (outs, (b * (PAIRS // 2) + jp + 1 + r) * 2 * DMA) if i == 1 else None,
                                           u * QT + i + 1)
                                if i == 0:
                                    project(1, (u + 3) * DMA, (his, outs), b + 1 + ((un + 2) >> 3))
                                if i:
                                    weigh(r, i - 1, u, uses(i - 1), (b * (PAIRS // 2) + jp + 1) * DMA)
                                if i == 2:
                                    project(0, (u + 3) * DMA, (his + 2, outs + 2))
                            weigh(r, QT - 1, u, uses(QT - 1), None)
                    v_uses = [T_FIRST + b * T_USES[h] + QT * PAIRS for h in range(2)]
                    if not final:
                        project_v(v_uses)
                    project_out(b, [uses + v_uses_of(final) for uses in v_uses], 2 * M_FIRST + b * M_OUTS + 2 * PROJ)

                with pe.Fori(0, B - 1) as b:
                    batch(b, False)
                batch(B - 1, True)

            @block.scalar
            def _(act):
                def split_keys(r, ready):
                    act.wait_ge(m_ready, ready)
                    for h in range(2):
                        act.activation(ks[r][h][HI][head_half(h), :], m_ps[head_half(h), :], ACT.Copy).then_inc(m_hi, 1)

                def split_queries(r, ready):
                    act.wait_ge(m_ready, ready)
                    for h in range(2):
                        act.activation(qs[r][h][head_half(h), :], m_ps[head_half(h), :], ACT.Copy).then_inc(m_hi, 1)

                def exponentials(i, step_no):
                    act.wait_ge(bias_done, step_no + 1)
                    for h in range(2):
                        part = probs[i][h][:, 0:(i + 1) * P]
                        act.activation(part, part, ACT.Exp, bias=bias[i][:, h:h + 1], scale=SCALE,
                                       accum_out=total[i][:, h:h + 1]).then_inc(exp_done, 1)

                def take_v(copied, ready):
                    for r in range(2) if copied is not None else ():
                        act.wait_ge(vp_loaded[r], copied)
                    for tok in range(QT):
                        act.wait_ge(t_ready[0], ready + tok + 1)
                        act.activation(v[:, tok, 0:T], t_ps[0][:, :], ACT.Copy).then_inc(t_out[0], 1)

                take_v(None, 0)
                split_keys(0, 1)
                split_queries(0, 2)
                split_keys(1, 3)
                split_queries(1, 4)
                for i in range(2):
                    exponentials(i, i)
                def batch(b, final):
                    with act.Fori(0, PAIRS // 2) as jp:
                        for r in range(2):
                            u = unit(b, jp, r)
                            for i in range(QT):
                                act.wait_ge(t_ready[0], T_FIRST + b * T_USES[0] + (jp * 2 + r) * QT + i + 1)
                                act.activation(probs_t[0][i % 2][:, 0:i + 1, :], t_ps[0][:, 0:(i + 1) * P].rearrange(
                                    "p (j n) -> p j n", n=P), ACT.Copy).then_inc(t_out[0], 1)
                                ready = M_FIRST + b * M_USES + (jp * 2 + r) * 2
                                if i == 1:
                                    split_keys(r, ready + 1)
                                if i == 3:
                                    split_queries(r, ready + 2)
                                exponentials((i + 2) % QT, u * QT + i + 2)
                            act.wait_ge(o_ready, START + u + 1)
                            act.activation(out_t[HI][:, bass.ds(jp * 2 + r, 1), :].rearrange("p a t -> p (a t)"),
                                           o_ps[:, :], ACT.Copy).then_inc(o_hi, 1)
                    if not final:
                        take_v((b + 1) * (PAIRS // 2) * DMA, T_FIRST + b * T_USES[0] + QT * PAIRS)

                with act.Fori(0, B - 1) as b:
                    batch(b, False)
                batch(B - 1, True)

            @block.vector
            def _(dve):
                def split_keys(r, his):
                    for h in range(2):
                        dve.wait_ge(m_hi, his + h + 1)
                        dve.tensor_tensor(ks[r][h][LO][head_half(h), :], m_ps[head_half(h), :],
                                          ks[r][h][HI][head_half(h), :].bitcast(F32), ALU.subtract).then_inc(m_out, 1)

                def split_queries(r, his):
                    for h in range(2):
                        dve.wait_ge(m_hi, his + h + 1)
                        dve.tensor_tensor(qs[r][h][head_half(1 - h), :], m_ps[head_half(h), :],
                                          qs[r][h][head_half(h), :].bitcast(F32), ALU.subtract).then_inc(m_out, 1)

                def maxima(i, step_no, between=None):
                    cols = (i + 1) * P
                    for h in range(2):
                        wait_apart(dve, s_ready, step_no * 2 + h + 1, begun)
                        dve.tensor_tensor_reduce(out=probs[i][h][:, 0:cols], in0=s_ps[i % 2][h][:, 0:cols],
                                                 in1=mask[:, T - cols:T], scale=1.0, scalar=-3e38, op0=ALU.add,
                                                 op1=ALU.max, accum_out=top[i][:, h:h + 1]).then_inc(s_out, 1)
                        if between and h == 0:
                            between()
                    dve.wait_ge(s_out, step_no * 2 + 2)
                    dve.tensor_scalar(bias[i][:, :], top[i][:, :], -SCALE, None, ALU.mult).then_inc(bias_done, 1)

                def invert(i, step_no):
                    dve.wait_ge(exp_done, step_no * 2 + 2)
                    dve.reciprocal(inverse[i][:, :], total[i][:, :]).then_inc(inverse_done, 1)

                def take_v(copied, ready):
                    for r in range(2) if copied is not None else ():
                        dve.wait_ge(vp_loaded[r], copied)
                    for tok in range(QT):
                        dve.wait_ge(t_ready[1], ready + tok + 1)
                        dve.tensor_copy(v[:, tok, T:2 * T], t_ps[1][:, :]).then_inc(t_out[1], 1)

                def look_up(batch):
                    for n in range(2):
                        dve.tensor_copy(place[:, n, :], keep["slot"][n][:, bass.ds(batch * QT, QT)]).then_inc(placed, 1)

                look_up(0)
                take_v(None, 0)
                split_keys(0, 0)
                split_queries(0, 2)
                split_keys(1, 4)
                split_queries(1, 6)
                for i in range(3):
                    maxima(i, i)
                for i in range(2):
                    invert(i, i)
                def batch(b, final):
                    with dve.Fori(0, PAIRS // 2) as jp:
                        for r in range(2):
                            u = unit(b, jp, r)
                            for i in range(QT):
                                dve.wait_ge(t_ready[1], T_FIRST + b * T_USES[1] + (jp * 2 + r) * QT + i + 1)
                                dve.tensor_copy(probs_t[1][i % 2][:, 0:i + 1, :], t_ps[1][:, 0:(i + 1) * P].rearrange(
                                    "p (j n) -> p j n", n=P)).then_inc(t_out[1], 1)
                                if i == 1:
                                    split_keys(r, 2 * M_FIRST + u * 4)
                                if i == 3:
                                    split_queries(r, 2 * M_FIRST + u * 4 + 2)
                                if i in (0,):
                                    maxima((i + 3) % QT, u * QT + i + 3,
                                           lambda: invert((i + 2) % QT, u * QT + i + 2))
                                else:
                                    maxima((i + 3) % QT, u * QT + i + 3)
                                    invert((i + 2) % QT, u * QT + i + 2)
                            dve.wait_ge(o_hi, u + 1)
                            dve.tensor_tensor(out_t[LO][:, bass.ds(jp * 2 + r, 1), :].rearrange("p a t -> p (a t)"),
                                              o_ps[:, :], out_t[HI][:, bass.ds(jp * 2 + r, 1), :].rearrange(
                                                  "p a t -> p (a t)").bitcast(F32), ALU.subtract).then_inc(o_out, 1)
                    dve.wait_ge(routed_added, START + b)
                    for n in range(2):
                        dve.tensor_copy(share[:, n, :], keep["weight"][n][:, bass.ds(b * QT, QT)]).then_inc(shared_out, 1)
                    if not final:
                        dve.wait_ge(gathered, (b + 1) * GATHERS * DMA)
                        look_up(b + 1)
                        take_v((b + 1) * (PAIRS // 2) * DMA, T_FIRST + b * T_USES[1] + QT * PAIRS)
                    dve.wait_ge(routed_added, START + b + 1)
                    dve.wait_ge(stored, START + b * DMA)
                    for q, via in enumerate(OUT_VIA):
                        if via == M:
                            dve.wait_ge(m_ready, M_FIRST + (b + 1) * M_USES - OUT_VIA[q + 1:].count(M))
                        else:
                            dve.wait_ge(t_ready[via], (b + 1) * T_USES[via] + v_uses_of(final))
                        dve.tensor_tensor(summed[:, q, :], (m_ps if via == M else t_ps[via])[:, 0:D], base[:, q, :],
                                          ALU.add).then_inc(m_out if via == M else t_out[via], 1)

                with dve.Fori(0, B - 1) as b:
                    batch(b, False)
                batch(B - 1, True)

            @block.gpsimd
            def _(pool):
                for counter in (o_out, o_ready, stored, routed_added):
                    pool.sem_inc(counter, START)

                def gather(nth):
                    wait_apart(pool, placed, (nth + 1) * 2, begun)
                    for q in range(QT):
                        for n in range(2):
                            pool.indirect_dma_start(
                                out=routed[:, n, q, :], out_offset=None, in_=dram["routed"][:, :],
                                in_offset=bass.IndirectOffsetOnAxis(ap=place[:, n, q:q + 1], axis=0),
                                bounds_check=SLOTS - 1, oob_is_err=False).then_inc(gathered, DMA)

                def normalise(i, step_no):
                    wait_apart(pool, inverse_done, step_no + 1, begun)
                    for h in range(2):
                        part = probs[i][h][:, 0:(i + 1) * P]
                        pool.tensor_scalar(part, part, inverse[i][:, h:h + 1], 1.0, ALU.mult, ALU.mult).then_inc(norm_done, 1)

                gather(0)
                for r in range(2):
                    for h in range(2):
                        last = pool.memset(ks[r][h][LO][head_half(1 - h), :].bitcast(F32), 0.0)
                    last.then_inc(cleared, 1)
                normalise(0, 0)
                def batch(b, final):
                    with pool.Fori(0, PAIRS // 2) as jp:
                        for r in range(2):
                            for i in range(QT):
                                normalise((i + 1) % QT, unit(b, jp, r) * QT + i + 1)
                    wait_apart(pool, shared_out, (b + 1) * 2, begun)
                    wait_apart(pool, base_loaded, (b + 1) * DMA, begun)
                    wait_apart(pool, gathered, (b + 1) * GATHERS * DMA, begun)
                    for n in range(2):
                        for q in range(QT):
                            last = pool.tensor_scalar(routed[:, n, q, :], routed[:, n, q, :], share[:, n, q:q + 1], 1.0,
                                                      ALU.mult, ALU.mult)
                        last.then_inc(weighted, 1)
                    wait_apart(pool, weighted, (b + 1) * 2, begun)
                    pool.tensor_tensor(base[:, :, :], base[:, :, :], routed[:, 0, :, :], ALU.add).then_inc(first_added, 1)
                    wait_apart(pool, first_added, b + 1, begun)
                    pool.tensor_tensor(base[:, :, :], base[:, :, :], routed[:, 1, :, :], ALU.add).then_inc(routed_added, 1)
                    if not final:
                        wait_apart(pool, routed_added, START + b + 1, begun)
                        gather(b + 1)

                with pool.Fori(0, B - 1) as b:
                    batch(b, False)
                batch(B - 1, True)
                pool.wait_ge(gathered, B * GATHERS * DMA)


def program(nc, ins, out):
    with ExitStack() as ctx:
        def sb(name, shape, dt=F32):
            return ctx.enter_context(nc.sbuf_tensor(name, shape, dt))

        dram = {
            "xn": nc.dram_tensor("xn_rows", [B, P, QT, D], F32).ap(),
            "xnt": nc.dram_tensor("xnt_split", [B, P, HALVES * KD * T], F32).ap(),
            "base": nc.dram_tensor("base_rows", [B, P, QT, D], F32).ap(),
            "experts": nc.dram_tensor("expert_rows", [E, P, WROW], F32).ap(),
            "queued": nc.dram_tensor("queued_rows", [SLOTS, D], F32).ap(),
            "routed": nc.dram_tensor("routed_rows", [SLOTS, D], F32).ap(),
        }
        keep = {
            "begun": ctx.enter_context(nc.semaphore("begun")),
            "ident": sb("ident", [P, P]),
            "mask": sb("mask", [P, T]),
            "wqk": sb("wqk_all", [P, PAIRS, 2, HALVES, KD, P], F32R),
            "wv": sb("wv_all", [P, HALVES, KD, H * DK], F32R),
            "wo": sb("wo_all", [P, HALVES, PAIRS, D], F32R),
            "shared": sb("shared_all", [P, HALVES, WROW], F32R),
            "weight": [sb(f"weight{n}", [P, TT]) for n in range(2)],
            "slot": [sb(f"slot{n}", [P, TT], I32) for n in range(2)],
            "weight_row": sb("weight_row", [P, SLOT_TILES], I32),
        }
        stage_a(nc, ins, dram, keep)
        stage_b(nc, ins, dram, keep)
        stage_c(nc, dram, keep)
        stage_d(nc, dram, keep, out)


NAMES = ["L0_attn_x", "L0_attn_Wq", "L0_attn_Wk", "L0_attn_Wv", "L0_attn_Wo", "L0_attn_bo", "L0_ffn_gate_w",
         "L0_ffn_gate_b", "L0_ffn_shared_wg", "L0_ffn_shared_wu", "L0_ffn_shared_wd", "L0_ffn_experts_wg",
         "L0_ffn_experts_wu", "L0_ffn_experts_wd"]


def kernel(**inputs):
    import concourse.bacc as bacc
    from concourse.bass_utils import run_bass_kernel_spmd

    nc = bacc.Bacc("TRN2", target_bir_lowering=False, num_devices=1)
    arrays, ins = {}, {}
    for name in NAMES:
        a = np.ascontiguousarray(inputs[name])
        arrays[f"in_{name}"] = a
        ins[name] = nc.dram_tensor(f"in_{name}", a.shape, mybir.dt.from_np(a.dtype), kind="ExternalInput").ap()
    out = nc.dram_tensor("out_0", (B, T, D), F32, kind="ExternalOutput").ap()
    program(nc, ins, out)
    result = run_bass_kernel_spmd(nc, [arrays], core_ids=[0])
    return result.results[0]["out_0"]
```
